# Optimizing a Trainium2 kernel written in Bass

```python
import numpy as np
import jax
import jax.numpy as jnp

def _softmax(x, axis=-1):
    return jax.nn.softmax(x, axis=axis)

def _gelu(x):
    return jax.nn.gelu(x, approximate=True)

def _silu(x):
    return jax.nn.silu(x)

def _sigmoid(x):
    return jax.nn.sigmoid(x)

def _layernorm(x, axis=-1, eps=1e-05):
    m = jnp.mean(x, axis=axis, keepdims=True)
    v = jnp.var(x, axis=axis, keepdims=True)
    return (x - m) / jnp.sqrt(v + eps)

def _scatter_add(tgt, idx, src, axis=0):
    return tgt.at[idx].add(src)

def _segment_sum(src, seg, n):
    return jax.ops.segment_sum(src, seg, n)
kernel_name = 'mk_xattn_ffn_d4_seqx_r8_e6ba6d'

def setup_inputs(seed: int=0):
    np.random.seed(seed)
    _w = jnp.asarray

    def _rec_inputs():
        import jax
        import jax.numpy as jnp
        _rk = jax.random.key(seed)
        x = 0.002226 + 0.9996 * jax.random.normal(jax.random.fold_in(_rk, 1), (4, 256, 128), jnp.float32)
        _lenS = 256 - jax.random.randint(jax.random.fold_in(_rk, 7), (4,), 0, max(1, 256 // 4) + 1, jnp.int32)
        _lenS2 = 512 - jax.random.randint(jax.random.fold_in(_rk, 8), (4,), 0, max(1, 512 // 4) + 1, jnp.int32)
        _ctx_1024P = jax.random.normal(jax.random.fold_in(_rk, 11), (4, 16, 128), jnp.float32)
        _ctx_1024c = jax.random.dirichlet(jax.random.fold_in(_rk, 511), 0.3 * jnp.ones((16,), jnp.float32), (4, 512))
        _ctx_1024t = jnp.einsum('bsk,bkd->bsd', _ctx_1024c, _ctx_1024P)
        _ctx_1024t = _ctx_1024t * jax.lax.rsqrt(jnp.mean(jnp.square(_ctx_1024t)) + 1e-12) * 0.953939
        ctx_1024 = -0.000125008 + 0.999885 * (_ctx_1024t + 0.3 * jax.random.normal(jax.random.fold_in(_rk, 611), (4, 512, 128), jnp.float32))
        _validS = jnp.arange(256)[None, :] < _lenS[:, None]
        _validS2 = jnp.arange(512)[None, :] < _lenS2[:, None]
        _causal = jnp.tril(jnp.ones((256, 256), dtype=bool))
        mask_BxS2_bk0 = jnp.logical_not(jnp.broadcast_to(_validS2[:, :], (4, 512)))
        mask_1x1xSxS2_bk0 = jnp.logical_not(jnp.broadcast_to(_validS2[0:1, None, None, :], (1, 1, 256, 512)))
        mask_BxS2_bf1 = jnp.ones((4, 512), dtype=bool)
        return (x, ctx_1024, mask_BxS2_bk0, mask_1x1xSxS2_bk0, mask_BxS2_bf1)
    x, ctx_1024, mask_BxS2_bk0, mask_1x1xSxS2_bk0, mask_BxS2_bf1 = _rec_inputs()

    def _L0_xattn_setup():
        import jax, jax.numpy as jnp
        import numpy as np
        EPS = 1e-05

        def layer_norm(x, g, b):
            mu = jnp.mean(x, axis=-1, keepdims=True)
            var = jnp.mean((x - mu) ** 2, axis=-1, keepdims=True)
            return (x - mu) * jax.lax.rsqrt(var + EPS) * g + b
        key = jax.random.key(seed)
        ks = jax.random.split(key, 8)
        b, n, l, D = (8, 512, 64, 128)
        heads, dim_head = (16, 64)
        inner = heads * dim_head
        x = jax.random.normal(ks[0], (b, n, D), dtype=jnp.float32)
        latents = jax.random.normal(ks[1], (b, l, D), dtype=jnp.float32)
        mask = jax.random.randint(ks[2], (b, n), 0, 2) > 0
        Wq = jax.random.normal(ks[3], (D, inner), dtype=jnp.float32) * D ** (-0.5)
        Wkv = jax.random.normal(ks[4], (D, 2 * inner), dtype=jnp.float32) * D ** (-0.5)
        Wout = jax.random.normal(ks[5], (inner, D), dtype=jnp.float32) * inner ** (-0.5)
        g1 = jnp.ones((D,), jnp.float32)
        b1 = jnp.zeros((D,), jnp.float32)
        g2 = jnp.ones((D,), jnp.float32)
        b2 = jnp.zeros((D,), jnp.float32)
        return {'x': x, 'latents': latents, 'mask': mask, 'g1': g1, 'b1': b1, 'g2': g2, 'b2': b2, 'Wq': Wq, 'Wkv': Wkv, 'Wout': Wout}
    _L0_xattn_all = _L0_xattn_setup()
    _L0_xattn_in = {k: v for k, v in _L0_xattn_all.items() if k in ('g1', 'b1', 'g2', 'b2', 'Wq', 'Wkv', 'Wout')}
    del _L0_xattn_all

    def _L0_ffn_setup():
        import jax, jax.numpy as jnp
        import numpy as np
        D_MODEL, FF_DIM = (128, 256)
        N_SHARED, N_ROUTED, TOP_K = (1, 8, 2)
        BATCH, SEQ = (2, 256)
        key = jax.random.key(seed)
        ks = jax.random.split(key, 8)
        init = lambda k, shape: jax.random.normal(k, shape, jnp.float32) * 0.02
        x = jax.random.normal(ks[0], (BATCH, SEQ, D_MODEL), jnp.float32)
        Wg = init(ks[1], (D_MODEL, N_ROUTED))
        Ws1 = init(ks[2], (D_MODEL, FF_DIM))
        Ws3 = init(ks[3], (D_MODEL, FF_DIM))
        Ws2 = init(ks[4], (FF_DIM, D_MODEL))
        We1 = init(ks[5], (N_ROUTED, D_MODEL, FF_DIM))
        We3 = init(ks[6], (N_ROUTED, D_MODEL, FF_DIM))
        We2 = init(ks[7], (N_ROUTED, FF_DIM, D_MODEL))
        return {'x': x, 'Wg': Wg, 'Ws1': Ws1, 'Ws3': Ws3, 'Ws2': Ws2, 'We1': We1, 'We3': We3, 'We2': We2}
    _L0_ffn_all = _L0_ffn_setup()
    _L0_ffn_in = {k: v for k, v in _L0_ffn_all.items() if k in ('Wg', 'Ws1', 'Ws3', 'Ws2', 'We1', 'We3', 'We2')}
    del _L0_ffn_all

    def _L1_xattn_setup():
        import jax, jax.numpy as jnp
        import numpy as np
        D_MODEL = 128
        NUM_HEADS = 16
        HEAD_DIM = D_MODEL // NUM_HEADS
        B, S = (2, 256)

        def _split_heads(x):
            b, s, _ = x.shape
            return x.reshape(b, s, NUM_HEADS, HEAD_DIM).transpose(0, 2, 1, 3)
        key = jax.random.key(seed)
        ks = jax.random.split(key, 8)
        scale = 1.0 / np.sqrt(D_MODEL)
        inp = {'query': jax.random.normal(ks[0], (B, S, D_MODEL), jnp.float32), 'key': jax.random.normal(ks[1], (B, S, D_MODEL), jnp.float32), 'value': jax.random.normal(ks[2], (B, S, D_MODEL), jnp.float32), 'mask': jnp.tril(jnp.ones((S, S), dtype=bool))[None, None, :, :], 'Wq': jax.random.normal(ks[3], (D_MODEL, D_MODEL), jnp.float32) * scale, 'Wk': jax.random.normal(ks[4], (D_MODEL, D_MODEL), jnp.float32) * scale, 'Wv': jax.random.normal(ks[5], (D_MODEL, D_MODEL), jnp.float32) * scale, 'Wo': jax.random.normal(ks[6], (D_MODEL, D_MODEL), jnp.float32) * scale, 'bo': jax.random.normal(ks[7], (D_MODEL,), jnp.float32) * scale}
        return inp
    _L1_xattn_all = _L1_xattn_setup()
    _L1_xattn_in = {k: v for k, v in _L1_xattn_all.items() if k in ('Wq', 'Wk', 'Wv', 'Wo', 'bo')}
    del _L1_xattn_all

    def _L1_ffn_setup():
        import jax, jax.numpy as jnp
        import numpy as np
        E = 8
        K = 2
        key = jax.random.key(seed)
        ks = jax.random.split(key, 8)
        B, T, d = (4, 256, 128)
        h = 4 * d // E
        s = 0.02
        X = jax.random.normal(ks[0], (B, T, d), jnp.float32)
        routing_W = jax.random.normal(ks[1], (E, d), jnp.float32) * s
        expert_bias = jnp.zeros((E,), jnp.float32)
        sW1 = jax.random.normal(ks[2], (d, h), jnp.float32) * s
        sb1 = jnp.zeros((h,), jnp.float32)
        sW2 = jax.random.normal(ks[3], (h, d), jnp.float32) * s
        sb2 = jnp.zeros((d,), jnp.float32)
        rW1 = jax.random.normal(ks[4], (E, d, h), jnp.float32) * s
        rb1 = jnp.zeros((E, h), jnp.float32)
        rW2 = jax.random.normal(ks[5], (E, h, d), jnp.float32) * s
        rb2 = jnp.zeros((E, d), jnp.float32)
        return dict(X=X, routing_W=routing_W, expert_bias=expert_bias, sW1=sW1, sb1=sb1, sW2=sW2, sb2=sb2, rW1=rW1, rb1=rb1, rW2=rW2, rb2=rb2)
    _L1_ffn_all = _L1_ffn_setup()
    _L1_ffn_in = {k: v for k, v in _L1_ffn_all.items() if k in ('routing_W', 'expert_bias', 'sW1', 'sb1', 'sW2', 'sb2', 'rW1', 'rb1', 'rW2', 'rb2')}
    del _L1_ffn_all

    def _L2_xattn_setup():
        import jax, jax.numpy as jnp
        import numpy as np
        B, L, D = (8, 256, 128)
        key = jax.random.key(seed)
        k1, k2, k3 = jax.random.split(key, 3)
        enc_outputs = jax.random.normal(k1, (B, L, D), dtype=jnp.float32)
        x = jax.random.normal(k2, (B, L, D), dtype=jnp.float32)
        Wq = jax.random.normal(k3, (D, D), dtype=jnp.float32) * (1.0 / np.sqrt(D))
        return {'enc_outputs': enc_outputs, 'x': x, 'Wq': Wq}
    _L2_xattn_all = _L2_xattn_setup()
    _L2_xattn_in = {k: v for k, v in _L2_xattn_all.items() if k in ('Wq',)}
    del _L2_xattn_all

    def _L2_ffn_setup():
        import jax, jax.numpy as jnp
        import numpy as np
        B, S, D, E, H, DO = (4, 256, 128, 8, 512, 128)
        TOP_K = 2
        LN_EPS = 1e-05
        key = jax.random.key(seed)
        ks = jax.random.split(key, 9)
        s = 0.02
        return {'x': jax.random.normal(ks[0], (B, S, D), dtype=jnp.float32), 'W1': jax.random.normal(ks[1], (E, D, H), dtype=jnp.float32) * s, 'b1': jnp.zeros((E, H), dtype=jnp.float32), 'W2': jax.random.normal(ks[2], (E, H, DO), dtype=jnp.float32) * s, 'b2': jnp.zeros((E, DO), dtype=jnp.float32), 'gate_W': jax.random.normal(ks[3], (D, E), dtype=jnp.float32) * s, 'shared_W': jax.random.normal(ks[4], (D, DO), dtype=jnp.float32) * s, 'shared_b': jnp.zeros((DO,), dtype=jnp.float32), 'gamma': jnp.ones((DO,), dtype=jnp.float32), 'beta': jnp.zeros((DO,), dtype=jnp.float32)}
    _L2_ffn_all = _L2_ffn_setup()
    _L2_ffn_in = {k: v for k, v in _L2_ffn_all.items() if k in ('W1', 'b1', 'W2', 'b2', 'gate_W', 'shared_W', 'shared_b', 'gamma', 'beta')}
    del _L2_ffn_all

    def _L3_xattn_setup():
        import jax, jax.numpy as jnp
        import numpy as np
        N_HEADS = 16
        D_MODEL = 128
        HEAD_DIM = D_MODEL // N_HEADS
        MASK_FILL = -100000000.0

        def _split_heads(x):
            B, S, _ = x.shape
            return x.reshape(B, S, N_HEADS, HEAD_DIM).transpose(0, 2, 1, 3)
        key = jax.random.key(seed)
        ks = jax.random.split(key, 12)
        B, L, P = (2, 256, 256)
        s = 1.0 / np.sqrt(D_MODEL).astype(np.float32)
        inp = {'q': jax.random.normal(ks[0], (B, L, D_MODEL), dtype=jnp.float32), 'k': jax.random.normal(ks[1], (B, P, D_MODEL), dtype=jnp.float32), 'v': jax.random.normal(ks[2], (B, P, D_MODEL), dtype=jnp.float32), 'attention_mask': jnp.ones((B, P), dtype=bool), 'Wq': jax.random.normal(ks[3], (D_MODEL, D_MODEL), dtype=jnp.float32) * s, 'bq': jnp.zeros((D_MODEL,), dtype=jnp.float32), 'Wk': jax.random.normal(ks[4], (D_MODEL, D_MODEL), dtype=jnp.float32) * s, 'bk': jnp.zeros((D_MODEL,), dtype=jnp.float32), 'Wv': jax.random.normal(ks[5], (D_MODEL, D_MODEL), dtype=jnp.float32) * s, 'bv': jnp.zeros((D_MODEL,), dtype=jnp.float32), 'Wo': jax.random.normal(ks[6], (D_MODEL, D_MODEL), dtype=jnp.float32) * s, 'bo': jnp.zeros((D_MODEL,), dtype=jnp.float32)}
        return inp
    _L3_xattn_all = _L3_xattn_setup()
    _L3_xattn_in = {k: v for k, v in _L3_xattn_all.items() if k in ('Wq', 'bq', 'Wk', 'bk', 'Wv', 'bv', 'Wo', 'bo')}
    del _L3_xattn_all

    def _L3_ffn_setup():
        import jax, jax.numpy as jnp
        import numpy as np
        B, S, D, F, O = (4, 256, 128, 512, 128)
        E, NS, K = (4, 2, 2)
        key = jax.random.key(seed)
        ks = jax.random.split(key, 6)

        def w(k, shape, fan_in):
            return jax.random.normal(k, shape, jnp.float32) * fan_in ** (-0.5)
        return {'x': jax.random.normal(ks[0], (B, S, D), jnp.float32), 'gate_w': w(ks[1], (D, E), D), 'gate_b': jnp.zeros((E,), jnp.float32), 'sw1': w(ks[2], (NS, D, F), D), 'sb1': jnp.zeros((NS, F), jnp.float32), 'sw2': w(ks[3], (NS, F, O), F), 'sb2': jnp.zeros((NS, O), jnp.float32), 'rw1': w(ks[4], (E, D, F), D), 'rb1': jnp.zeros((E, F), jnp.float32), 'rw2': w(ks[5], (E, F, O), F), 'rb2': jnp.zeros((E, O), jnp.float32)}
    _L3_ffn_all = _L3_ffn_setup()
    _L3_ffn_in = {k: v for k, v in _L3_ffn_all.items() if k in ('gate_w', 'gate_b', 'sw1', 'sb1', 'sw2', 'sb2', 'rw1', 'rb1', 'rw2', 'rb2')}
    del _L3_ffn_all
    return {'x': x, 'ctx_1024': ctx_1024, 'mask_BxS2_bk0': mask_BxS2_bk0, 'mask_1x1xSxS2_bk0': mask_1x1xSxS2_bk0, 'mask_BxS2_bf1': mask_BxS2_bf1, 'L0_xattn_g1': _L0_xattn_in['g1'], 'L0_xattn_b1': _L0_xattn_in['b1'], 'L0_xattn_g2': _L0_xattn_in['g2'], 'L0_xattn_b2': _L0_xattn_in['b2'], 'L0_xattn_Wq': _L0_xattn_in['Wq'], 'L0_xattn_Wkv': _L0_xattn_in['Wkv'], 'L0_xattn_Wout': _L0_xattn_in['Wout'], 'L0_ffn_Wg': _L0_ffn_in['Wg'], 'L0_ffn_Ws1': _L0_ffn_in['Ws1'], 'L0_ffn_Ws3': _L0_ffn_in['Ws3'], 'L0_ffn_Ws2': _L0_ffn_in['Ws2'], 'L0_ffn_We1': _L0_ffn_in['We1'], 'L0_ffn_We3': _L0_ffn_in['We3'], 'L0_ffn_We2': _L0_ffn_in['We2'], 'L1_xattn_Wq': _L1_xattn_in['Wq'], 'L1_xattn_Wk': _L1_xattn_in['Wk'], 'L1_xattn_Wv': _L1_xattn_in['Wv'], 'L1_xattn_Wo': _L1_xattn_in['Wo'], 'L1_xattn_bo': _L1_xattn_in['bo'], 'L1_ffn_routing_W': _L1_ffn_in['routing_W'], 'L1_ffn_expert_bias': _L1_ffn_in['expert_bias'], 'L1_ffn_sW1': _L1_ffn_in['sW1'], 'L1_ffn_sb1': _L1_ffn_in['sb1'], 'L1_ffn_sW2': _L1_ffn_in['sW2'], 'L1_ffn_sb2': _L1_ffn_in['sb2'], 'L1_ffn_rW1': _L1_ffn_in['rW1'], 'L1_ffn_rb1': _L1_ffn_in['rb1'], 'L1_ffn_rW2': _L1_ffn_in['rW2'], 'L1_ffn_rb2': _L1_ffn_in['rb2'], 'L2_xattn_Wq': _L2_xattn_in['Wq'], 'L2_ffn_W1': _L2_ffn_in['W1'], 'L2_ffn_b1': _L2_ffn_in['b1'], 'L2_ffn_W2': _L2_ffn_in['W2'], 'L2_ffn_b2': _L2_ffn_in['b2'], 'L2_ffn_gate_W': _L2_ffn_in['gate_W'], 'L2_ffn_shared_W': _L2_ffn_in['shared_W'], 'L2_ffn_shared_b': _L2_ffn_in['shared_b'], 'L2_ffn_gamma': _L2_ffn_in['gamma'], 'L2_ffn_beta': _L2_ffn_in['beta'], 'L3_xattn_Wq': _L3_xattn_in['Wq'], 'L3_xattn_bq': _L3_xattn_in['bq'], 'L3_xattn_Wk': _L3_xattn_in['Wk'], 'L3_xattn_bk': _L3_xattn_in['bk'], 'L3_xattn_Wv': _L3_xattn_in['Wv'], 'L3_xattn_bv': _L3_xattn_in['bv'], 'L3_xattn_Wo': _L3_xattn_in['Wo'], 'L3_xattn_bo': _L3_xattn_in['bo'], 'L3_ffn_gate_w': _L3_ffn_in['gate_w'], 'L3_ffn_gate_b': _L3_ffn_in['gate_b'], 'L3_ffn_sw1': _L3_ffn_in['sw1'], 'L3_ffn_sb1': _L3_ffn_in['sb1'], 'L3_ffn_sw2': _L3_ffn_in['sw2'], 'L3_ffn_sb2': _L3_ffn_in['sb2'], 'L3_ffn_rw1': _L3_ffn_in['rw1'], 'L3_ffn_rb1': _L3_ffn_in['rb1'], 'L3_ffn_rw2': _L3_ffn_in['rw2'], 'L3_ffn_rb2': _L3_ffn_in['rb2']}

def reference(x, ctx_1024, mask_BxS2_bk0, mask_1x1xSxS2_bk0, mask_BxS2_bf1, L0_xattn_g1, L0_xattn_b1, L0_xattn_g2, L0_xattn_b2, L0_xattn_Wq, L0_xattn_Wkv, L0_xattn_Wout, L0_ffn_Wg, L0_ffn_Ws1, L0_ffn_Ws3, L0_ffn_Ws2, L0_ffn_We1, L0_ffn_We3, L0_ffn_We2, L1_xattn_Wq, L1_xattn_Wk, L1_xattn_Wv, L1_xattn_Wo, L1_xattn_bo, L1_ffn_routing_W, L1_ffn_expert_bias, L1_ffn_sW1, L1_ffn_sb1, L1_ffn_sW2, L1_ffn_sb2, L1_ffn_rW1, L1_ffn_rb1, L1_ffn_rW2, L1_ffn_rb2, L2_xattn_Wq, L2_ffn_W1, L2_ffn_b1, L2_ffn_W2, L2_ffn_b2, L2_ffn_gate_W, L2_ffn_shared_W, L2_ffn_shared_b, L2_ffn_gamma, L2_ffn_beta, L3_xattn_Wq, L3_xattn_bq, L3_xattn_Wk, L3_xattn_bk, L3_xattn_Wv, L3_xattn_bv, L3_xattn_Wo, L3_xattn_bo, L3_ffn_gate_w, L3_ffn_gate_b, L3_ffn_sw1, L3_ffn_sb1, L3_ffn_sw2, L3_ffn_sb2, L3_ffn_rw1, L3_ffn_rb1, L3_ffn_rw2, L3_ffn_rb2):
    import jax
    import jax.numpy as jnp

    def _L0_xattn_ref(x, latents, mask, g1, b1, g2, b2, Wq, Wkv, Wout):
        import jax, jax.numpy as jnp
        import numpy as np
        EPS = 1e-05

        def layer_norm(x, g, b):
            mu = jnp.mean(x, axis=-1, keepdims=True)
            var = jnp.mean((x - mu) ** 2, axis=-1, keepdims=True)
            return (x - mu) * jax.lax.rsqrt(var + EPS) * g + b
        heads, dim_head = (16, 64)
        b, n, D = x.shape
        l = latents.shape[1]
        xn = layer_norm(x, g1, b1)
        ln_lat = layer_norm(latents, g2, b2)
        q = ln_lat @ Wq
        kv = jnp.concatenate([xn, ln_lat], axis=1) @ Wkv
        k, v = jnp.split(kv, 2, axis=-1)

        def to_heads(t):
            return t.reshape(t.shape[0], t.shape[1], heads, dim_head).transpose(0, 2, 1, 3)
        q, k, v = (to_heads(q), to_heads(k), to_heads(v))
        scale = 1.0 / np.sqrt(np.sqrt(dim_head)).astype(np.float32)
        weight = jnp.einsum('bhld,bhnd->bhln', q * scale, k * scale)
        full_mask = jnp.concatenate([mask, jnp.ones((b, l), dtype=bool)], axis=1)
        neg = -jnp.finfo(weight.dtype).max
        weight = jnp.where(full_mask[:, None, None, :], weight, neg)
        weight = jax.nn.softmax(weight.astype(jnp.float32), axis=-1).astype(q.dtype)
        out = jnp.einsum('bhln,bhnd->bhld', weight, v)
        out = out.transpose(0, 2, 1, 3).reshape(b, l, heads * dim_head)
        return out @ Wout

    def _L0_ffn_ref(x, Wg, Ws1, Ws3, Ws2, We1, We3, We2):
        import jax, jax.numpy as jnp
        import numpy as np
        D_MODEL, FF_DIM = (128, 256)
        N_SHARED, N_ROUTED, TOP_K = (1, 8, 2)
        BATCH, SEQ = (2, 256)
        B, S, d = x.shape
        E = Wg.shape[1]
        xf = x.reshape(-1, d)
        T = xf.shape[0]
        gates = jax.nn.sigmoid(xf @ Wg)
        vals, idx = jax.lax.top_k(gates, TOP_K)
        vals = vals / vals.sum(axis=-1, keepdims=True)
        w = jnp.zeros((T, E), x.dtype).at[jnp.arange(T)[:, None], idx].add(vals)
        shared = jax.nn.silu(xf @ Ws1) * (xf @ Ws3) @ Ws2
        h = jax.nn.silu(jnp.einsum('td,edf->tef', xf, We1)) * jnp.einsum('td,edf->tef', xf, We3)
        routed = jnp.einsum('tef,efd,te->td', h, We2, w)
        out = (shared + routed) / (N_SHARED + TOP_K)
        return out.reshape(B, S, d)

    def _L1_xattn_ref(query, key, value, mask, Wq, Wk, Wv, Wo, bo):
        import jax, jax.numpy as jnp
        import numpy as np
        D_MODEL = 128
        NUM_HEADS = 16
        HEAD_DIM = D_MODEL // NUM_HEADS
        B, S = (2, 256)

        def _split_heads(x):
            b, s, _ = x.shape
            return x.reshape(b, s, NUM_HEADS, HEAD_DIM).transpose(0, 2, 1, 3)
        q = _split_heads(query @ Wq.T)
        k = _split_heads(key @ Wk.T)
        v = _split_heads(value @ Wv.T)
        scores = jnp.einsum('bhqd,bhkd->bhqk', q, k) / jnp.sqrt(jnp.float32(HEAD_DIM))
        scores = jnp.where(mask, scores, jnp.float32(-jnp.inf))
        attn = jax.nn.softmax(scores, axis=-1)
        out = jnp.einsum('bhqk,bhkd->bhqd', attn, v)
        out = out.transpose(0, 2, 1, 3).reshape(query.shape[0], q.shape[2], D_MODEL)
        return out @ Wo.T + bo

    def _L1_ffn_ref(X, routing_W, expert_bias, sW1, sb1, sW2, sb2, rW1, rb1, rW2, rb2):
        import jax, jax.numpy as jnp
        import numpy as np
        E = 8
        K = 2
        B, T, d = X.shape
        shared = jax.nn.silu(X @ sW1 + sb1) @ sW2 + sb2
        logits = jnp.einsum('btd,ed->bte', X, routing_W) + expert_bias
        activation = jnp.sqrt(jax.nn.softplus(logits))
        top_vals, top_idx = jax.lax.top_k(activation, K)
        combine = jnp.sum(jax.nn.one_hot(top_idx, E, dtype=X.dtype) * top_vals[..., None], axis=-2)
        Xf = X.reshape(-1, d)
        cf = combine.reshape(-1, E)
        hdn = jax.nn.silu(jnp.einsum('nd,edh->enh', Xf, rW1) + rb1[:, None, :])
        y = jnp.einsum('enh,ehd->end', hdn, rW2) + rb2[:, None, :]
        routed = jnp.einsum('ne,end->nd', cf, y).reshape(B, T, d)
        return shared + routed

    def _L2_xattn_ref(enc_outputs, x, Wq):
        import jax, jax.numpy as jnp
        import numpy as np
        B, L, D = (8, 256, 128)
        d_k = x.shape[-1]
        q = jnp.einsum('bld,hd->blh', x, Wq)
        k = jnp.einsum('bld,hd->blh', enc_outputs, Wq)
        v = k
        scores = jnp.einsum('bqh,bkh->bqk', q, k) / jnp.sqrt(jnp.float32(d_k))
        Lq, Lk = (scores.shape[1], scores.shape[2])
        causal = jnp.tril(jnp.ones((Lq, Lk), dtype=bool))
        scores = jnp.where(causal, scores, -jnp.inf)
        attn = jax.nn.softmax(scores, axis=-1)
        return jnp.einsum('bqk,bkh->bqh', attn, v)

    def _L2_ffn_ref(x, W1, b1, W2, b2, gate_W, shared_W, shared_b, gamma, beta):
        import jax, jax.numpy as jnp
        import numpy as np
        B, S, D, E, H, DO = (4, 256, 128, 8, 512, 128)
        TOP_K = 2
        LN_EPS = 1e-05
        d = x.shape[-1]
        flat = x.reshape(-1, d)
        n_exp = gate_W.shape[-1]
        probs = jax.nn.softmax(flat @ gate_W, axis=-1)
        topk_w, topk_idx = jax.lax.top_k(probs, TOP_K)
        topk_w = topk_w / topk_w.sum(axis=-1, keepdims=True)
        combine = (jax.nn.one_hot(topk_idx, n_exp, dtype=flat.dtype) * topk_w[..., None]).sum(axis=1)
        out = 0.5 * jax.nn.gelu(flat @ shared_W + shared_b, approximate=False)
        for e in range(n_exp):
            h = jax.nn.gelu(flat @ W1[e] + b1[e], approximate=False)
            out = out + combine[:, e:e + 1] * (h @ W2[e] + b2[e])
        mean = out.mean(axis=-1, keepdims=True)
        var = ((out - mean) ** 2).mean(axis=-1, keepdims=True)
        out = (out - mean) * jax.lax.rsqrt(var + LN_EPS) * gamma + beta
        return out.reshape(*x.shape[:-1], out.shape[-1])

    def _L3_xattn_ref(q, k, v, attention_mask, Wq, bq, Wk, bk, Wv, bv, Wo, bo):
        import jax, jax.numpy as jnp
        import numpy as np
        N_HEADS = 16
        D_MODEL = 128
        HEAD_DIM = D_MODEL // N_HEADS
        MASK_FILL = -100000000.0

        def _split_heads(x):
            B, S, _ = x.shape
            return x.reshape(B, S, N_HEADS, HEAD_DIM).transpose(0, 2, 1, 3)
        qm = _split_heads(q @ Wq.T + bq)
        km = _split_heads(k @ Wk.T + bk)
        vm = _split_heads(v @ Wv.T + bv)
        scores = jnp.einsum('bnlh,bnph->bnlp', qm, km) / np.sqrt(HEAD_DIM).astype(np.float32)
        mask = attention_mask[:, None, None, :]
        scores = jnp.where(mask, scores, MASK_FILL)
        attn = jax.nn.softmax(scores, axis=-1)
        out = jnp.einsum('bnlp,bnph->bnlh', attn, vm)
        B, _, L, _ = out.shape
        out = out.transpose(0, 2, 1, 3).reshape(B, L, D_MODEL)
        return out @ Wo.T + bo

    def _L3_ffn_ref(x, gate_w, gate_b, sw1, sb1, sw2, sb2, rw1, rb1, rw2, rb2):
        import jax, jax.numpy as jnp
        import numpy as np
        B, S, D, F, O = (4, 256, 128, 512, 128)
        E, NS, K = (4, 2, 2)
        weights = jax.nn.softmax(x @ gate_w + gate_b, axis=-1)
        topk_w, topk_i = jax.lax.top_k(weights, K)
        sh = jax.nn.relu(jnp.einsum('bsd,ndf->bsnf', x, sw1) + sb1)
        shared = (jnp.einsum('bsnf,nfo->bsno', sh, sw2) + sb2).sum(axis=2) / NS
        rh = jax.nn.relu(jnp.einsum('bsd,edf->bsef', x, rw1) + rb1)
        eo = jnp.einsum('bsef,efo->bseo', rh, rw2) + rb2
        gathered = jnp.take_along_axis(eo, topk_i[..., None], axis=2)
        routed = (gathered * topk_w[..., None]).sum(axis=2)
        return shared + routed
    x = x + _L0_xattn_ref(ctx_1024, _layernorm(x, axis=-1), mask_BxS2_bk0, L0_xattn_g1, L0_xattn_b1, L0_xattn_g2, L0_xattn_b2, L0_xattn_Wq, L0_xattn_Wkv, L0_xattn_Wout)
    x = x + _L0_ffn_ref(_layernorm(x, axis=-1), L0_ffn_Wg, L0_ffn_Ws1, L0_ffn_Ws3, L0_ffn_Ws2, L0_ffn_We1, L0_ffn_We3, L0_ffn_We2)
    x = x + _L1_xattn_ref(_layernorm(x, axis=-1), ctx_1024, ctx_1024, mask_1x1xSxS2_bk0, L1_xattn_Wq, L1_xattn_Wk, L1_xattn_Wv, L1_xattn_Wo, L1_xattn_bo)
    x = x + _L1_ffn_ref(_layernorm(x, axis=-1), L1_ffn_routing_W, L1_ffn_expert_bias, L1_ffn_sW1, L1_ffn_sb1, L1_ffn_sW2, L1_ffn_sb2, L1_ffn_rW1, L1_ffn_rb1, L1_ffn_rW2, L1_ffn_rb2)
    x = x + _L2_xattn_ref(ctx_1024, _layernorm(x, axis=-1), L2_xattn_Wq)
    x = x + _L2_ffn_ref(_layernorm(x, axis=-1), L2_ffn_W1, L2_ffn_b1, L2_ffn_W2, L2_ffn_b2, L2_ffn_gate_W, L2_ffn_shared_W, L2_ffn_shared_b, L2_ffn_gamma, L2_ffn_beta)
    x = x + _L3_xattn_ref(_layernorm(x, axis=-1), ctx_1024, ctx_1024, mask_BxS2_bf1, L3_xattn_Wq, L3_xattn_bq, L3_xattn_Wk, L3_xattn_bk, L3_xattn_Wv, L3_xattn_bv, L3_xattn_Wo, L3_xattn_bo)
    x = x + _L3_ffn_ref(_layernorm(x, axis=-1), L3_ffn_gate_w, L3_ffn_gate_b, L3_ffn_sw1, L3_ffn_sb1, L3_ffn_sw2, L3_ffn_sb2, L3_ffn_rw1, L3_ffn_rb1, L3_ffn_rw2, L3_ffn_rb2)
    return x

_drawn_inputs = setup_inputs


def setup_inputs(seed=0):
    import zlib

    import numpy as np

    out = dict(_drawn_inputs(seed))
    spreads = {'L0_xattn_g1': (1.0, 0.2),
     'L0_xattn_b1': (0.0, 0.1),
     'L0_xattn_g2': (1.0, 0.2),
     'L0_xattn_b2': (0.0, 0.1),
     'L1_ffn_expert_bias': (0.0, 0.1),
     'L1_ffn_sb1': (0.0, 0.328),
     'L1_ffn_sb2': (0.0, 0.1),
     'L1_ffn_rb1': (0.0, 0.1),
     'L1_ffn_rb2': (0.0, 0.1),
     'L2_ffn_b1': (0.0, 0.1),
     'L2_ffn_b2': (0.0, 0.1),
     'L2_ffn_shared_b': (0.0, 0.1),
     'L2_ffn_gamma': (1.0, 0.2),
     'L2_ffn_beta': (0.0, 0.1),
     'L3_xattn_bq': (0.0, 0.546),
     'L3_xattn_bk': (0.0, 0.8),
     'L3_xattn_bv': (0.0, 0.1),
     'L3_xattn_bo': (0.0, 0.1),
     'L3_ffn_gate_b': (0.0, 0.307),
     'L3_ffn_sb1': (0.0, 0.345),
     'L3_ffn_sb2': (0.0, 0.1),
     'L3_ffn_rb1': (0.0, 0.366),
     'L3_ffn_rb2': (0.0, 0.1)}
    factors = {'L0_ffn_Wg': 5.626,
     'L0_ffn_Ws1': 4.111,
     'L0_ffn_Ws3': 4.235,
     'L0_ffn_Ws2': 4.392,
     'L0_ffn_We1': 4.36,
     'L0_ffn_We3': 4.395,
     'L0_ffn_We2': 4.319}
    for name, (base, spread) in spreads.items():
        noise = np.random.default_rng([zlib.crc32(name.encode()), seed]).standard_normal(out[name].shape)
        drawn = base * np.exp(spread * noise) if base else spread * noise
        out[name] = jnp.asarray(drawn.astype(out[name].dtype))
    for name, factor in factors.items():
        out[name] = (out[name] * factor).astype(out[name].dtype)
    return out
```

```python
from contextlib import ExitStack

import concourse.bass as bass
from concourse import mybir

ALU = mybir.AluOpType
ACT = mybir.ActivationFunctionType
F32 = mybir.dt.float32
U8 = mybir.dt.uint8
AX_X = mybir.AxisListType.X

P = 128
D = 128
EPS = 1e-5
FAR = 1e30
NEVER = 3.0e38
HEADS = 16
MOE = {
    "f0": dict(routed=8, shared=1, fixed=1.0, chunks=2),
    "f1": dict(routed=8, shared=1, fixed=1.0, chunks=1),
    "f2": dict(routed=8, shared=0, fixed=0.0, chunks=4),
    "f3": dict(routed=4, shared=2, fixed=0.5, chunks=4),
}
PHASES = ["a0", "f0", "a1", "f1", "a2", "f2", "a3", "f3"]
BEFORE = dict(zip(PHASES[1:], PHASES))


def build(nc, a, out):
    B, S, _ = a["x"].shape
    S2 = a["ctx_1024"].shape[1]
    NT, CT = S // P, S2 // P
    KV0 = S2 + S
    HALF = HEADS // 2
    ATT = {
        "a0": dict(nk=KV0, hpc=2, rows=64, scale=1.0 / 8.0),
        "a1": dict(nk=S2, hpc=4, rows=32, scale=float(8 ** -0.5)),
        "a3": dict(nk=S2, hpc=4, rows=32, scale=float(8 ** -0.5)),
    }

    with ExitStack() as ctx:
        def sb(name, shape, dt=F32):
            return ctx.enter_context(nc.sbuf_tensor(name, shape, dt))

        wq0 = sb("wq0", [P, 1024])
        wkv0 = sb("wkv0", [P, 2048])
        wo0 = sb("wo0", [P, HALF, D])
        wqkv = {t: sb("wqkv_" + t, [P, 3, D]) for t in ("a1", "a3")}
        wo_pad = {t: sb("wo_pad_" + t, [P, 4, D]) for t in ("a1", "a3")}
        wq2 = sb("wq2", [P, D])
        w_up = {"f1": sb("up_f1", [P, 10, 64])}
        w_dn = {"f1": sb("dn_f1", [P, 10, D])}
        big = sb("big", [P, 2 * 8 * 512])
        w_up["f0"] = big[:, 0:9 * 512].rearrange("p (e j f) -> p e j f", e=9, j=2)
        w_dn["f0"] = big[:, 9 * 512:9 * 768].rearrange("p (e c o) -> p e c o", e=9, c=2)
        w_up["f2"] = w_up["f3"] = big_up = big[:, 0:4096].rearrange("p (e f) -> p e f", e=8)
        w_dn["f2"] = w_dn["f3"] = big_dn = big[:, 4096:8192].rearrange("p (e c o) -> p e c o", e=8, c=4)
        w_shared2 = sb("w_shared2", [P, D])
        w_gate = {t: sb("gate_" + t, [P, MOE[t]["routed"]]) for t in MOE}
        b_gate = {"f1": sb("bgate_f1", [P, 8]), "f3": sb("bgate_f3", [P, 4])}
        b_up = {"f1": sb("bup_f1", [P, 5]), "f2": sb("bup_f2", [P, 32]), "f3": sb("bup_f3", [P, 24])}
        b_dn = {"f1": sb("bdn_f1", [9, D]), "f2": sb("bdn_f2", [8, D]), "f3": sb("bdn_f3", [6, D])}
        gb0 = sb("gb0", [P, 4])
        bqk3 = sb("bqk3", [P, 2])
        bv_pad = sb("bv_pad", [P, 4])
        bo = {"a1": sb("bo_a1", [P, D]), "a3": sb("bo_a3", [P, D])}
        sb2 = sb("sb2", [P, 3, D])
        ident = sb("ident", [P, P])
        rowmask = sb("rowmask", [P, 2 + HEADS])
        neg_half = sb("neg_half", [P, 6])
        pos_half = sb("pos_half", [P, 2, 8])
        bias1 = sb("bias1", [P, NT, S2])
        bias2 = sb("bias2", [P, NT, S])
        mask1_u8 = sb("mask1_u8", [P, NT, S2], U8)
        tok = sb("tok", [P, CT + NT, D])
        X = tok[:, CT:CT + NT, :]
        nrm = sb("nrm", [P, CT + NT, D])
        stats = sb("stats", [P, CT + NT, 6])
        mv = sb("mv", [P, CT + NT, 2])
        var_eps = sb("var_eps", [P, CT + NT])
        rstd = sb("rstd", [P, CT + NT])
        ctxT = sb("ctxT", [P, S2])
        kvT = sb("kvT", [P, KV0])
        xnT = sb("xnT", [P, S])
        mask_u8 = sb("mask_u8", [P, 2, S2], U8)
        bias0 = sb("bias0", [P, KV0])
        bias3 = sb("bias3", [P, S2])
        keysT = sb("keysT", [P, HALF, KV0])
        vals = sb("vals", [P, 6, 1024])
        vals_pad = vals[:, 0:2, :].rearrange("p a b -> p (a b)").rearrange("p (k h r) -> p k h r", k=CT, h=HEADS)
        qm = sb("qm", [P, HEADS, S])
        prob = sb("prob", [P, 4, KV0])
        probT = sb("probT", [P, 2, 6, S])
        negmax = sb("negmax", [P, HEADS * NT])
        lsum = sb("lsum", [P, HEADS, NT])
        linv = sb("linv", [P, HEADS, NT])
        linv_wide = sb("linv_wide", [P, 2, NT, P])
        o_raw = sb("o_raw", [P, 2, S])
        oT = sb("oT", [P, HALF, S])
        hT = keysT[:, 0:4, 0:512].rearrange("p a (b c) -> p a b c", b=2)
        act_tmp = sb("act_tmp", [P, 4, S])
        logit = sb("logit", [P, NT, 8])
        top8 = sb("top8", [P, NT, 8])
        cut = sb("cut", [P, NT, 8])
        rt = [sb(f"rt{i}", [P, NT, 8]) for i in range(5)]
        rsum = sb("rsum", [P, NT])
        rinv = sb("rinv", [P, NT])
        comb = sb("comb", [P, NT, 10])
        combT = sb("combT", [16, S])
        acc = sb("acc", [P, NT, D])
        gl = sb("gl", [P, NT, D])
        ps = ctx.enter_context(nc.psum_tensor("ps", [P, 8, 512], F32))

        def sem(name):
            return ctx.enter_context(nc.semaphore(name))

        w_early, w_rest, w_out = sem("w_early"), sem("w_rest"), sem("w_out")
        masks = sem("masks")
        zeroed = sem("zeroed")
        consts_ready = sem("consts_ready")
        setup_dve, setup_pe = sem("setup_dve"), sem("setup_pe")
        go = {e: sem("go_" + e) for e in ("pe", "act", "dve", "pool")}
        names = ["stats", "rstd", "normed", "xT", "xnT", "x_done", "loaded", "vals_zeroed", "big0_loaded", "big2_loaded", "big3_loaded", "dve_step", "pool_step", "stored", "ended"]
        for t in PHASES:
            if t[0] == "a":
                names += [t + "_" + n for n in ("proj", "ev_dve", "ev_act", "qproj", "qm", "scores", "biased", "exped",
                                                "turned", "pt_dve", "y")]
                if t != "a2":
                    names += [t + "_" + n for n in ("pt_act", "av", "o_raw", "linv", "r", "oT",
                                                    "qm_act" if t == "a0" else "q_sb")]
            else:
                names += [t + "_" + n for n in ("logits", "logit", "r_act", "comb", "up", "act", "down", "y_used")]
                names += ["f0_h"] if t == "f0" else [t + "_" + n for n in ("combT", "combT_sb", "b2", "r_mid")]
        names += ["f1_r_pool", "f2_sh", "f2_sh_used", "f2_gl"]
        s = {n: sem(n) for n in names}
        nums = sorted(x.num for x in s.values())
        assert nums == list(range(nums[0], nums[0] + len(nums)))
        block = ctx.enter_context(nc.Block())

        def before(t, name):
            once = {"stats": NT, "rstd": 1, "normed": NT, "xT": NT, "xnT": 1, "x_done": NT}[name]
            twice = {"stats": NT, "rstd": 1, "normed": NT}.get(name, 0)
            first = {"stats": CT + NT, "rstd": 1, "normed": CT + NT, "xT": CT, "xnT": 1}.get(name, 0)
            done = PHASES[:PHASES.index(t)]
            return once * len(done) + first * ("a0" in done) + twice * ("f2" in done)

        def proj_jobs(t):
            if t == "a0":
                keys = [(hi - lo, wkv0[:, P * c:P * c + P], kvT[:, lo:hi])
                        for c in range(HALF) for lo, hi in ((0, S2), (S2, KV0))]
                return keys + [(512, kvT[:, P * k:P * k + P], wkv0[:, 1024 + 512 * j:1536 + 512 * j])
                               for k in range(KV0 // P) for j in range(2)]
            return [(S2, wqkv[t][:, 1, :], ctxT[:])] + \
                [(D, ctxT[:, P * k:P * k + P], wqkv[t][:, 2, :]) for k in range(CT)]

        def proj_out(t, j):
            if t == "a0":
                if j < 2 * HALF:
                    lo, hi = ((0, S2), (S2, KV0))[j % 2]
                    return keysT[:, j // 2, lo:hi], ps[:, j % 6, 0:hi - lo]
                k, half = (j - 2 * HALF) // 2, j % 2
                return vals[:, k, 512 * half:512 * half + 512], ps[:, j % 6, :]
            if j == 0:
                return keysT[:, 0, 0:S2], ps[:, 0, :]
            return vals_pad[:, j - 1, :, 0:8], ps[:, j % 6, 0:D].rearrange("p (h i) -> p h i", i=8)

        def expert_groups(t):
            e, n = MOE[t]["routed"], MOE[t]["shared"]
            if t == "f1":
                return [[8]] + [[i, i + 1] for i in range(0, e, 2)]
            return [[i] for i in (*range(e, e + n), *range(e))]

        def first_of(groups, g):
            return sum(len(x) for x in groups[:g])

        def down_before(t, u):
            return first_of(expert_groups(t), (u - 8) // MOE[t]["chunks"] + 1)

        def iteration_end(eng, me):
            eng.drain().then_inc(s["ended"], 1)
            eng.wait_ge(go[me], 1)
            eng.sem_clear(go[me])

        n_early, n_rest = [0], [0]
        N_LOAD, N_BIG0, N_BIG = 16 * 5, 16 * 13, 16 * 4
        N_CONSTS = 1 + NT + 2

        @block.sync
        def _(sp):
            def early(dst, src):
                sp.dma_start(dst, src).then_inc(w_early, 16)
                n_early[0] += 16

            def rest(dst, src):
                sp.dma_start(dst, src).then_inc(w_rest, 16)
                n_rest[0] += 16

            def col(name):
                return a[name].rearrange("(p o) -> p o", o=1)

            for j, n in enumerate(("g1", "b1", "g2", "b2")):
                early(gb0[:, j:j + 1], col("L0_xattn_" + n))
            early(wkv0[:], a["L0_xattn_Wkv"])
            early(wq0[:], a["L0_xattn_Wq"])
            early(wo0[:], a["L0_xattn_Wout"].rearrange("(c p) o -> p c o", p=P))
            early(mask1_u8[:], a["mask1"].rearrange("(t p) k -> p t k", p=P))

            for t, l in (("a1", "L1"), ("a3", "L3")):
                early(bo[t][:], a[f"{l}_xattn_bo"].rearrange("(o d) -> o d", o=1).broadcast_to([P, D]))
            sp.wait_ge(zeroed, 5)
            for t, l in (("a1", "L1"), ("a3", "L3")):
                wo = a[f"{l}_xattn_WoT"].rearrange("(c j i) o -> j i c o", c=4, j=4)
                for j in range(4):
                    early(wo_pad[t][32 * j:32 * j + 8], wo[j])
            bv = a["L3_xattn_bv"].rearrange("(c j i) -> j i c", c=4, j=4)
            with nc.allow_non_contiguous_dma(reason="128 biases into columns"):
                for j in range(4):
                    early(bv_pad[32 * j:32 * j + 8, :], bv[j])
            rest(w_gate["f0"][:], a["L0_ffn_Wg"])
            for t, l in (("a1", "L1"), ("a3", "L3")):
                for j, n in enumerate("qkv"):
                    rest(wqkv[t][:, j, :], a[f"{l}_xattn_W{n}T"])
            rest(bqk3[:, 0:1], col("L3_xattn_bq"))
            rest(bqk3[:, 1:2], col("L3_xattn_bk"))
            rest(w_gate["f1"][:], a["L1_ffn_routing_WT"])
            rest(b_gate["f1"][:], a["L1_ffn_expert_bias"].rearrange("(o d) -> o d", o=1).broadcast_to([P, 8]))
            rest(w_up["f1"][:, 0:8, :], a["L1_ffn_rW1"].rearrange("e d f -> d e f"))
            rest(w_up["f1"][:, 8, :], a["L1_ffn_sW1"])
            rest(b_dn["f1"][0:8, :], a["L1_ffn_rb2"])
            rest(b_dn["f1"][8:9, :], a["L1_ffn_sb2"].rearrange("(o d) -> o d", o=1))
            rest(wq2[:], a["L2_xattn_WqT"])
            rest(w_gate["f2"][:], a["L2_ffn_gate_W"])
            rest(w_shared2[:], a["L2_ffn_shared_W"])
            rest(b_up["f2"][:], a["L2_ffn_b1c"])
            rest(b_dn["f2"][:], a["L2_ffn_b2"])
            for j, n in enumerate(("shared_b", "gamma", "beta")):
                rest(sb2[:, j, :], a["L2_ffn_" + n].rearrange("(o d) -> o d", o=1).broadcast_to([P, D]))
            rest(w_gate["f3"][:], a["L3_ffn_gate_w"])
            rest(b_gate["f3"][:], a["L3_ffn_gate_b"].rearrange("(o d) -> o d", o=1).broadcast_to([P, 4]))
            rest(b_up["f3"][:, 0:16], a["L3_ffn_rb1c"])
            rest(b_up["f3"][:, 16:24], a["L3_ffn_sb1c"])
            rest(b_dn["f3"][0:4, :], a["L3_ffn_rb2"])
            rest(b_dn["f3"][4:6, :], a["L3_ffn_sb2"])
            rest(b_up["f1"][:, 0:4], a["L1_ffn_rb1c"])
            rest(b_up["f1"][0:64, 4:5], col("L1_ffn_sb1"))
            w2 = a["L1_ffn_rW2"].rearrange("(q two) h o -> two h q o", two=2)
            pad_dn = w_dn["f1"][:].rearrange("p (q two) o -> p two q o", two=2)
            rest(pad_dn[0:64, 0, 0:4, :], w2[0])
            rest(pad_dn[64:128, 1, 0:4, :], w2[1])
            rest(w_dn["f1"][0:64, 8, :], a["L1_ffn_sW2"])

            with sp.Fori(0, B) as b:
                def load(dst, src):
                    sp.dma_start(dst, src).then_inc(s["loaded"], 16)

                load(tok[:, 0:CT, :], a["ctx_1024"][bass.ds(b, 1)].rearrange("o (t p) d -> p (o t) d", p=P))
                load(X, a["x"][bass.ds(b, 1)].rearrange("o (t p) d -> p (o t) d", p=P))
                load(mask_u8[:, 0, :], a["mask0"][bass.ds(b, 1), :].broadcast_to([P, S2]))
                load(mask_u8[:, 1, :], a["mask3"][bass.ds(b, 1), :].broadcast_to([P, S2]))
                load(ctxT[:], a["ctxT"][bass.ds(b, 1)].rearrange("o d s -> d (o s)"))

                def load_big(which, dst, src):
                    sp.dma_start(dst, src).then_inc(s[which], 16)

                load_big("big0_loaded", w_up["f0"][:, 8, 0, :], a["L0_ffn_Ws1"])
                load_big("big0_loaded", w_up["f0"][:, 8, 1, :], a["L0_ffn_Ws3"])
                load_big("big0_loaded", w_dn["f0"][:, 8], a["L0_ffn_Ws2"].rearrange("(c p) o -> p c o", p=P))
                load_big("big0_loaded", w_up["f0"][:, 0:8, 0, :], a["L0_ffn_We1"].rearrange("e d f -> d e f"))
                load_big("big0_loaded", w_up["f0"][:, 0:8, 1, :], a["L0_ffn_We3"].rearrange("e d f -> d e f"))
                for e in range(8):
                    load_big("big0_loaded", w_dn["f0"][:, e], a["L0_ffn_We2"][e].rearrange("(c p) o -> p c o", p=P))
                sp.wait_ge(s["x_done"], before("f0", "x_done") + NT)

                for e in range(0, 8, 4):
                    load_big("big2_loaded", big_up[:, e:e + 4, :], a["L2_ffn_W1"][e:e + 4].rearrange("e d f -> d e f"))
                    load_big("big2_loaded", big_dn[:, e:e + 4], a["L2_ffn_W2"][e:e + 4].rearrange("e (c p) o -> p e c o", p=P))
                sp.wait_ge(s["x_done"], before("f2", "x_done") + NT)
                load_big("big3_loaded", big_up[:, 0:4, :], a["L3_ffn_rw1"].rearrange("e d f -> d e f"))
                load_big("big3_loaded", big_up[:, 4:6, :], a["L3_ffn_sw1"].rearrange("e d f -> d e f"))
                load_big("big3_loaded", big_dn[:, 0:4], a["L3_ffn_rw2"].rearrange("e (c p) o -> p e c o", p=P))
                load_big("big3_loaded", big_dn[:, 4:6], a["L3_ffn_sw2"].rearrange("e (c p) o -> p e c o", p=P))
                sp.wait_ge(s["x_done"], before("f3", "x_done") + NT)
                sp.dma_start(out[bass.ds(b, 1)].rearrange("o (t p) d -> p (o t) d", p=P), X).then_inc(s["stored"], 16)
                sp.wait_ge(s["stored"], 16)
                sp.wait_ge(s["ended"], 4)
                sp.sem_clear(range(nums[0], nums[-1] + 1))
                for e in go:
                    sp.sem_inc(go[e], 1)


        @block.gpsimd
        def _(pool):
            nc.gpsimd.memset(wo_pad["a1"][:], 0.0).then_inc(zeroed, 1)
            nc.gpsimd.memset(wo_pad["a3"][:], 0.0).then_inc(zeroed, 1)
            nc.gpsimd.memset(bv_pad[:], 0.0).then_inc(zeroed, 1)
            nc.gpsimd.memset(b_up["f1"][:], 0.0).then_inc(zeroed, 1)
            nc.gpsimd.memset(w_dn["f1"][:], 0.0).then_inc(zeroed, 1)
            nc.gpsimd.memset(w_up["f1"][:, 9, :], 0.0).then_inc(zeroed, 1)
            nc.gpsimd.memset(bias0[:], 0.0).then_inc(zeroed, 1)
            nc.gpsimd.memset(neg_half[:], -0.5).then_inc(zeroed, 1)
            nc.gpsimd.memset(pos_half[:], 0.5).then_inc(zeroed, 1)
            nc.gpsimd.memset(ident[:], 0.0).then_inc(zeroed, 1)
            nc.gpsimd.memset(rowmask[:], 1.0).then_inc(zeroed, 1)
            nc.gpsimd.memset(bias2[:], 0.0).then_inc(zeroed, 1)
            pool.wait_ge(zeroed, 12)
            nc.gpsimd.affine_select(out=ident[:], in_=ident[:], compare_op=ALU.not_equal, fill=1.0, base=0,
                                    pattern=[[-1, P]], channel_multiplier=1).then_inc(consts_ready, 1)
            for t in range(NT):
                nc.gpsimd.affine_select(out=bias2[:, t, :], in_=bias2[:, t, :], compare_op=ALU.is_ge, fill=-FAR,
                                        base=P * t, pattern=[[-1, S]], channel_multiplier=1).then_inc(consts_ready, 1)
            for c0, n, w in ((0, 2, 64), (2, HEADS, 8)):
                m = rowmask[:, c0:c0 + n]
                nc.gpsimd.affine_select(out=m, in_=m, compare_op=ALU.is_ge, fill=0.0, base=0, pattern=[[-w, n]],
                                        channel_multiplier=1).then_inc(masks, 1)
            pool.wait_ge(masks, 2)
            for c0, n, w in ((0, 2, 64), (2, HEADS, 8)):
                m = rowmask[:, c0:c0 + n]
                nc.gpsimd.affine_select(out=m, in_=m, compare_op=ALU.is_ge, fill=0.0, base=w - 1, pattern=[[w, n]],
                                        channel_multiplier=-1).then_inc(consts_ready, 1)
            with pool.Fori(0, B):
                def rstd_of(t, lo, hi, k):
                    pool.wait_ge(s["stats"], before(t, "stats") + k)
                    nc.gpsimd.tensor_scalar(var_eps[:, lo:hi], mv[:, lo:hi, 1], EPS, None, ALU.add) \
                        .then_inc(s["pool_step"], 1)
                    n_pool[0] += 1
                    pool.wait_ge(s["pool_step"], n_pool[0])
                    nc.gpsimd.tensor_tensor(rstd[:, lo:hi], var_eps[:, lo:hi], neg_half[:, lo:hi], ALU.pow) \
                        .then_inc(s["rstd"], 1)

                n_pool = [0]
                for t in PHASES:
                    if t == "a0":
                        rstd_of(t, 0, CT + NT, CT + NT)
                        rstd_of(t, CT, CT + NT, CT + 2 * NT)
                        continue
                    if t == "f0":
                        pool.wait_ge(s["x_done"], before("a0", "x_done") + NT)
                        nc.gpsimd.memset(vals_pad, 0.0).then_inc(s["vals_zeroed"], 1)
                    rstd_of(t, CT, CT + NT, NT)
                    if t == "f1":
                        pool.wait_ge(s["f1_r_mid"], 2)
                        nc.gpsimd.tensor_tensor(rt[3][:], rt[2][:], pos_half[:], ALU.pow).then_inc(s["f1_r_pool"], 1)
                    if t == "f2":
                        rstd_of(t, CT, CT + NT, 2 * NT)
                iteration_end(pool, "pool")

        @block.tensor
        def _(pe):
            mm, tr = nc.tensor.matmul, nc.tensor.transpose
            pe.wait_ge(consts_ready, N_CONSTS)
            pe.wait_ge(w_early, n_early[0])
            pe.wait_ge(setup_dve, 1)
            for c in range(4):
                m = mm(ps[:, 0, 0:D], vals[:, c, 0:P], wo_pad["a3"][:, c, :],
                       start=(c == 0), stop=(c == 3))
            m.then_inc(setup_pe, 1)
            pe.wait_ge(setup_dve, 2)

            def turn_x(t):
                for k in range(NT):
                    pe.wait_ge(s["normed"], before(t, "normed") + k + 1)
                    tr(ps[:, 7, P * k:P * k + P], nrm[:, CT + k, :], ident[:]).then_inc(s["xT"], 1)

            def projections(t):
                for j, (n, lhsT, rhs) in enumerate(proj_jobs(t)):
                    if j >= 6:
                        k = j - 6
                        pe.wait_ge(s[t + ("_ev_act" if k % 2 else "_ev_dve")], k // 2 + 1)
                    mm(ps[:, j % 6, 0:n], lhsT, rhs, start=True, stop=True).then_inc(s[t + "_proj"], 1)

            def q_projection(t):
                pe.wait_ge(s["xnT"], before(t, "xnT") + 1)
                for c in range(HALF if t == "a0" else 1):
                    if c >= 2:
                        pe.wait_ge(s[t + ("_qm_act" if c % 2 else "_qm")], 2 * (c // 2))
                    lhsT = wq0[:, P * c:P * c + P] if t == "a0" else wqkv[t][:, 0, :]
                    rhs = kvT[:, S2:KV0] if t == "a0" else xnT[:]
                    mm(ps[:, 6 + c % 2, 0:S], lhsT, rhs, start=True, stop=True).then_inc(s[t + "_qproj"], 1)

            def attention(t):
                nk, hpc, rows = ATT[t]["nk"], ATT[t]["hpc"], ATT[t]["rows"]
                half = nk // P // 2
                nj = len(proj_jobs(t))
                pe.wait_ge(s[t + "_ev_dve"], (nj + 1) // 2)
                pe.wait_ge(s[t + "_ev_act"], nj // 2)
                U = HEADS * NT

                def scores(u):
                    h, qt = u // NT, u % NT
                    kt = keysT[:, h // 2, :] if t == "a0" else keysT[:, 0, :]
                    if t == "a0":
                        pe.wait_ge(s[t + ("_qm_act" if h // 2 % 2 else "_qm")], 2 * (h // 4) + h % 2 + 1)
                    else:
                        pe.wait_ge(s[t + "_qm"], h + 1)
                    if u >= 2:
                        pe.wait_ge(s[t + "_biased"], u - 1)
                    lhsT = qm[:, h, P * qt:P * qt + P]
                    m = mm(ps[:, 2 * (u % 2), 0:512], lhsT, kt[:, 0:512], start=True, stop=True)
                    if nk > 512:
                        m = mm(ps[:, 2 * (u % 2) + 1, 0:nk - 512], lhsT, kt[:, 512:nk], start=True, stop=True)
                    m.then_inc(s[t + "_scores"], 1)

                def turn(u):
                    pe.wait_ge(s[t + "_exped"], u + 1)
                    for g in range(2):
                        if u >= 1:
                            pe.wait_ge(s[t + ("_pt_act" if g else "_pt_dve")], u)
                        for k in range(half):
                            kk = g * half + k
                            m = tr(ps[:, 4 + g, P * k:P * k + P], prob[:, u % 4, P * kk:P * kk + P], ident[:])
                        m.then_inc(s[t + "_turned"], 1)

                def av(h):
                    pe.wait_ge(s[t + "_pt_dve"], NT * (h + 1))
                    pe.wait_ge(s[t + "_pt_act"], NT * (h + 1))
                    c, r = h // hpc, rows * (h % hpc)
                    if h == 0:
                        pe.wait_ge(s[t + "_qm"], HEADS // 2 if t == "a0" else HEADS)
                        if t == "a0":
                            pe.wait_ge(s[t + "_qm_act"], HEADS // 2)
                    if h % hpc == 0 and c >= 1:
                        pe.wait_ge(s[t + "_o_raw"], c)
                    for k in range(nk // P):
                        v = vals[:, k, 64 * h:64 * h + 64] if t == "a0" else vals_pad[:, k, h, :]
                        m = mm(ps[r:r + rows, 6, 0:S], v, probT[:, h % 2, k, :], start=(k == 0), stop=(k == nk // P - 1))
                    m.then_inc(s[t + "_av"], 1)
                    if h % hpc == hpc - 1:
                        pe.wait_ge(s[t + "_linv"], c + 1)
                        if c >= 1:
                            pe.wait_ge(s[t + "_oT"], c)
                        for qt in range(NT):
                            li = linv_wide[:, c % 2, qt, :]
                            m = tr(ps[:, 7, P * qt:P * qt + P], li, ident[:])
                        m.then_inc(s[t + "_r"], 1)

                for i in range(U + 5):
                    if i < U:
                        scores(i)
                    if 3 <= i < U + 3:
                        turn(i - 3)
                    if i >= 6 and i % 2 == 0:
                        av((i - 6) // 2)
                nch = HEADS // hpc
                wo = wo0 if t == "a0" else wo_pad[t]
                pe.wait_ge(s[t + "_oT"], nch)
                for qt in range(NT):
                    for c in range(nch):
                        m = mm(ps[:, 0, P * qt:P * qt + P], oT[:, c, P * qt:P * qt + P], wo[:, c, :],
                               start=(c == 0), stop=(c == nch - 1))
                    m.then_inc(s[t + "_y"], 1)

            def attention2():
                t = "a2"
                mm(ps[:, 0, 0:S], wq2[:], ctxT[:, 0:S], start=True, stop=True).then_inc(s[t + "_proj"], 1)
                for k in range(NT):
                    mm(ps[:, 1, P * k:P * k + P], ctxT[:, P * k:P * k + P], wq2[:], start=True, stop=True) \
                        .then_inc(s[t + "_proj"], 1)
                turn_x(t)
                pe.wait_ge(s["xnT"], before(t, "xnT") + 1)
                mm(ps[:, 6, 0:S], wq2[:], xnT[:], start=True, stop=True).then_inc(s[t + "_qproj"], 1)
                pe.wait_ge(s[t + "_qm"], 1)
                pe.wait_ge(s[t + "_ev_dve"], 1)
                pe.wait_ge(s[t + "_ev_act"], 1)
                for qt in range(NT):
                    mm(ps[:, 2 + qt, 0:S], qm[:, 0, P * qt:P * qt + P], keysT[:, 0, 0:S], start=True, stop=True) \
                        .then_inc(s[t + "_scores"], 1)
                for qt in range(NT):
                    pe.wait_ge(s[t + "_exped"], qt + 1)
                    for k in range(qt + 1):
                        m = tr(ps[:, 4 + qt, P * k:P * k + P], prob[:, qt, P * k:P * k + P], ident[:])
                    m.then_inc(s[t + "_turned"], 1)
                for qt in range(NT):
                    pe.wait_ge(s[t + "_pt_dve"], qt + 1)
                    for k in range(qt + 1):
                        m = mm(ps[:, qt, 0:D], probT[:, qt, k, 0:P], vals[:, 2, P * k:P * k + P],
                               start=(k == 0), stop=(k == qt))
                    m.then_inc(s[t + "_y"], 1)

            def mixture(t):
                cfg = MOE[t]
                ne, nch = cfg["routed"] + cfg["shared"], cfg["chunks"]
                turn_x(t)
                pe.wait_ge(s["xnT"], before(t, "xnT") + 1)
                for k in range(NT):
                    m = mm(ps[:, 6, 8 * k:8 * k + cfg["routed"]], xnT[:, P * k:P * k + P], w_gate[t][:],
                           start=True, stop=True)
                m.then_inc(s[t + "_logits"], 1)
                if t == "f2":
                    pe.wait_ge(s["big2_loaded"], N_BIG)
                    for k in range(NT):
                        m = mm(ps[:, 7, P * k:P * k + P], xnT[:, P * k:P * k + P], w_shared2[:], start=True, stop=True)
                    m.then_inc(s["f2_sh"], 1)
                if t == "f3":
                    pe.wait_ge(s["big3_loaded"], N_BIG)
                groups = expert_groups(t)
                units = [(g, c) for g in range(len(groups)) for c in range(nch)]

                def up(u):
                    g, c = units[u]
                    if u >= 4:
                        pe.wait_ge(s[t + ("_h" if t == "f0" else "_act")], u - 3)
                    e = groups[g][0]
                    if t == "f0":
                        for j in range(2):
                            m = mm(ps[:, u % 4, S * j:S * j + S], w_up[t][:, e, j, P * c:P * c + P], xnT[:],
                                   start=True, stop=True)
                    elif t == "f1":
                        m = mm(ps[:, u % 4, 0:S], w_up[t][:, e:e + 2, :].rearrange("p a b -> p (a b)"), xnT[:],
                               start=True, stop=True)
                    else:
                        m = mm(ps[:, u % 4, 0:S], w_up[t][:, e, P * c:P * c + P], xnT[:], start=True, stop=True)
                    m.then_inc(s[t + "_up"], 1)

                def down(g):
                    pe.wait_ge(s[t + ("_h" if t == "f0" else "_act")], nch * (g + 1))
                    for i, e in enumerate(groups[g]):
                        n = first_of(groups, g) + i
                        if n >= 2:
                            pe.wait_ge(s[t + "_y_used"], NT * (n - 1))
                        for k in range(NT):
                            for c in range(nch):
                                u = g * nch + c
                                w = w_dn[t][:, e, :] if t == "f1" else w_dn[t][:, e, c, :]
                                m = mm(ps[:, 4 + n % 2, P * k:P * k + P], hT[:, u % 8 // 2, u % 2, P * k:P * k + P], w,
                                       start=(c == 0), stop=(c == nch - 1))
                        m.then_inc(s[t + "_down"], 1)

                def biases():
                    pe.wait_ge(s[t + "_comb"], 1)
                    for k in range(NT):
                        m = tr(ps[0:ne, 6, P * k:P * k + P], comb[:, k, 0:ne], ident[:])
                    m.then_inc(s[t + "_combT"], 1)
                    pe.wait_ge(s[t + "_combT_sb"], 1)
                    if t == "f2":
                        pe.wait_ge(s["f2_sh_used"], 1)
                    for k in range(NT):
                        m = mm(ps[:, 7, P * k:P * k + P], combT[0:ne, P * k:P * k + P], b_dn[t][:], start=True, stop=True)
                    m.then_inc(s[t + "_b2"], 1)

                for u in range(nch):
                    up(u)
                for g in range(len(groups)):
                    for u in range(nch * (g + 1), min(nch * (g + 2), len(units))):
                        up(u)
                    down(g)
                    if g == 1 and t != "f0":
                        biases()

            with pe.Fori(0, B):
                for t in PHASES:
                    if t in BEFORE:
                        pe.wait_ge(s["x_done"], before(BEFORE[t], "x_done") + NT)
                    if t == "f0":
                        pe.wait_ge(w_rest, n_rest[0])
                        pe.wait_ge(s["big0_loaded"], N_BIG0)
                    if t == "a0":
                        for k in range(CT + NT):
                            pe.wait_ge(s["normed"], before(t, "normed") + (k + 1 if k < CT else k + 1 + NT))
                            tr(ps[:, 6 + k // 4, P * (k % 4):P * (k % 4) + P], nrm[:, k, :], ident[:]) \
                                .then_inc(s["xT"], 1)
                        pe.wait_ge(s["xnT"], before(t, "xnT") + 2)
                        projections(t)
                        q_projection(t)
                        attention(t)
                    elif t == "a2":
                        attention2()
                    elif t[0] == "a":
                        pe.wait_ge(s["loaded"], N_LOAD)
                        projections(t)
                        turn_x(t)
                        q_projection(t)
                        attention(t)
                    else:
                        mixture(t)
                iteration_end(pe, "pe")

        @block.scalar
        def _(act):
            f = nc.scalar.activation

            def attention(t):
                nk, hpc = ATT[t]["nk"], ATT[t]["hpc"]
                half = nk // P // 2
                U = HEADS * NT

                def exps(u):
                    act.wait_ge(s[t + "_biased"], u + 1)
                    p = prob[:, u % 4, 0:nk]
                    f(p, p, ACT.Exp, bias=negmax[:, u:u + 1], scale=-1.0, accum_out=lsum[:, u // NT, u % NT:u % NT + 1]) \
                        .then_inc(s[t + "_exped"], 1)

                def copy_turned(u):
                    h, qt = u // NT, u % NT
                    act.wait_ge(s[t + "_turned"], 2 * u + 2)
                    if h >= 2:
                        act.wait_ge(s[t + "_av"], h - 1)
                    nc.scalar.copy(probT[:, h % 2, half:2 * half, P * qt:P * qt + P],
                                   ps[:, 5, 0:half * P].rearrange("p (k q) -> p k q", q=P)).then_inc(s[t + "_pt_act"], 1)

                def copy_out(c):
                    act.wait_ge(s[t + "_av"], hpc * (c + 1))
                    if c >= 2:
                        act.wait_ge(s[t + "_oT"], c - 1)
                    nc.scalar.copy(o_raw[:, c % 2, :], ps[:, 6, 0:S]).then_inc(s[t + "_o_raw"], 1)

                for i in range(U + 7):
                    if i < U:
                        exps(i)
                    if 3 <= i < U + 3:
                        copy_turned(i - 3)
                    if i >= 6 and (i - 6) % (NT * hpc) == NT * hpc - 1 and (i - 6) // (NT * hpc) < HEADS // hpc:
                        copy_out((i - 6) // (NT * hpc))

            def mixture(t):
                act.wait_ge(s["xT"], before(t, "xT") + NT)
                nc.scalar.copy(xnT[:], ps[:, 7, 0:S]).then_inc(s["xnT"], 1)
                if t == "f0":
                    act.wait_ge(s[t + "_logit"], 1)
                    f(rt[1][:], logit[:], ACT.Exp, scale=-1.0).then_inc(s[t + "_r_act"], 1)
                elif t == "f1":
                    act.wait_ge(s[t + "_logit"], 1)
                    f(rt[1][:], logit[:], ACT.Abs).then_inc(s[t + "_r_act"], 1)
                    act.wait_ge(s[t + "_r_act"], 1)
                    f(rt[1][:], rt[1][:], ACT.Exp, scale=-1.0).then_inc(s[t + "_r_act"], 1)
                    act.wait_ge(s[t + "_r_act"], 2)
                    f(rt[1][:], rt[1][:], ACT.Ln, bias=1.0).then_inc(s[t + "_r_act"], 1)
                else:
                    act.wait_ge(s[t + "_r_mid"], 1)
                    f(rt[3][:], rt[1][:], ACT.Exp).then_inc(s[t + "_r_act"], 1)
                if t == "f2":
                    act.wait_ge(s["f2_sh_used"], 1)
                    f(gl[:], gl[:], ACT.Gelu).then_inc(s["f2_gl"], 1)
                groups, nch = expert_groups(t), MOE[t]["chunks"]
                for u in range(len(groups) * nch):
                    e, c = groups[u // nch][0], u % nch
                    act.wait_ge(s[t + "_up"], u + 1)
                    h = hT[:, u % 8 // 2, u % 2, :]
                    if t == "f0":
                        if u >= 4:
                            act.wait_ge(s[t + "_h"], u - 3)
                        f(act_tmp[:, u % 4, :], ps[:, u % 4, 0:S], ACT.Silu).then_inc(s[t + "_act"], 1)
                        continue
                    if u >= 8:
                        act.wait_ge(s[t + "_down"], down_before(t, u))
                    col = e // 2 if t == "f1" else e * nch + c
                    f(h, ps[:, u % 4, 0:S], {"f1": ACT.Silu, "f2": ACT.Gelu, "f3": ACT.Relu}[t],
                      bias=b_up[t][:, col:col + 1]).then_inc(s[t + "_act"], 1)

            with act.Fori(0, B):
                for t in PHASES:
                    if t[0] == "f":
                        mixture(t)
                        continue
                    if t == "a0":
                        act.wait_ge(w_early, n_early[0])
                        act.wait_ge(s["xT"], before(t, "xT") + CT + NT)
                        f(kvT[:, S2:KV0], ps[:, 7, 0:S], ACT.Identity, bias=gb0[:, 3:4], scale=gb0[:, 2:3]) \
                            .then_inc(s["xnT"], 1)
                    if t == "a2":
                        act.wait_ge(s[t + "_proj"], 1 + NT)
                        nc.scalar.copy(vals[:, 2, 0:S], ps[:, 1, 0:S]).then_inc(s[t + "_ev_act"], 1)
                    else:
                        nj = len(proj_jobs(t))
                        if t == "a1":
                            act.wait_ge(s["vals_zeroed"], 1)
                        for j in range(1, nj, 2):
                            act.wait_ge(s[t + "_proj"], j + 1)
                            dst, src = proj_out(t, j)
                            nc.scalar.copy(dst, src).then_inc(s[t + "_ev_act"], 1)
                    if t != "a0":
                        act.wait_ge(s["xT"], before(t, "xT") + NT)
                        nc.scalar.copy(xnT[:], ps[:, 7, 0:S]).then_inc(s["xnT"], 1)
                    if t == "a0":
                        for c in range(1, HALF, 2):
                            act.wait_ge(s[t + "_qproj"], c + 1)
                            for j in range(2):
                                f(qm[:, 2 * c + j, :], ps[:, 7, 0:S], ACT.Copy, scale=rowmask[:, j:j + 1]) \
                                    .then_inc(s[t + "_qm_act"], 1)
                        attention(t)
                    elif t == "a2":
                        for qt in range(NT):
                            act.wait_ge(s[t + "_biased"], qt + 1)
                            p = prob[:, qt, 0:S]
                            f(p, p, ACT.Exp, bias=negmax[:, qt:qt + 1], scale=-1.0, accum_out=lsum[:, 0, qt:qt + 1]) \
                                .then_inc(s[t + "_exped"], 1)
                    else:
                        act.wait_ge(s[t + "_qproj"], 1)
                        if t == "a3":
                            f(act_tmp[:, 0, :], ps[:, 6, 0:S], ACT.Identity, bias=bqk3[:, 0:1]).then_inc(s[t + "_q_sb"], 1)
                        else:
                            nc.scalar.copy(act_tmp[:, 0, :], ps[:, 6, 0:S]).then_inc(s[t + "_q_sb"], 1)
                        attention(t)
                iteration_end(act, "act")

        @block.vector
        def _(dve):
            v = nc.vector
            dve.wait_ge(consts_ready, N_CONSTS)
            dve.wait_ge(w_early, n_early[0])
            v.tensor_scalar(bias1[:], mask1_u8[:], -1.0, FAR, ALU.add, ALU.mult)
            v.tensor_copy(vals[:, 0:4, 0:P], bv_pad[:].rearrange("p (c o) -> p c o", o=1).broadcast_to([P, 4, P])) \
                .then_inc(setup_dve, 1)
            dve.wait_ge(setup_pe, 1)
            v.tensor_tensor(bo["a3"][:], bo["a3"][:], ps[:, 0, 0:D], ALU.add).then_inc(setup_dve, 1)
            dve.wait_ge(setup_dve, 2)

            step = [0]

            def link(ins):
                step[0] += 1
                ins.then_inc(s["dve_step"], 1)
                dve.wait_ge(s["dve_step"], step[0])

            def norm(t, src, dst, lo, hi, n_rstd):
                for k in range(lo, hi):
                    ins = v.bn_stats(stats[:, k, :], src(k))
                    if k < hi - 1:
                        continue
                    link(ins)
                for k in range(lo, hi):
                    v.bn_aggr(mv[:, k, :], stats[:, k, :]).then_inc(s["stats"], 1)
                dve.wait_ge(s["rstd"], before(t, "rstd") + n_rstd)
                for k in range(lo, hi):
                    v.tensor_scalar(dst(k), src(k), mv[:, k, 0:1], rstd[:, k:k + 1], ALU.subtract, ALU.mult) \
                        .then_inc(s["normed"], 1)

            def tok_of(k):
                return tok[:, k, :]

            def nrm_of(k):
                return nrm[:, k, :]

            def attention(t):
                nk, hpc, rows, scale = (ATT[t][x] for x in ("nk", "hpc", "rows", "scale"))
                half = nk // P // 2
                U = HEADS * NT

                def add_bias(u):
                    dve.wait_ge(s[t + "_scores"], u + 1)
                    if u >= 4:
                        dve.wait_ge(s[t + "_turned"], 2 * (u - 3))
                    b = 2 * (u % 2)
                    sc = ps[:, b:b + 2, :].rearrange("p b n -> p (b n)")[:, 0:nk]
                    bias = {"a0": bias0[:], "a1": bias1[:, u % NT, :], "a3": bias3[:]}[t]
                    v.tensor_tensor_reduce(out=prob[:, u % 4, 0:nk], in0=sc, in1=bias, scale=-scale, scalar=NEVER,
                                           op0=ALU.add, op1=ALU.min, accum_out=negmax[:, u:u + 1]) \
                        .then_inc(s[t + "_biased"], 1)

                def copy_turned(u):
                    h, qt = u // NT, u % NT
                    dve.wait_ge(s[t + "_turned"], 2 * u + 1)
                    if h >= 2:
                        dve.wait_ge(s[t + "_av"], h - 1)
                    v.tensor_copy(probT[:, h % 2, 0:half, P * qt:P * qt + P],
                                  ps[:, 4, 0:half * P].rearrange("p (k q) -> p k q", q=P)).then_inc(s[t + "_pt_dve"], 1)

                def inverse(c):
                    dve.wait_ge(s[t + "_exped"], NT * hpc * (c + 1))
                    hs = slice(hpc * c, hpc * c + hpc)
                    link(v.reciprocal(linv[:, hs, :], lsum[:, hs, :]))
                    if c >= 2:
                        dve.wait_ge(s[t + "_r"], c - 1)
                    for qt in range(NT):
                        ins = v.tensor_copy(linv_wide[:, c % 2, qt, :].rearrange("p (h r) -> p h r", h=hpc),
                                            linv[:, hs, qt:qt + 1].broadcast_to([P, hpc, rows]))
                    ins.then_inc(s[t + "_linv"], 1)

                def scale_out(c):
                    dve.wait_ge(s[t + "_r"], c + 1)
                    dve.wait_ge(s[t + "_o_raw"], c + 1)
                    v.tensor_tensor(oT[:, c, :], o_raw[:, c % 2, :], ps[:, 7, 0:S], ALU.mult).then_inc(s[t + "_oT"], 1)

                w = NT * hpc
                for i in range(U + 8):
                    if i < U:
                        add_bias(i)
                    if 3 <= i < U + 3:
                        copy_turned(i - 3)
                    if i >= 3 and (i - 3) % w == w - 1 and (i - 3) // w < HEADS // hpc:
                        inverse((i - 3) // w)
                    if i >= 7 and (i - 7) % w == w - 1 and (i - 7) // w < HEADS // hpc:
                        scale_out((i - 7) // w)
                if t != "a0":
                    for k in range(NT):
                        link(v.tensor_tensor(X[:, k, :], X[:, k, :], bo[t][:], ALU.add))
                dve.wait_ge(s[t + "_y"], NT)
                for k in range(NT):
                    v.tensor_tensor(X[:, k, :], X[:, k, :], ps[:, 0, P * k:P * k + P], ALU.add).then_inc(s["x_done"], 1)

            def attention2():
                t = "a2"
                norm(t, tok_of, nrm_of, CT, CT + NT, 1)
                dve.wait_ge(s[t + "_proj"], 1)
                v.tensor_copy(keysT[:, 0, 0:S], ps[:, 0, 0:S]).then_inc(s[t + "_ev_dve"], 1)
                dve.wait_ge(s[t + "_qproj"], 1)
                v.tensor_copy(qm[:, 0, :], ps[:, 6, 0:S]).then_inc(s[t + "_qm"], 1)
                for qt in range(NT):
                    dve.wait_ge(s[t + "_scores"], qt + 1)
                    v.tensor_tensor_reduce(out=prob[:, qt, 0:S], in0=ps[:, 2 + qt, 0:S], in1=bias2[:, qt, :],
                                           scale=-float(D ** -0.5), scalar=NEVER, op0=ALU.add, op1=ALU.min,
                                           accum_out=negmax[:, qt:qt + 1]).then_inc(s[t + "_biased"], 1)
                for qt in range(NT):
                    dve.wait_ge(s[t + "_turned"], qt + 1)
                    n = P * (qt + 1)
                    v.tensor_copy(probT[:, qt, 0:qt + 1, 0:P], ps[:, 4 + qt, 0:n].rearrange("p (k q) -> p k q", q=P)) \
                        .then_inc(s[t + "_pt_dve"], 1)
                dve.wait_ge(s[t + "_exped"], NT)
                link(v.reciprocal(linv[:, 0, :], lsum[:, 0, :]))
                for qt in range(NT):
                    dve.wait_ge(s[t + "_y"], qt + 1)
                    v.scalar_tensor_tensor(out=X[:, qt, :], in0=ps[:, qt, 0:D], scalar=linv[:, 0, qt:qt + 1],
                                           in1=X[:, qt, :], op0=ALU.mult, op1=ALU.add).then_inc(s["x_done"], 1)

            def router(t):
                E = MOE[t]["routed"]
                if E < 8:
                    link(v.memset(logit[:], -1e38))
                fixed = 1.0 / 3.0 if t == "f0" else MOE[t]["fixed"]
                v.memset(comb[:], fixed)
                dve.wait_ge(s[t + "_logits"], 1)
                lg = ps[:, 6, 0:8 * NT].rearrange("p (k e) -> p k e", e=8)[:, :, 0:E]
                if t in b_gate:
                    for k in range(NT):
                        ins = v.tensor_tensor(logit[:, k, 0:E], b_gate[t][:], lg[:, k, :], ALU.add)
                else:
                    ins = v.tensor_copy(logit[:, :, 0:E], lg)
                ins.then_inc(s[t + "_logit"], 1)
                dve.wait_ge(s[t + "_logit"], 1)
                for k in range(NT):
                    ins = v.max(top8[:, k, :], logit[:, k, :])
                link(ins)
                if t in ("f2", "f3"):
                    for k in range(NT):
                        ins = v.tensor_scalar(rt[1][:, k, :], logit[:, k, :], top8[:, k, 0:1], None, ALU.subtract)
                    ins.then_inc(s[t + "_r_mid"], 1)
                link(v.memset(top8[:, :, 2:8], NEVER))
                for k in range(NT):
                    ins = v.match_replace(cut[:, k, :], top8[:, k, :], logit[:, k, :], -NEVER)
                link(ins)
                link(v.tensor_tensor(rt[0][:], cut[:], logit[:], ALU.not_equal))
                if t == "f0":
                    dve.wait_ge(s[t + "_r_act"], 1)
                    link(v.tensor_scalar(rt[2][:], rt[1][:], 1.0, None, ALU.add))
                    link(v.reciprocal(rt[3][:], rt[2][:]))
                elif t == "f1":
                    dve.wait_ge(s[t + "_r_act"], 3)
                    v.scalar_tensor_tensor(out=rt[2][:], in0=logit[:], scalar=0.0, in1=rt[1][:], op0=ALU.max,
                                           op1=ALU.add).then_inc(s[t + "_r_mid"], 2)
                    dve.wait_ge(s[t + "_r_pool"], 1)
                else:
                    dve.wait_ge(s[t + "_r_act"], 1)
                if t == "f1":
                    v.tensor_tensor(comb[:, :, 0:E], rt[3][:, :, 0:E], rt[0][:, :, 0:E], ALU.mult).then_inc(s[t + "_comb"], 1)
                else:
                    link(v.tensor_tensor(rt[4][:], rt[3][:], rt[0][:], ALU.mult))
                    link(v.tensor_reduce(rsum[:], (rt[3] if t == "f3" else rt[4])[:], AX_X, ALU.add))
                    link(v.reciprocal(rinv[:], rsum[:]))
                    for k in range(NT):
                        ins = v.tensor_scalar(comb[:, k, 0:E], rt[4][:, k, 0:E], rinv[:, k:k + 1],
                                              1.0 / 3.0 if t == "f0" else 1.0, ALU.mult, ALU.mult)
                    ins.then_inc(s[t + "_comb"], 1)
                dve.wait_ge(s[t + "_comb"], 1)

            def mixture(t):
                groups, nch = expert_groups(t), MOE[t]["chunks"]
                ne = first_of(groups, len(groups))
                norm(t, tok_of, nrm_of, CT, CT + NT, 1)
                router(t)
                total = acc if t == "f2" else X
                if t == "f2":
                    dve.wait_ge(s["f2_sh"], 1)
                    for k in range(NT):
                        ins = v.tensor_tensor(gl[:, k, :], sb2[:, 0, :], ps[:, 7, P * k:P * k + P], ALU.add)
                    ins.then_inc(s["f2_sh_used"], 1)
                    dve.wait_ge(s["f2_gl"], 1)
                    link(v.tensor_scalar(acc[:], gl[:], 0.5, None, ALU.mult))

                def hidden(u):
                    dve.wait_ge(s[t + "_act"], u + 1)
                    if u >= 8:
                        dve.wait_ge(s[t + "_down"], down_before(t, u))
                    v.tensor_tensor(hT[:, u % 8 // 2, u % 2, :], act_tmp[:, u % 4, :], ps[:, u % 4, S:2 * S], ALU.mult) \
                        .then_inc(s[t + "_h"], 1)

                def add_expert(n, e):
                    dve.wait_ge(s[t + "_down"], n + 1)
                    for k in range(NT):
                        if n >= 1:
                            dve.wait_ge(s[t + "_y_used"], NT * (n - 1) + k + 1)
                        last = t == "f0" and n == ne - 1
                        v.scalar_tensor_tensor(out=total[:, k, :], in0=ps[:, 4 + n % 2, P * k:P * k + P],
                                               scalar=comb[:, k, e:e + 1], in1=total[:, k, :], op0=ALU.mult,
                                               op1=ALU.add).then_inc(s["x_done" if last else t + "_y_used"], 1)

                def turned_weights():
                    dve.wait_ge(s[t + "_combT"], 1)
                    v.tensor_copy(combT[0:ne, :], ps[0:ne, 6, 0:S]).then_inc(s[t + "_combT_sb"], 1)

                if t == "f0":
                    for u in range(nch):
                        hidden(u)
                for g in range(len(groups)):
                    if t == "f0":
                        for u in range(nch * (g + 1), min(nch * (g + 2), nch * len(groups))):
                            hidden(u)
                    for i, e in enumerate(groups[g]):
                        add_expert(first_of(groups, g) + i, e)
                    if g == 1 and t != "f0":
                        turned_weights()
                if t == "f0":
                    return
                dve.wait_ge(s[t + "_b2"], 1)
                dve.wait_ge(s[t + "_y_used"], NT * ne)
                for k in range(NT):
                    ins = v.tensor_tensor(total[:, k, :], total[:, k, :], ps[:, 7, P * k:P * k + P], ALU.add)
                    if t == "f2":
                        link(ins)
                    else:
                        ins.then_inc(s["x_done"], 1)
                if t == "f2":
                    norm(t, lambda k: acc[:, k - CT, :], nrm_of, CT, CT + NT, 2)
                    dve.wait_ge(s["normed"], before("f2", "normed") + 2 * NT)
                    for k in range(NT):
                        n = nrm[:, CT + k, :]
                        link(v.tensor_tensor(n, n, sb2[:, 1, :], ALU.mult))
                        link(v.tensor_tensor(n, n, sb2[:, 2, :], ALU.add))
                        v.tensor_tensor(X[:, k, :], X[:, k, :], n, ALU.add).then_inc(s["x_done"], 1)

            with dve.Fori(0, B):
                step[0] = 0
                for t in PHASES:
                    if t in BEFORE:
                        dve.wait_ge(s["x_done"], before(BEFORE[t], "x_done") + NT)
                    if t[0] == "f":
                        if t == "f0":
                            dve.wait_ge(w_rest, n_rest[0])
                        mixture(t)
                        continue
                    if t == "a2":
                        attention2()
                        continue
                    if t == "a0":
                        dve.wait_ge(s["loaded"], N_LOAD)
                        norm(t, tok_of, nrm_of, 0, CT + NT, 1)
                        v.tensor_scalar(bias0[:, 0:S2], mask_u8[:, 0, :], -1.0, FAR, ALU.add, ALU.mult)
                        v.tensor_scalar(bias3[:], mask_u8[:, 1, :], -1.0, FAR, ALU.add, ALU.mult)
                        dve.wait_ge(s["normed"], before(t, "normed") + CT + NT)
                        norm(t, nrm_of, nrm_of, CT, CT + NT, 2)
                        dve.wait_ge(s["xT"], before(t, "xT") + CT)
                        v.tensor_scalar(kvT[:, 0:S2], ps[:, 6, 0:S2], gb0[:, 0:1], gb0[:, 1:2], ALU.mult, ALU.add) \
                            .then_inc(s["xnT"], 1)
                    else:
                        norm(t, tok_of, nrm_of, CT, CT + NT, 1)
                        dve.wait_ge(s["vals_zeroed"], 1)
                    for j in range(0, len(proj_jobs(t)), 2):
                        dve.wait_ge(s[t + "_proj"], j + 1)
                        dst, src = proj_out(t, j)
                        if t == "a3" and j == 0:
                            ins = v.tensor_scalar(dst, src, bqk3[:, 1:2], None, ALU.add)
                        else:
                            ins = v.tensor_copy(dst, src)
                        ins.then_inc(s[t + "_ev_dve"], 1)
                    if t == "a0":
                        for c in range(0, HALF, 2):
                            dve.wait_ge(s[t + "_qproj"], c + 1)
                            for j in range(2):
                                v.tensor_scalar(qm[:, 2 * c + j, :], ps[:, 6, 0:S], rowmask[:, j:j + 1], None, ALU.mult) \
                                    .then_inc(s[t + "_qm"], 1)
                    else:
                        dve.wait_ge(s[t + "_q_sb"], 1)
                        for h in range(HEADS):
                            v.tensor_scalar(qm[:, h, :], act_tmp[:, 0, :], rowmask[:, 2 + h:3 + h], None, ALU.mult) \
                                .then_inc(s[t + "_qm"], 1)
                    attention(t)
                iteration_end(dve, "dve")


def kernel(**inputs):
    import numpy as _np
    import concourse.bacc as _bacc
    from concourse import mybir as _mybir
    from concourse.bass_utils import run_bass_kernel_spmd as _run

    given = {k: _np.asarray(v) for k, v in inputs.items()}
    given["mask0"] = given.pop("mask_BxS2_bk0")
    given["mask3"] = given.pop("mask_BxS2_bf1")
    m = given.pop("mask_1x1xSxS2_bk0")
    given["mask1"] = m.reshape(m.shape[2:])
    given["ctxT"] = given["ctx_1024"].transpose(0, 2, 1)
    for name in ("L1_xattn_Wq", "L1_xattn_Wk", "L1_xattn_Wv", "L1_xattn_Wo", "L1_ffn_routing_W", "L2_xattn_Wq",
                 "L3_xattn_Wq", "L3_xattn_Wk", "L3_xattn_Wv", "L3_xattn_Wo"):
        given[name + "T"] = given.pop(name).T
    for name in ("L1_ffn_rb1", "L2_ffn_b1", "L3_ffn_sb1", "L3_ffn_rb1"):
        given[name + "c"] = given.pop(name).reshape(-1, P).T

    nc = _bacc.Bacc("TRN2", target_bir_lowering=False, num_devices=1)
    arrays, aps = {}, {}
    for name, x in given.items():
        x = _np.ascontiguousarray(x)
        arrays[f"in_{name}_dram"] = x
        aps[name] = nc.dram_tensor(f"in_{name}_dram", x.shape, _mybir.dt.from_np(x.dtype), kind="ExternalInput").ap()
    shape = given["x"].shape
    out = nc.dram_tensor("out_0_dram", shape, _mybir.dt.float32, kind="ExternalOutput").ap()
    build(nc, aps, out)
    r = _run(nc, [arrays], core_ids=[0])
    return r.results[0]["out_0_dram"]
```

```python
from contextlib import ExitStack

import concourse.bass as bass
from concourse import mybir

ALU = mybir.AluOpType
ACT = mybir.ActivationFunctionType
F32 = mybir.dt.float32
F32R = mybir.dt.float32r
U8 = mybir.dt.uint8
AX_X = mybir.AxisListType.X
AX_XY = mybir.AxisListType.XY

P = 128
D = 128
EPS = 1e-5
FAR = 1e30
NEVER = 3.0e38
HEADS = 16
MOE = {
    "f0": dict(routed=8, shared=1, fixed=1.0, chunks=2),
    "f1": dict(routed=8, shared=1, fixed=1.0, chunks=1),
    "f2": dict(routed=8, shared=0, fixed=0.0, chunks=4),
    "f3": dict(routed=4, shared=2, fixed=0.5, chunks=4),
}
PHASES = ["a0", "f0", "a1", "f1", "a2", "f2", "a3", "f3"]
RUNS = [(t, r) for t in PHASES for r in range(2)]


def build(nc, a, out):
    B, S, _ = a["x"].shape
    S2 = a["ctx_1024"].shape[1]
    NT, CT = S // P, S2 // P
    KV0 = S2 + S
    HALF = HEADS // 2
    ATT = {
        "a0": dict(nk=KV0, hpc=2, rows=64, scale=1.0 / 8.0),
        "a1": dict(nk=S2, hpc=4, rows=32, scale=float(8 ** -0.5)),
        "a3": dict(nk=S2, hpc=4, rows=32, scale=float(8 ** -0.5)),
    }

    with ExitStack() as ctx:
        def sb(name, shape, dt=F32):
            return ctx.enter_context(nc.sbuf_tensor(name, shape, dt))

        wq0 = sb("wq0", [P, 1024])
        wkv0 = sb("wkv0", [P, 2048])
        wo0 = sb("wo0", [P, HALF, D])
        wqkv = {t: sb("wqkv_" + t, [P, 3, D]) for t in ("a1", "a3")}
        wo_pad = {t: sb("wo_pad_" + t, [P, 4, D]) for t in ("a1", "a3")}
        wq2 = sb("wq2", [P, D])
        w_up = {"f1": sb("up_f1", [P, 10, 64])}
        w_dn = {"f1": sb("dn_f1", [P, 10, D])}
        big = sb("big", [P, 2 * 8 * 512])
        w_up["f0"] = big[:, 0:9 * 512].rearrange("p (e j f) -> p e j f", e=9, j=2)
        w_dn["f0"] = big[:, 9 * 512:9 * 768].rearrange("p (e c o) -> p e c o", e=9, c=2)
        w_up["f2"] = w_up["f3"] = big_up = big[:, 0:4096].rearrange("p (e f) -> p e f", e=8)
        w_dn["f2"] = w_dn["f3"] = big_dn = big[:, 4096:8192].rearrange("p (e c o) -> p e c o", e=8, c=4)
        w_shared2 = sb("w_shared2", [P, D])
        w_gate = {t: sb("gate_" + t, [P, MOE[t]["routed"]]) for t in MOE}
        b_gate = {"f1": sb("bgate_f1", [P, 8]), "f3": sb("bgate_f3", [P, 4])}
        b_up = {"f1": sb("bup_f1", [P, 5]), "f2": sb("bup_f2", [P, 32]), "f3": sb("bup_f3", [P, 24])}
        b_dn = {"f1": sb("bdn_f1", [9, D]), "f2": sb("bdn_f2", [8, D]), "f3": sb("bdn_f3", [6, D])}
        gb0 = sb("gb0", [P, 4])
        split = sb("split", [P, 2])
        lane8 = sb("lane8", [P, 4])
        bqk3 = sb("bqk3", [P, 2, 4])
        bqk3_split = sb("bqk3_split", [P, 2, 4])
        bv_pad = sb("bv_pad", [P, 4])
        bo = {"a1": sb("bo_a1", [P, D]), "a3": sb("bo_a3", [P, D])}
        sb2 = sb("sb2", [P, 3, D])
        ident = sb("ident", [P, P])
        rowmask = sb("rowmask", [P, 2 + HEADS])
        neg_half = sb("neg_half", [P, 6])
        pos_half = sb("pos_half", [P, 2, 8])
        bias1 = sb("bias1", [P, NT, S2])
        bias2 = sb("bias2", [P, NT, S])
        mask1_u8 = sb("mask1_u8", [P, NT, S2], U8)
        tok = sb("tok", [P, 2, CT + NT, D])
        X = tok[:, :, CT:CT + NT, :]
        nrm = sb("nrm", [P, CT + NT, D])
        stats = sb("stats", [P, CT + NT, 6])
        mv = sb("mv", [P, CT + NT, 2])
        var_eps = sb("var_eps", [P, CT + NT])
        rstd = sb("rstd", [P, CT + NT])
        ctxT = sb("ctxT", [P, 2, S2])
        kvT = sb("kvT", [P, KV0])
        xnT = sb("xnT", [P, 2, S])
        mask_u8 = sb("mask_u8", [P, 2, 2, S2], U8)
        bias0 = sb("bias0", [P, KV0])
        bias3 = bias0[:, 0:S2]
        with nc.sbuf_tensor("keysT", [P, HALF, KV0], F32) as keysT, \
                nc.sbuf_tensor("qm", [P, HEADS, S], F32) as qm:
            pass
        kst = sb("kst", [P, 4, S2], F32R)
        qst = sb("qst", [P, 4, S], F32R)
        qst_m = sb("qst_m", [P, HEADS, S], F32R)
        room = sb("room", [P, HALF * KV0 + HEADS * S - 4 * S2 - 4 * S - HEADS * S])
        vals = sb("vals", [P, 6, 1024])
        vals_pad = vals[:, 0:2, :].rearrange("p a b -> p (a b)").rearrange("p (k h r) -> p k h r", k=CT, h=HEADS)
        prob = sb("prob", [P, 4, KV0])
        probT = sb("probT", [P, 24, P])
        negmax = sb("negmax", [P, HEADS * NT])
        lsum = sb("lsum", [P, HEADS, NT])
        linv = sb("linv", [P, HEADS, NT])
        linv_wide = sb("linv_wide", [P, 2, NT, P])
        o_raw = sb("o_raw", [P, 2, S])
        oT = sb("oT", [P, HALF, S])
        hT = keysT[:, 0:4, 0:512].rearrange("p a (b c) -> p a b c", b=2)
        act_tmp = prob[:, :, 0:S]
        logit = sb("logit", [P, NT, 8])
        top8 = sb("top8", [P, NT, 8])
        cut = sb("cut", [P, NT, 8])
        rt = [sb(f"rt{i}", [P, NT, 8]) for i in range(5)]
        rsum = sb("rsum", [P, NT])
        rinv = sb("rinv", [P, NT])
        comb = sb("comb", [P, 2, NT, 10])
        combT = sb("combT", [16, S])
        acc = o_raw[:, 0, :].rearrange("p (k d) -> p k d", d=D)
        gl = sb("gl", [P, 2, NT, D])
        end_stats = sb("end_stats", [P, NT, 6])
        end_mv = sb("end_mv", [P, NT, 2])
        end_var = sb("end_var", [P, NT])
        end_rstd = sb("end_rstd", [P, NT])
        ps = ctx.enter_context(nc.psum_tensor("ps", [P, 8, 512], F32))

        def sem(name):
            return ctx.enter_context(nc.semaphore(name))

        w_early, w_rest, w_out = sem("w_early"), sem("w_rest"), sem("w_out")
        masks = sem("masks")
        zeroed = sem("zeroed")
        consts_ready = sem("consts_ready")
        setup_dve, setup_pe = sem("setup_dve"), sem("setup_pe")
        go = {e: sem("go_" + e) for e in ("pe", "act", "dve", "pool")}
        names = ["stats", "rstd", "normed", "xT", "xnT", "x_done", "loaded", "vals_zeroed", "big0_loaded", "big2_loaded", "big3_loaded", "dve_step", "pool_step", "stored", "ended"]
        for t in PHASES:
            if t[0] == "a":
                names += [t + "_" + n for n in ("proj", "ev_dve", "ev_act", "qproj", "qm", "scores", "biased", "exped",
                                                "turned", "pt_dve", "y")]
                if t != "a2":
                    names += [t + "_" + n for n in ("pt_act", "av", "o_raw", "linv", "r", "oT",
                                                    "qm_act")]
            else:
                names += [t + "_" + n for n in ("logits", "logit", "r_act", "comb", "up", "act", "down", "y_used")]
                names += ["f0_h"] if t == "f0" else [t + "_" + n for n in ("combT", "combT_sb", "b2", "r_mid")]
        names += ["f1_r_pool", "f2_sh", "f2_gl", "f2_e_stats", "f2_e_rstd"]
        s = {n: sem(n) for n in names}
        nums = sorted(x.num for x in s.values())
        assert nums == list(range(nums[0], nums[0] + len(nums)))
        block = ctx.enter_context(nc.Block())

        def unit(t, u):
            c, rest = divmod(u, NT * ATT[t]["hpc"])
            qt, j = divmod(rest, ATT[t]["hpc"])
            return c * ATT[t]["hpc"] + j, qt

        def turned_at(t, u):
            n = ATT[t]["nk"] // P
            return u % (24 // n) * n

        def contracted(t, u):
            old = u - 24 // (ATT[t]["nk"] // P)
            return old // ATT[t]["hpc"] + 1 if old >= 0 else 0

        def nth(t, r):
            return RUNS.index((t, r))

        def before(t, r, name):
            once = {"stats": NT, "rstd": 1, "normed": NT, "xT": NT, "xnT": 1, "x_done": NT}[name]
            more = {"stats": CT + NT, "rstd": 1, "normed": CT + NT, "xT": CT, "xnT": 1}.get(name, 0)
            return once * nth(t, r) + more * min(nth(t, r), 2)

        def since(t, r, name):
            if r == 0:
                return 0
            if t == "a2":
                return {"proj": 1 + NT, "scores": NT, "biased": NT, "exped": NT, "turned": NT, "pt_dve": NT,
                        "y": NT}.get(name, 1)
            if t[0] == "a":
                nj, nch, units = len(proj_jobs(t)), HEADS // ATT[t]["hpc"], HEADS * NT
                if t != "a0" and name in ("proj", "ev_act", "ev_dve"):
                    return 8 if name == "ev_dve" else 9
                return {"proj": nj, "ev_dve": (nj + 1) // 2, "ev_act": nj // 2, "qproj": HALF,
                        "qm": HALF, "qm_act": HALF, "scores": units,
                        "biased": units, "exped": units, "turned": 2 * units, "pt_dve": units, "pt_act": units,
                        "av": units // ATT[t]["hpc"], "y": NT}.get(name, nch)
            groups = expert_groups(t)
            ne, units = first_of(groups, len(groups)), len(groups) * MOE[t]["chunks"]
            return {"up": units, "act": units, "h": units, "down": ne, "y_used": NT * (ne - (t == "f0")),
                    "r_act": 3 if t == "f1" else 1}.get(name, 1)

        def proj_jobs(t, r=0):
            if t == "a0":
                keys = [(hi - lo, wkv0[:, P * c:P * c + P], kvT[:, lo:hi])
                        for c in range(HALF) for lo, hi in ((0, S2), (S2, KV0))]
                return keys + [(512, kvT[:, P * k:P * k + P], wkv0[:, 1024 + 512 * j:1536 + 512 * j])
                               for k in range(KV0 // P) for j in range(2)]
            return []

        def proj_out(t, j):
            if t == "a0":
                if j < 2 * HALF:
                    lo, hi = ((0, S2), (S2, KV0))[j % 2]
                    return keysT[:, j // 2, lo:hi], ps[:, j % 6, 0:hi - lo]
                k, half = (j - 2 * HALF) // 2, j % 2
                return vals[:, k, 512 * half:512 * half + 512], ps[:, j % 6, :]

        def stack_out(g, keys):
            return ps[:, (0, 2, 1, 3)[g], :] if keys else ps[:, 4 + g, 0:S]

        def turned_bank(t, u, half):
            return 4 + half if t == "a0" or u % 2 == 0 else 1 + 2 * half

        def expert_groups(t):
            e, n = MOE[t]["routed"], MOE[t]["shared"]
            if t == "f1":
                return [[8]] + [[i, i + 1] for i in range(0, e, 2)]
            return [[i] for i in (*range(e, e + n), *range(e))]

        def first_of(groups, g):
            return sum(len(x) for x in groups[:g])

        def down_before(t, u):
            return first_of(expert_groups(t), (u - 8) // MOE[t]["chunks"] + 1)

        def iteration_end(eng, me):
            eng.drain().then_inc(s["ended"], 1)
            eng.wait_ge(go[me], 1)
            eng.sem_clear(go[me])

        n_early, n_rest = [0], [0]
        N_LOAD, N_BIG0, N_BIG = 16 * 10, 16 * 13, 16 * 4
        N_CONSTS = 1 + NT + 2

        @block.sync
        def _(sp):
            def early(dst, src):
                sp.dma_start(dst, src).then_inc(w_early, 16)
                n_early[0] += 16

            def rest(dst, src):
                sp.dma_start(dst, src).then_inc(w_rest, 16)
                n_rest[0] += 16

            def col(name):
                return a[name].rearrange("(p o) -> p o", o=1)

            for j, n in enumerate(("g1", "b1", "g2", "b2")):
                early(gb0[:, j:j + 1], col("L0_xattn_" + n))
            early(wkv0[:], a["L0_xattn_Wkv"])
            early(wq0[:], a["L0_xattn_Wq"])
            early(wo0[:], a["L0_xattn_Wout"].rearrange("(c p) o -> p c o", p=P))
            early(mask1_u8[:], a["mask1"].rearrange("(t p) k -> p t k", p=P))

            for t, l in (("a1", "L1"), ("a3", "L3")):
                early(bo[t][:], a[f"{l}_xattn_bo"].rearrange("(o d) -> o d", o=1).broadcast_to([P, D]))
            sp.wait_ge(zeroed, 5)
            for t, l in (("a1", "L1"), ("a3", "L3")):
                wo = a[f"{l}_xattn_WoT"].rearrange("(c j i) o -> j i c o", c=4, j=4)
                for j in range(4):
                    early(wo_pad[t][32 * j:32 * j + 8], wo[j])
            bv = a["L3_xattn_bv"].rearrange("(c j i) -> j i c", c=4, j=4)
            with nc.allow_non_contiguous_dma(reason="128 biases into columns"):
                for j in range(4):
                    early(bv_pad[32 * j:32 * j + 8, :], bv[j])
            rest(w_gate["f0"][:], a["L0_ffn_Wg"])
            for t, l in (("a1", "L1"), ("a3", "L3")):
                for j, n in enumerate("qkv"):
                    rest(wqkv[t][:, j, :], a[f"{l}_xattn_W{n}T"])
            with nc.allow_non_contiguous_dma(reason="128 biases into columns"):
                for j, n in enumerate(("bq", "bk")):
                    for k in range(4):
                        early(bqk3[32 * k:32 * k + 32, j, :], a["L3_xattn_" + n].rearrange("(g r) -> r g", r=32))
            rest(w_gate["f1"][:], a["L1_ffn_routing_WT"])
            rest(b_gate["f1"][:], a["L1_ffn_expert_bias"].rearrange("(o d) -> o d", o=1).broadcast_to([P, 8]))
            rest(w_up["f1"][:, 0:8, :], a["L1_ffn_rW1"].rearrange("e d f -> d e f"))
            rest(w_up["f1"][:, 8, :], a["L1_ffn_sW1"])
            rest(b_dn["f1"][0:8, :], a["L1_ffn_rb2"])
            rest(b_dn["f1"][8:9, :], a["L1_ffn_sb2"].rearrange("(o d) -> o d", o=1))
            rest(wq2[:], a["L2_xattn_WqT"])
            rest(w_gate["f2"][:], a["L2_ffn_gate_W"])
            rest(w_shared2[:], a["L2_ffn_shared_W"])
            rest(b_up["f2"][:], a["L2_ffn_b1c"])
            rest(b_dn["f2"][:], a["L2_ffn_b2"])
            for j, n in enumerate(("shared_b", "gamma", "beta")):
                rest(sb2[:, j, :], a["L2_ffn_" + n].rearrange("(o d) -> o d", o=1).broadcast_to([P, D]))
            rest(w_gate["f3"][:], a["L3_ffn_gate_w"])
            rest(b_gate["f3"][:], a["L3_ffn_gate_b"].rearrange("(o d) -> o d", o=1).broadcast_to([P, 4]))
            rest(b_up["f3"][:, 0:16], a["L3_ffn_rb1c"])
            rest(b_up["f3"][:, 16:24], a["L3_ffn_sb1c"])
            rest(b_dn["f3"][0:4, :], a["L3_ffn_rb2"])
            rest(b_dn["f3"][4:6, :], a["L3_ffn_sb2"])
            rest(b_up["f1"][:, 0:4], a["L1_ffn_rb1c"])
            rest(b_up["f1"][0:64, 4:5], col("L1_ffn_sb1"))
            w2 = a["L1_ffn_rW2"].rearrange("(q two) h o -> two h q o", two=2)
            pad_dn = w_dn["f1"][:].rearrange("p (q two) o -> p two q o", two=2)
            rest(pad_dn[0:64, 0, 0:4, :], w2[0])
            rest(pad_dn[64:128, 1, 0:4, :], w2[1])
            rest(w_dn["f1"][0:64, 8, :], a["L1_ffn_sW2"])

            with sp.Fori(0, B // 2) as i:
                def load(dst, src):
                    sp.dma_start(dst, src).then_inc(s["loaded"], 16)

                for r in range(2):
                    one = bass.ds(2 * i + r, 1)
                    load(tok[:, r, 0:CT, :], a["ctx_1024"][one].rearrange("o (t p) d -> p (o t) d", p=P))
                    load(X[:, r], a["x"][one].rearrange("o (t p) d -> p (o t) d", p=P))
                    load(mask_u8[:, r, 0, :], a["mask0"][one, :].broadcast_to([P, S2]))
                    load(mask_u8[:, r, 1, :], a["mask3"][one, :].broadcast_to([P, S2]))
                    load(ctxT[:, r, :], a["ctxT"][one].rearrange("o d s -> d (o s)"))

                def load_big(which, dst, src):
                    sp.dma_start(dst, src).then_inc(s[which], 16)

                load_big("big0_loaded", w_up["f0"][:, 8, 0, :], a["L0_ffn_Ws1"])
                load_big("big0_loaded", w_up["f0"][:, 8, 1, :], a["L0_ffn_Ws3"])
                load_big("big0_loaded", w_dn["f0"][:, 8], a["L0_ffn_Ws2"].rearrange("(c p) o -> p c o", p=P))
                load_big("big0_loaded", w_up["f0"][:, 0:8, 0, :], a["L0_ffn_We1"].rearrange("e d f -> d e f"))
                load_big("big0_loaded", w_up["f0"][:, 0:8, 1, :], a["L0_ffn_We3"].rearrange("e d f -> d e f"))
                for e in range(8):
                    load_big("big0_loaded", w_dn["f0"][:, e], a["L0_ffn_We2"][e].rearrange("(c p) o -> p c o", p=P))
                sp.wait_ge(s["x_done"], before("f0", 1, "x_done") + NT)

                for e in range(0, 8, 4):
                    load_big("big2_loaded", big_up[:, e:e + 4, :], a["L2_ffn_W1"][e:e + 4].rearrange("e d f -> d e f"))
                    load_big("big2_loaded", big_dn[:, e:e + 4], a["L2_ffn_W2"][e:e + 4].rearrange("e (c p) o -> p e c o", p=P))
                sp.wait_ge(s["x_done"], before("f2", 1, "x_done") + NT)
                load_big("big3_loaded", big_up[:, 0:4, :], a["L3_ffn_rw1"].rearrange("e d f -> d e f"))
                load_big("big3_loaded", big_up[:, 4:6, :], a["L3_ffn_sw1"].rearrange("e d f -> d e f"))
                load_big("big3_loaded", big_dn[:, 0:4], a["L3_ffn_rw2"].rearrange("e (c p) o -> p e c o", p=P))
                load_big("big3_loaded", big_dn[:, 4:6], a["L3_ffn_sw2"].rearrange("e (c p) o -> p e c o", p=P))
                for r in range(2):
                    sp.wait_ge(s["x_done"], before("f3", r, "x_done") + NT)
                    sp.dma_start(out[bass.ds(2 * i + r, 1)].rearrange("o (t p) d -> p (o t) d", p=P), X[:, r]) \
                        .then_inc(s["stored"], 16)
                sp.wait_ge(s["stored"], 32)
                sp.wait_ge(s["ended"], 4)
                sp.sem_clear(range(nums[0], nums[-1] + 1))
                for e in go:
                    sp.sem_inc(go[e], 1)


        @block.gpsimd
        def _(pool):
            nc.gpsimd.memset(wo_pad["a1"][:], 0.0).then_inc(zeroed, 1)
            nc.gpsimd.memset(wo_pad["a3"][:], 0.0).then_inc(zeroed, 1)
            nc.gpsimd.memset(bv_pad[:], 0.0).then_inc(zeroed, 1)
            nc.gpsimd.memset(b_up["f1"][:], 0.0).then_inc(zeroed, 1)
            nc.gpsimd.memset(w_dn["f1"][:], 0.0).then_inc(zeroed, 1)
            nc.gpsimd.memset(w_up["f1"][:, 9, :], 0.0).then_inc(zeroed, 1)
            nc.gpsimd.memset(bias0[:], 0.0).then_inc(zeroed, 1)
            nc.gpsimd.memset(neg_half[:], -0.5).then_inc(zeroed, 1)
            nc.gpsimd.memset(pos_half[:], 0.5).then_inc(zeroed, 1)
            nc.gpsimd.memset(ident[:], 0.0).then_inc(zeroed, 1)
            nc.gpsimd.memset(rowmask[:], 1.0).then_inc(zeroed, 1)
            nc.gpsimd.memset(bias2[:], 0.0).then_inc(zeroed, 1)
            pool.wait_ge(zeroed, 12)
            nc.gpsimd.affine_select(out=ident[:], in_=ident[:], compare_op=ALU.not_equal, fill=1.0, base=0,
                                    pattern=[[-1, P]], channel_multiplier=1).then_inc(consts_ready, 1)
            for t in range(NT):
                nc.gpsimd.affine_select(out=bias2[:, t, :], in_=bias2[:, t, :], compare_op=ALU.is_ge, fill=-FAR,
                                        base=P * t, pattern=[[-1, S]], channel_multiplier=1).then_inc(consts_ready, 1)
            for c0, n, w in ((0, 2, 64), (2, HEADS, 8)):
                m = rowmask[:, c0:c0 + n]
                nc.gpsimd.affine_select(out=m, in_=m, compare_op=ALU.is_ge, fill=0.0, base=0, pattern=[[-w, n]],
                                        channel_multiplier=1).then_inc(masks, 1)
            pool.wait_ge(masks, 2)
            for c0, n, w in ((0, 2, 64), (2, HEADS, 8)):
                m = rowmask[:, c0:c0 + n]
                nc.gpsimd.affine_select(out=m, in_=m, compare_op=ALU.is_ge, fill=0.0, base=w - 1, pattern=[[w, n]],
                                        channel_multiplier=-1).then_inc(consts_ready, 1)
            with pool.Fori(0, B // 2):
                def root(mean_var, tmp, dst, signal):
                    nc.gpsimd.tensor_scalar(tmp, mean_var[:, :, 1], EPS, None, ALU.add).then_inc(s["pool_step"], 1)
                    n_pool[0] += 1
                    pool.wait_ge(s["pool_step"], n_pool[0])
                    nc.gpsimd.tensor_tensor(dst, tmp, neg_half[:, 0:tmp.shape[1]], ALU.pow).then_inc(signal, 1)

                n_pool = [0]

                def ready_next(t, r):
                    n = before(t, r, "stats")
                    if t == "a0":
                        pool.wait_ge(s["stats"], n + CT + NT)
                        root(mv[:], var_eps[:], rstd[:], s["rstd"])
                        n += CT + NT
                    pool.wait_ge(s["stats"], n + NT)
                    root(mv[:, CT:CT + NT, :], var_eps[:, CT:CT + NT], rstd[:, CT:CT + NT], s["rstd"])
                    if t == "f1":
                        pool.wait_ge(s["f1_r_mid"], since(t, r, "r_mid") + 1)
                        nc.gpsimd.tensor_tensor(rt[3][:], rt[2][:], pos_half[:], ALU.pow).then_inc(s["f1_r_pool"], 1)

                ready_next(*RUNS[0])
                for n, (t, r) in enumerate(RUNS):
                    if (t, r) == ("f0", 0):
                        pool.wait_ge(s["x_done"], before(t, r, "x_done"))
                        nc.gpsimd.memset(vals_pad, 0.0).then_inc(s["vals_zeroed"], 1)
                    if n + 1 < len(RUNS):
                        ready_next(*RUNS[n + 1])
                    if t == "f2":
                        pool.wait_ge(s["f2_e_stats"], since(t, r, "e_stats") * NT + NT)
                        root(end_mv[:], end_var[:], end_rstd[:], s["f2_e_rstd"])
                iteration_end(pool, "pool")

        @block.tensor
        def _(pe):
            mm, tr = nc.tensor.matmul, nc.tensor.transpose
            pe.wait_ge(consts_ready, N_CONSTS)
            pe.wait_ge(w_early, n_early[0])
            pe.wait_ge(setup_dve, 1)
            for c in range(4):
                m = mm(ps[:, 0, 0:D], vals[:, c, 0:P], wo_pad["a3"][:, c, :],
                       start=(c == 0), stop=(c == 3))
            m.then_inc(setup_pe, 1)
            pe.wait_ge(setup_dve, 2)

            def turn_x(t, r):
                ready, seen = before(t, r, "normed"), before(t, r, "xnT")
                if t == "a0":
                    for k in range(CT):
                        pe.wait_ge(s["normed"], ready + k + 1)
                        tr(ps[:, 7, P * k:P * k + P], nrm[:, k, :], ident[:]).then_inc(s["xT"], 1)
                    ready += CT + NT
                    pe.wait_ge(s["xnT"], seen + 1)
                for k in range(NT):
                    pe.wait_ge(s["normed"], ready + k + 1)
                    tr(ps[:, 7, P * k:P * k + P], nrm[:, CT + k, :], ident[:]).then_inc(s["xT"], 1)

            def route(t, r):
                if t[0] == "a":
                    return
                pe.wait_ge(s["xnT"], before(t, r, "xnT") + 1)
                for k in range(NT):
                    m = mm(ps[:, 7, 8 * k:8 * k + MOE[t]["routed"]], xnT[:, r, P * k:P * k + P], w_gate[t][:],
                           start=True, stop=True)
                if t == "f2":
                    for k in range(NT):
                        m = mm(ps[:, 7, S + P * k:S + P * k + P], xnT[:, r, P * k:P * k + P], w_shared2[:],
                               start=True, stop=True)
                m.then_inc(s[t + "_logits"], 1)

            def projections(t, r):
                for j, (n, lhsT, rhs) in enumerate(proj_jobs(t, r)):
                    if j >= 6:
                        k = j - 6
                        pe.wait_ge(s[t + ("_ev_act" if k % 2 else "_ev_dve")],
                                   since(t, r, "ev_act" if k % 2 else "ev_dve") + k // 2 + 1)
                    mm(ps[:, j % 6, 0:n], lhsT, rhs, start=True, stop=True).then_inc(s[t + "_proj"], 1)

            def stacked_projections(t, r):
                for g in range(4):
                    if g == 2:
                        pe.wait_ge(s["x_done"], before(t, r, "x_done"))
                    for w, rhs in ((1, ctxT[:, r, :]), (0, xnT[:, r, :])):
                        for k in range(4):
                            m = mm(stack_out(g, w == 1)[32 * k:32 * k + 32, :], wqkv[t][:, w, 32 * g:32 * g + 32], rhs,
                                   start=True, stop=True)
                        m.then_inc(s[t + "_proj"], 1)
                pe.wait_ge(s[t + "_ev_dve"], since(t, r, "ev_dve") + 2)
                for k in range(CT):
                    m = mm(ps[:, 4, P * k:P * k + P], ctxT[:, r, P * k:P * k + P], wqkv[t][:, 2, :], start=True, stop=True)
                m.then_inc(s[t + "_proj"], 1)

            def q_projection(t, r):
                if nth(t, r):
                    pe.wait_ge(s["x_done"], before(t, r, "x_done"))
                for c in range(HALF):
                    if c >= 2:
                        pe.wait_ge(s[t + ("_qm_act" if c % 2 else "_qm")], since(t, r, "qm") + 2 * (c // 2))
                    mm(ps[:, 6 + c % 2, 0:S], wq0[:, P * c:P * c + P], kvT[:, S2:KV0], start=True, stop=True) \
                        .then_inc(s[t + "_qproj"], 1)

            def attention(t, r, after):
                nk, hpc, rows = ATT[t]["nk"], ATT[t]["hpc"], ATT[t]["rows"]
                half = nk // P // 2
                if t == "a0":
                    nj = len(proj_jobs(t))
                    pe.wait_ge(s[t + "_ev_dve"], since(t, r, "ev_dve") + (nj + 1) // 2)
                    pe.wait_ge(s[t + "_ev_act"], since(t, r, "ev_act") + nj // 2)
                U = HEADS * NT

                def scores(u):
                    h, qt = unit(t, u)
                    if t == "a0":
                        pe.wait_ge(s[t + ("_qm_act" if h // 2 % 2 else "_qm")],
                                   since(t, r, "qm") + 2 * (h // 4) + h % 2 + 1)
                    else:
                        pe.wait_ge(s[t + "_ev_dve"], since(t, r, "ev_dve") + (4 if u == 1 else 2 * (h // 4) + 2))
                        pe.wait_ge(s[t + ("_qm_act" if h % 4 >= 2 else "_qm")],
                                   since(t, r, "qm") + 2 * (h // 4) + h % 2 + 1)
                    if u >= 2:
                        pe.wait_ge(s[t + "_biased"], since(t, r, "biased") + u - 1)
                    if t == "a0":
                        lhsT, kt = qm[:, h, P * qt:P * qt + P], keysT[:, h // 2, :]
                        mm(ps[:, 2 * (u % 2), 0:512], lhsT, kt[:, 0:512], start=True, stop=True)
                        m = mm(ps[:, 2 * (u % 2) + 1, 0:nk - 512], lhsT, kt[:, 512:nk], start=True, stop=True)
                    else:
                        m = mm(ps[:, 2 * (u % 2), :], qst_m[:, h, P * qt:P * qt + P], kst[:, h // 4, :],
                               start=True, stop=True)
                    m.then_inc(s[t + "_scores"], 1)

                def turn(u):
                    pe.wait_ge(s[t + "_exped"], since(t, r, "exped") + u + 1)
                    if t != "a0" and u == 0:
                        pe.wait_ge(s[t + "_ev_dve"], since(t, r, "ev_dve") + 8)
                        pe.wait_ge(s[t + "_ev_act"], since(t, r, "ev_act") + 9)
                    ago = 1 if t == "a0" else 2
                    for g in range(2):
                        if u >= ago:
                            pe.wait_ge(s[t + ("_pt_act" if g else "_pt_dve")], since(t, r, "pt_dve") + u - ago + 1)
                        for k in range(half):
                            kk = g * half + k
                            m = tr(ps[:, turned_bank(t, u, g), P * k:P * k + P], prob[:, u % 4, P * kk:P * kk + P],
                                   ident[:])
                        m.then_inc(s[t + "_turned"], 1)

                def av(g):
                    (c, qt), units = divmod(g, NT), range(hpc * g, hpc * g + hpc)
                    pe.wait_ge(s[t + "_pt_dve"], since(t, r, "pt_dve") + units[-1] + 1)
                    pe.wait_ge(s[t + "_pt_act"], since(t, r, "pt_act") + units[-1] + 1)
                    if g == 0:
                        if t == "a0":
                            pe.wait_ge(s[t + "_qm"], since(t, r, "qm") + HEADS // 2)
                            pe.wait_ge(s[t + "_qm_act"], since(t, r, "qm_act") + HEADS // 2)
                    if qt == 0 and c >= 1:
                        pe.wait_ge(s[t + "_oT"], since(t, r, "oT") + c)
                    for k in range(nk // P):
                        for j, u in enumerate(units):
                            h = hpc * c + j
                            val = vals[:, k, 64 * h:64 * h + 64] if t == "a0" else vals_pad[:, k, h, :]
                            m = mm(ps[rows * j:rows * j + rows, 6, P * qt:P * qt + P], val,
                                   probT[:, turned_at(t, u) + k, :], start=(k == 0), stop=(k == nk // P - 1))
                    m.then_inc(s[t + "_av"], 1)
                    if qt == NT - 1:
                        pe.wait_ge(s[t + "_linv"], since(t, r, "linv") + c + 1)
                        for q in range(NT):
                            m = tr(ps[:, 6, S + P * q:S + P * q + P], linv_wide[:, c % 2, q, :], ident[:])
                        m.then_inc(s[t + "_r"], 1)

                for i in range(U + 5):
                    if i < U:
                        scores(i)
                    if 3 <= i < U + 3:
                        turn(i - 3)
                    if i >= 5 and (i - 5) % hpc == hpc - 1:
                        av((i - 5) // hpc)
                    if after and i == 17:
                        turn_x(*after)
                    if after and i == 25:
                        route(*after)
                nch = HEADS // hpc
                wo = wo0 if t == "a0" else wo_pad[t]
                pe.wait_ge(s[t + "_oT"], since(t, r, "oT") + nch)
                for qt in range(NT):
                    for c in range(nch):
                        m = mm(ps[:, 6, P * qt:P * qt + P], oT[:, c, P * qt:P * qt + P], wo[:, c, :],
                               start=(c == 0), stop=(c == nch - 1))
                    m.then_inc(s[t + "_y"], 1)

            def attention2(r, after):
                t = "a2"
                pe.wait_ge(s["x_done"], before(t, r, "x_done"))
                mm(ps[:, 0, 0:S], wq2[:], ctxT[:, r, 0:S], start=True, stop=True).then_inc(s[t + "_proj"], 1)
                for k in range(NT):
                    mm(ps[:, 1, P * k:P * k + P], ctxT[:, r, P * k:P * k + P], wq2[:], start=True, stop=True) \
                        .then_inc(s[t + "_proj"], 1)
                mm(ps[:, 6, 0:S], wq2[:], xnT[:, r, :], start=True, stop=True).then_inc(s[t + "_qproj"], 1)
                turn_x(*after)
                pe.wait_ge(s[t + "_qm"], since(t, r, "qm") + 1)
                pe.wait_ge(s[t + "_ev_dve"], since(t, r, "ev_dve") + 1)
                pe.wait_ge(s[t + "_ev_act"], since(t, r, "ev_act") + 1)
                for qt in range(NT):
                    mm(ps[:, 2 + qt, 0:S], qm[:, 0, P * qt:P * qt + P], keysT[:, 0, 0:S], start=True, stop=True) \
                        .then_inc(s[t + "_scores"], 1)
                for qt in range(NT):
                    pe.wait_ge(s[t + "_exped"], since(t, r, "exped") + qt + 1)
                    for k in range(qt + 1):
                        m = tr(ps[:, 4 + qt, P * k:P * k + P], prob[:, qt, P * k:P * k + P], ident[:])
                    m.then_inc(s[t + "_turned"], 1)
                route(*after)
                for qt in range(NT):
                    pe.wait_ge(s[t + "_pt_dve"], since(t, r, "pt_dve") + qt + 1)
                    for k in range(qt + 1):
                        m = mm(ps[:, 6, P * qt:P * qt + P], probT[:, NT * qt + k, :], vals[:, 2, P * k:P * k + P],
                               start=(k == 0), stop=(k == qt))
                    m.then_inc(s[t + "_y"], 1)

            def mixture(t, r, after):
                cfg = MOE[t]
                ne, nch = cfg["routed"] + cfg["shared"], cfg["chunks"]
                if t == "f2":
                    pe.wait_ge(s["big2_loaded"], N_BIG)
                if t == "f3":
                    pe.wait_ge(s["big3_loaded"], N_BIG)
                groups = expert_groups(t)
                units = [(g, c) for g in range(len(groups)) for c in range(nch)]

                def up(u):
                    g, c = units[u]
                    if u >= 4:
                        pe.wait_ge(s[t + ("_h" if t == "f0" else "_act")], since(t, r, "up") + u - 3)
                    e = groups[g][0]
                    if t == "f0":
                        for j in range(2):
                            m = mm(ps[:, u % 4, S * j:S * j + S], w_up[t][:, e, j, P * c:P * c + P], xnT[:, r, :],
                                   start=True, stop=True)
                    elif t == "f1":
                        m = mm(ps[:, u % 4, 0:S], w_up[t][:, e:e + 2, :].rearrange("p a b -> p (a b)"), xnT[:, r, :],
                               start=True, stop=True)
                    else:
                        m = mm(ps[:, u % 4, 0:S], w_up[t][:, e, P * c:P * c + P], xnT[:, r, :], start=True, stop=True)
                    m.then_inc(s[t + "_up"], 1)

                def down(g):
                    pe.wait_ge(s[t + ("_h" if t == "f0" else "_act")], since(t, r, "up") + nch * (g + 1))
                    for i, e in enumerate(groups[g]):
                        n = first_of(groups, g) + i
                        if n >= 2:
                            pe.wait_ge(s[t + "_y_used"], since(t, r, "y_used") + NT * (n - 1))
                        elif r == 1 and t == "f0":
                            pe.wait_ge(s["x_done"], before(t, r, "x_done"))
                        elif r == 1:
                            pe.wait_ge(s[t + "_y_used"], NT * (ne - (ne - 1 - n) % 2))
                        for k in range(NT):
                            for c in range(nch):
                                u = g * nch + c
                                w = w_dn[t][:, e, :] if t == "f1" else w_dn[t][:, e, c, :]
                                m = mm(ps[:, 4 + n % 2, P * k:P * k + P], hT[:, u % 8 // 2, u % 2, P * k:P * k + P], w,
                                       start=(c == 0), stop=(c == nch - 1))
                        m.then_inc(s[t + "_down"], 1)

                def biases():
                    pe.wait_ge(s["x_done"], before(t, r, "x_done"))
                    pe.wait_ge(s[t + "_comb"], since(t, r, "comb") + 1)
                    for k in range(NT):
                        m = tr(ps[0:ne, 6, P * k:P * k + P], comb[:, r, k, 0:ne], ident[:])
                    m.then_inc(s[t + "_combT"], 1)
                    pe.wait_ge(s[t + "_combT_sb"], since(t, r, "combT_sb") + 1)
                    for k in range(NT):
                        m = mm(ps[:, 6, P * k:P * k + P], combT[0:ne, P * k:P * k + P], b_dn[t][:], start=True, stop=True)
                    m.then_inc(s[t + "_b2"], 1)

                for u in range(nch):
                    up(u)
                for g in range(len(groups)):
                    for u in range(nch * (g + 1), min(nch * (g + 2), len(units))):
                        up(u)
                    down(g)
                    if g == 1 and t != "f0":
                        biases()
                    if after and g == 2:
                        turn_x(*after)
                    if after and g == 3:
                        route(*after)

            with pe.Fori(0, B // 2):
                turn_x(*RUNS[0])
                for n, (t, r) in enumerate(RUNS):
                    after = RUNS[n + 1] if n + 1 < len(RUNS) else None
                    if n and RUNS[n - 1][0][0] == "f" and t[0] == "a":
                        pe.wait_ge(s["x_done"], before(t, r, "x_done"))
                    if t == "f0":
                        pe.wait_ge(s["big0_loaded"], N_BIG0)
                        pe.wait_ge(w_rest, n_rest[0])
                    if t[0] == "f":
                        mixture(t, r, after)
                        continue
                    pe.wait_ge(s["xnT"], before(t, r, "xnT") + (2 if t == "a0" else 1))
                    if t == "a2":
                        attention2(r, after)
                        continue
                    if t == "a0":
                        projections(t, r)
                        q_projection(t, r)
                    else:
                        stacked_projections(t, r)
                    attention(t, r, after)
                iteration_end(pe, "pe")

        @block.scalar
        def _(act):
            f = nc.scalar.activation

            def attention(t, r, after):
                nk, hpc = ATT[t]["nk"], ATT[t]["hpc"]
                half = nk // P // 2
                U = HEADS * NT

                def exps(u):
                    act.wait_ge(s[t + "_biased"], since(t, r, "biased") + u + 1)
                    p = prob[:, u % 4, 0:nk]
                    h, qt = unit(t, u)
                    f(p, p, ACT.Exp, bias=negmax[:, u:u + 1], scale=-1.0, accum_out=lsum[:, h, qt:qt + 1]) \
                        .then_inc(s[t + "_exped"], 1)

                def copy_turned(u):
                    at = turned_at(t, u)
                    act.wait_ge(s[t + "_turned"], since(t, r, "turned") + 2 * u + 2)
                    if contracted(t, u):
                        act.wait_ge(s[t + "_av"], since(t, r, "av") + contracted(t, u))
                    nc.scalar.copy(probT[:, at + half:at + 2 * half, :],
                                   ps[:, turned_bank(t, u, 1), 0:half * P].rearrange("p (k q) -> p k q", q=P)) \
                        .then_inc(s[t + "_pt_act"], 1)

                def copy_out(c):
                    act.wait_ge(s[t + "_r"], since(t, r, "r") + c + 1)
                    if c >= 2:
                        act.wait_ge(s[t + "_oT"], since(t, r, "oT") + c - 1)
                    nc.scalar.copy(o_raw[:, c % 2, :], ps[:, 6, 0:S]).then_inc(s[t + "_o_raw"], 1)

                for i in range(U + 7):
                    if t != "a0" and i % 8 in (1, 3) and i < 24:
                        stacked_queries(t, r, 4 * (i // 8 + 1) + 2 + i % 8 // 2)
                    if i >= 6 and (i - 6) % (NT * hpc) == NT * hpc - 1 and (i - 6) // (NT * hpc) < HEADS // hpc:
                        copy_out((i - 6) // (NT * hpc))
                    if 3 <= i < U + 3:
                        copy_turned(i - 3)
                    if i < U:
                        exps(i)
                    if after and i == 18:
                        ready_tokens(*after)
                    if after and i == 27:
                        ready_router(*after)

            def stacked(t, g, keys):
                j = 1 if keys else 0
                dst, src = (kst if keys else qst)[:, g, :], stack_out(g, keys)
                if t == "a3":
                    ins = f(dst, src, ACT.Identity, bias=bqk3_split[:, j, g:g + 1], scale=split[:, j:j + 1])
                else:
                    ins = f(dst, src, ACT.Copy, scale=split[:, j:j + 1])
                ins.then_inc(s[t + "_ev_act"], 1)

            def stacked_queries(t, r, h):
                act.wait_ge(s[t + "_ev_dve"], since(t, r, "ev_dve") + 2 * (h // 4) + 2)
                f(qst_m[:, h, :], qst[:, h // 4, :], ACT.Copy, scale=lane8[:, h % 4:h % 4 + 1]) \
                    .then_inc(s[t + "_qm_act"], 1)

            def ready_tokens(t, r):
                n = before(t, r, "xT")
                if t == "a0":
                    act.wait_ge(w_early, n_early[0])
                    act.wait_ge(s["xT"], n + CT + NT)
                    if r == 1:
                        act.wait_ge(s["a0_qproj"], HALF)
                    f(kvT[:, S2:KV0], ps[:, 7, 0:S], ACT.Identity, bias=gb0[:, 3:4], scale=gb0[:, 2:3]) \
                        .then_inc(s["xnT"], 1)
                    return
                act.wait_ge(s["xT"], n + NT)
                nc.scalar.copy(xnT[:, r, :], ps[:, 7, 0:S]).then_inc(s["xnT"], 1)

            def ready_router(t, r):
                if t == "f0":
                    act.wait_ge(s[t + "_logit"], since(t, r, "logit") + 1)
                    f(rt[1][:], logit[:], ACT.Exp, scale=-1.0).then_inc(s[t + "_r_act"], 1)
                elif t == "f1":
                    act.wait_ge(s[t + "_logit"], since(t, r, "logit") + 1)
                    f(rt[1][:], logit[:], ACT.Abs).then_inc(s[t + "_r_act"], 1)
                    act.wait_ge(s[t + "_r_act"], since(t, r, "r_act") + 1)
                    f(rt[1][:], rt[1][:], ACT.Exp, scale=-1.0).then_inc(s[t + "_r_act"], 1)
                    act.wait_ge(s[t + "_r_act"], since(t, r, "r_act") + 2)
                    f(rt[1][:], rt[1][:], ACT.Ln, bias=1.0).then_inc(s[t + "_r_act"], 1)
                elif t[0] == "f":
                    act.wait_ge(s[t + "_r_mid"], since(t, r, "r_mid") + 1)
                    f(rt[3][:], rt[1][:], ACT.Exp).then_inc(s[t + "_r_act"], 1)
                if t == "f2":
                    act.wait_ge(s["f2_sh"], since("f2", r, "sh") + 1)
                    f(gl[:, r], gl[:, r], ACT.Gelu).then_inc(s["f2_gl"], 1)

            def mixture(t, r, after):
                groups, nch = expert_groups(t), MOE[t]["chunks"]
                for u in range(len(groups) * nch):
                    if after and u == 3 * nch:
                        ready_tokens(*after)
                    if after and u == (5 * nch if t == "f0" else 4 * nch + nch // 2):
                        ready_router(*after)
                    e, c = groups[u // nch][0], u % nch
                    act.wait_ge(s[t + "_up"], since(t, r, "up") + u + 1)
                    h = hT[:, u % 8 // 2, u % 2, :]
                    if t == "f0":
                        if u >= 4:
                            act.wait_ge(s[t + "_h"], since(t, r, "h") + u - 3)
                        f(act_tmp[:, u % 4, :], ps[:, u % 4, 0:S], ACT.Silu).then_inc(s[t + "_act"], 1)
                        continue
                    if u >= 8:
                        act.wait_ge(s[t + "_down"], since(t, r, "down") + down_before(t, u))
                    col = e // 2 if t == "f1" else e * nch + c
                    f(h, ps[:, u % 4, 0:S], {"f1": ACT.Silu, "f2": ACT.Gelu, "f3": ACT.Relu}[t],
                      bias=b_up[t][:, col:col + 1]).then_inc(s[t + "_act"], 1)

            with act.Fori(0, B // 2):
                ready_tokens(*RUNS[0])
                for n, (t, r) in enumerate(RUNS):
                    after = RUNS[n + 1] if n + 1 < len(RUNS) else None
                    if t[0] == "f":
                        mixture(t, r, after)
                        continue
                    if t == "a2":
                        act.wait_ge(s[t + "_proj"], since(t, r, "proj") + 1 + NT)
                        nc.scalar.copy(vals[:, 2, 0:S], ps[:, 1, 0:S]).then_inc(s[t + "_ev_act"], 1)
                    elif t == "a0":
                        nj = len(proj_jobs(t))
                        for j in range(1, nj, 2):
                            act.wait_ge(s[t + "_proj"], since(t, r, "proj") + j + 1)
                            dst, src = proj_out(t, j)
                            nc.scalar.copy(dst, src).then_inc(s[t + "_ev_act"], 1)
                    if t == "a0":
                        for c in range(1, HALF, 2):
                            act.wait_ge(s[t + "_qproj"], since(t, r, "qproj") + c + 1)
                            for j in range(2):
                                f(qm[:, 2 * c + j, :], ps[:, 7, 0:S], ACT.Copy, scale=rowmask[:, j:j + 1]) \
                                    .then_inc(s[t + "_qm_act"], 1)
                        attention(t, r, after)
                    elif t == "a2":
                        for qt in range(NT):
                            act.wait_ge(s[t + "_biased"], since(t, r, "biased") + qt + 1)
                            p = prob[:, qt, 0:S]
                            f(p, p, ACT.Exp, bias=negmax[:, qt:qt + 1], scale=-1.0, accum_out=lsum[:, 0, qt:qt + 1]) \
                                .then_inc(s[t + "_exped"], 1)
                            if qt == 0:
                                ready_tokens(*after)
                        ready_router(*after)
                    else:
                        for j in range(8):
                            act.wait_ge(s[t + "_proj"], since(t, r, "proj") + j + 1)
                            stacked(t, j // 2, j % 2 == 0)
                        for h in (2, 3):
                            stacked_queries(t, r, h)
                        if t == "a1":
                            act.wait_ge(s["vals_zeroed"], 1)
                        act.wait_ge(s[t + "_proj"], since(t, r, "proj") + 9)
                        nc.scalar.copy(vals_pad[:, :, :, 0:8], ps[:, 4, :].rearrange("p (k h i) -> p k h i", k=CT, i=8)) \
                            .then_inc(s[t + "_ev_act"], 1)
                        attention(t, r, after)
                iteration_end(act, "act")

        @block.vector
        def _(dve):
            v = nc.vector
            dve.wait_ge(consts_ready, N_CONSTS)
            dve.wait_ge(w_early, n_early[0])
            v.tensor_scalar(bias1[:], mask1_u8[:], -1.0, FAR, ALU.add, ALU.mult)
            v.tensor_copy(vals[:, 0:4, 0:P], bv_pad[:].rearrange("p (c o) -> p c o", o=1).broadcast_to([P, 4, P])) \
                .then_inc(setup_dve, 1)
            dve.wait_ge(setup_pe, 1)
            v.tensor_tensor(bo["a3"][:], bo["a3"][:], ps[:, 0, 0:D], ALU.add).then_inc(setup_dve, 1)
            v.tensor_reduce(lane8[:], rowmask[:, 2:2 + HEADS].rearrange("p (q j) -> p j q", j=4), AX_X, ALU.add)
            v.tensor_scalar(split[:, 0:1], rowmask[:, 1:2], -1.0, None, ALU.mult)
            v.tensor_reduce(split[:, 1:2], rowmask[:, 2:2 + HEADS].rearrange("p (a b j) -> p b a j", a=2, b=2)[:, 1],
                            AX_XY, ALU.add, negate=True).then_inc(setup_dve, 1)
            dve.wait_ge(setup_dve, 3)
            for j in range(2):
                ins = v.tensor_scalar(bqk3_split[:, j, :], bqk3[:, j, :], split[:, j:j + 1], None, ALU.mult)
            ins.then_inc(setup_dve, 1)
            dve.wait_ge(setup_dve, 4)

            step = [0]

            def link(ins):
                step[0] += 1
                ins.then_inc(s["dve_step"], 1)
                dve.wait_ge(s["dve_step"], step[0])

            def spread(src, lo, hi):
                for k in range(lo, hi):
                    ins = v.bn_stats(stats[:, k, :], src[:, k, :])
                link(ins)
                for k in range(lo, hi):
                    v.bn_aggr(mv[:, k, :], stats[:, k, :]).then_inc(s["stats"], 1)

            def normed(src, lo, hi, n_rstd):
                dve.wait_ge(s["rstd"], n_rstd)
                for k in range(lo, hi):
                    v.tensor_scalar(nrm[:, k, :], src[:, k, :], mv[:, k, 0:1], rstd[:, k:k + 1], ALU.subtract, ALU.mult) \
                        .then_inc(s["normed"], 1)

            def ready_spread(t, r):
                if nth(t, r) >= 2:
                    dve.wait_ge(s["x_done"], NT * (nth(t, r) - 1))
                dve.wait_ge(s["xT"], before(t, r, "xT"))
                if t == "a0":
                    spread(tok[:, r], 0, CT + NT)
                else:
                    spread(tok[:, r], CT, CT + NT)

            def ready_normed(t, r):
                n, m = before(t, r, "rstd"), before(t, r, "normed")
                if t != "a0":
                    normed(tok[:, r], CT, CT + NT, n + 1)
                    return
                normed(tok[:, r], 0, CT + NT, n + 1)
                dve.wait_ge(s["normed"], m + CT + NT)
                spread(nrm, CT, CT + NT)
                normed(nrm, CT, CT + NT, n + 2)

            def ready_context(t, r):
                if t != "a0":
                    return
                dve.wait_ge(s["xT"], before(t, r, "xT") + CT)
                if r == 1:
                    dve.wait_ge(s["a0_qproj"], HALF)
                v.tensor_scalar(kvT[:, 0:S2], ps[:, 7, 0:S2], gb0[:, 0:1], gb0[:, 1:2], ALU.mult, ALU.add) \
                    .then_inc(s["xnT"], 1)

            def attention(t, r, after):
                nk, hpc, rows, scale = (ATT[t][x] for x in ("nk", "hpc", "rows", "scale"))
                half = nk // P // 2
                U = HEADS * NT

                def add_bias(u):
                    dve.wait_ge(s[t + "_scores"], since(t, r, "scores") + u + 1)
                    if u >= 4:
                        dve.wait_ge(s[t + "_turned"], since(t, r, "turned") + 2 * (u - 3))
                    b = 2 * (u % 2)
                    sc = ps[:, b:b + 2, :].rearrange("p b n -> p (b n)")[:, 0:nk]
                    bias = {"a0": bias0[:], "a1": bias1[:, unit(t, u)[1], :], "a3": bias3[:]}[t]
                    v.tensor_tensor_reduce(out=prob[:, u % 4, 0:nk], in0=sc, in1=bias, scale=-scale, scalar=NEVER,
                                           op0=ALU.add, op1=ALU.min, accum_out=negmax[:, u:u + 1]) \
                        .then_inc(s[t + "_biased"], 1)

                def copy_turned(u):
                    at = turned_at(t, u)
                    dve.wait_ge(s[t + "_turned"], since(t, r, "turned") + 2 * u + 1)
                    if contracted(t, u):
                        dve.wait_ge(s[t + "_av"], since(t, r, "av") + contracted(t, u))
                    v.tensor_copy(probT[:, at:at + half, :],
                                  ps[:, turned_bank(t, u, 0), 0:half * P].rearrange("p (k q) -> p k q", q=P)) \
                        .then_inc(s[t + "_pt_dve"], 1)

                def inverse(c):
                    dve.wait_ge(s[t + "_exped"], since(t, r, "exped") + NT * hpc * (c + 1))
                    hs = slice(hpc * c, hpc * c + hpc)
                    link(v.reciprocal(linv[:, hs, :], lsum[:, hs, :]))
                    if c >= 2:
                        dve.wait_ge(s[t + "_r"], since(t, r, "r") + c - 1)
                    for qt in range(NT):
                        ins = v.tensor_copy(linv_wide[:, c % 2, qt, :].rearrange("p (h r) -> p h r", h=hpc),
                                            linv[:, hs, qt:qt + 1].broadcast_to([P, hpc, rows]))
                    ins.then_inc(s[t + "_linv"], 1)

                def scale_out(c):
                    dve.wait_ge(s[t + "_r"], since(t, r, "r") + c + 1)
                    dve.wait_ge(s[t + "_o_raw"], since(t, r, "o_raw") + c + 1)
                    v.tensor_tensor(oT[:, c, :], o_raw[:, c % 2, :], ps[:, 6, S:2 * S], ALU.mult).then_inc(s[t + "_oT"], 1)

                w = NT * hpc
                for i in range(U + 8):
                    if i >= 4 and (i - 4) % w == w - 1 and (i - 4) // w < HEADS // hpc:
                        inverse((i - 4) // w)
                    if i >= 7 and (i - 7) % w == w - 1 and (i - 7) // w < HEADS // hpc:
                        scale_out((i - 7) // w)
                    if i < U:
                        add_bias(i)
                    if t != "a0" and i % 8 in (1, 3) and i < 24:
                        stacked_queries(t, r, 4 * (i // 8 + 1) + i % 8 // 2)
                    if after and i == 8:
                        ready_spread(*after)
                    if after and i == 11:
                        ready_normed(*after)
                    if after and i == 17:
                        ready_context(*after)
                    if after and i == 26:
                        ready_logits(*after)
                    if after and i == 30:
                        ready_weights(*after)
                    if 3 <= i < U + 3:
                        copy_turned(i - 3)
                if t != "a0":
                    for k in range(NT):
                        link(v.tensor_tensor(X[:, r, k, :], X[:, r, k, :], bo[t][:], ALU.add))
                dve.wait_ge(s[t + "_y"], since(t, r, "y") + NT)
                for k in range(NT):
                    v.tensor_tensor(X[:, r, k, :], X[:, r, k, :], ps[:, 6, P * k:P * k + P], ALU.add) \
                        .then_inc(s["x_done"], 1)

            def stacked(t, r, g, keys):
                j = 1 if keys else 0
                dst, src = (kst if keys else qst)[:, g, :], stack_out(g, keys)
                dve.wait_ge(s[t + "_ev_act"], since(t, r, "ev_act") + 2 * g + 2 - j)
                if t == "a3":
                    ins = v.scalar_tensor_tensor(out=dst, in0=src, scalar=bqk3[:, j, g:g + 1], in1=dst, op0=ALU.add,
                                                 op1=ALU.add)
                else:
                    ins = v.tensor_tensor(dst, src, dst, ALU.add)
                ins.then_inc(s[t + "_ev_dve"], 1)

            def stacked_queries(t, r, h):
                dve.wait_ge(s[t + "_ev_dve"], since(t, r, "ev_dve") + 2 * (h // 4) + 2)
                v.tensor_scalar(qst_m[:, h, :], qst[:, h // 4, :], lane8[:, h % 4:h % 4 + 1], None, ALU.mult) \
                    .then_inc(s[t + "_qm"], 1)

            def attention2(r, after):
                t = "a2"
                ready_spread(*after)
                dve.wait_ge(s[t + "_proj"], since(t, r, "proj") + 1)
                v.tensor_copy(keysT[:, 0, 0:S], ps[:, 0, 0:S]).then_inc(s[t + "_ev_dve"], 1)
                dve.wait_ge(s[t + "_qproj"], since(t, r, "qproj") + 1)
                v.tensor_copy(qm[:, 0, :], ps[:, 6, 0:S]).then_inc(s[t + "_qm"], 1)
                ready_normed(*after)
                for qt in range(NT):
                    dve.wait_ge(s[t + "_scores"], since(t, r, "scores") + qt + 1)
                    v.tensor_tensor_reduce(out=prob[:, qt, 0:S], in0=ps[:, 2 + qt, 0:S], in1=bias2[:, qt, :],
                                           scale=-float(D ** -0.5), scalar=NEVER, op0=ALU.add, op1=ALU.min,
                                           accum_out=negmax[:, qt:qt + 1]).then_inc(s[t + "_biased"], 1)
                for qt in range(NT):
                    dve.wait_ge(s[t + "_turned"], since(t, r, "turned") + qt + 1)
                    n = P * (qt + 1)
                    v.tensor_copy(probT[:, NT * qt:NT * qt + qt + 1, :], ps[:, 4 + qt, 0:n].rearrange("p (k q) -> p k q", q=P)) \
                        .then_inc(s[t + "_pt_dve"], 1)
                ready_logits(*after)
                dve.wait_ge(s[t + "_exped"], since(t, r, "exped") + NT)
                link(v.reciprocal(linv[:, 0, :], lsum[:, 0, :]))
                for qt in range(NT):
                    dve.wait_ge(s[t + "_y"], since(t, r, "y") + NT)
                    v.scalar_tensor_tensor(out=X[:, r, qt, :], in0=ps[:, 6, P * qt:P * qt + P], scalar=linv[:, 0, qt:qt + 1],
                                           in1=X[:, r, qt, :], op0=ALU.mult, op1=ALU.add).then_inc(s["x_done"], 1)
                ready_weights(*after)

            def ready_logits(t, r):
                if t[0] == "a":
                    return
                E = MOE[t]["routed"]
                if E < 8:
                    link(v.memset(logit[:], -1e38))
                fixed = 1.0 / 3.0 if t == "f0" else MOE[t]["fixed"]
                v.memset(comb[:, r], fixed)
                dve.wait_ge(s[t + "_logits"], since(t, r, "logits") + 1)
                lg = ps[:, 7, 0:8 * NT].rearrange("p (k e) -> p k e", e=8)[:, :, 0:E]
                if t in b_gate:
                    for k in range(NT):
                        ins = v.tensor_tensor(logit[:, k, 0:E], b_gate[t][:], lg[:, k, :], ALU.add)
                else:
                    ins = v.tensor_copy(logit[:, :, 0:E], lg)
                ins.then_inc(s[t + "_logit"], 1)
                if t == "f2":
                    for k in range(NT):
                        ins = v.tensor_tensor(gl[:, r, k, :], sb2[:, 0, :], ps[:, 7, S + P * k:S + P * k + P], ALU.add)
                    ins.then_inc(s["f2_sh"], 1)
                dve.wait_ge(s[t + "_logit"], since(t, r, "logit") + 1)
                for k in range(NT):
                    ins = v.max(top8[:, k, :], logit[:, k, :])
                link(ins)
                if t in ("f2", "f3"):
                    for k in range(NT):
                        ins = v.tensor_scalar(rt[1][:, k, :], logit[:, k, :], top8[:, k, 0:1], None, ALU.subtract)
                    ins.then_inc(s[t + "_r_mid"], 1)
                link(v.memset(top8[:, :, 2:8], NEVER))
                for k in range(NT):
                    ins = v.match_replace(cut[:, k, :], top8[:, k, :], logit[:, k, :], -NEVER)
                link(ins)
                link(v.tensor_tensor(rt[0][:], cut[:], logit[:], ALU.not_equal))

            def ready_weights(t, r):
                if t[0] == "a":
                    return
                E = MOE[t]["routed"]
                if t == "f0":
                    dve.wait_ge(s[t + "_r_act"], since(t, r, "r_act") + 1)
                    link(v.tensor_scalar(rt[2][:], rt[1][:], 1.0, None, ALU.add))
                    link(v.reciprocal(rt[3][:], rt[2][:]))
                elif t == "f1":
                    dve.wait_ge(s[t + "_r_act"], since(t, r, "r_act") + 3)
                    v.scalar_tensor_tensor(out=rt[2][:], in0=logit[:], scalar=0.0, in1=rt[1][:], op0=ALU.max,
                                           op1=ALU.add).then_inc(s[t + "_r_mid"], 1)
                    dve.wait_ge(s["f1_r_pool"], since("f1", r, "r_pool") + 1)
                else:
                    dve.wait_ge(s[t + "_r_act"], since(t, r, "r_act") + 1)
                if t == "f1":
                    v.tensor_tensor(comb[:, r, :, 0:E], rt[3][:, :, 0:E], rt[0][:, :, 0:E], ALU.mult).then_inc(s[t + "_comb"], 1)
                else:
                    link(v.tensor_tensor(rt[4][:], rt[3][:], rt[0][:], ALU.mult))
                    link(v.tensor_reduce(rsum[:], (rt[3] if t == "f3" else rt[4])[:], AX_X, ALU.add))
                    link(v.reciprocal(rinv[:], rsum[:]))
                    for k in range(NT):
                        ins = v.tensor_scalar(comb[:, r, k, 0:E], rt[4][:, k, 0:E], rinv[:, k:k + 1],
                                              1.0 / 3.0 if t == "f0" else 1.0, ALU.mult, ALU.mult)
                    ins.then_inc(s[t + "_comb"], 1)
                dve.wait_ge(s[t + "_comb"], since(t, r, "comb") + 1)

            def mixture(t, r, after):
                groups, nch = expert_groups(t), MOE[t]["chunks"]
                ne = first_of(groups, len(groups))
                total = acc if t == "f2" else X[:, r]
                if t == "f2":
                    dve.wait_ge(s["f2_gl"], since("f2", r, "gl") + 1)
                    link(v.tensor_scalar(acc, gl[:, r], 0.5, None, ALU.mult))

                def hidden(u):
                    dve.wait_ge(s[t + "_act"], since(t, r, "act") + u + 1)
                    if u >= 8:
                        dve.wait_ge(s[t + "_down"], since(t, r, "down") + down_before(t, u))
                    v.tensor_tensor(hT[:, u % 8 // 2, u % 2, :], act_tmp[:, u % 4, :], ps[:, u % 4, S:2 * S], ALU.mult) \
                        .then_inc(s[t + "_h"], 1)

                def add_expert(n, e):
                    dve.wait_ge(s[t + "_down"], since(t, r, "down") + n + 1)
                    for k in range(NT):
                        if n >= 1:
                            dve.wait_ge(s[t + "_y_used"], since(t, r, "y_used") + NT * (n - 1) + k + 1)
                        last = t == "f0" and n == ne - 1
                        v.scalar_tensor_tensor(out=total[:, k, :], in0=ps[:, 4 + n % 2, P * k:P * k + P],
                                               scalar=comb[:, r, k, e:e + 1], in1=total[:, k, :], op0=ALU.mult,
                                               op1=ALU.add).then_inc(s["x_done" if last else t + "_y_used"], 1)

                def turned_weights():
                    dve.wait_ge(s[t + "_combT"], since(t, r, "combT") + 1)
                    v.tensor_copy(combT[0:ne, :], ps[0:ne, 6, 0:S]).then_inc(s[t + "_combT_sb"], 1)

                if t == "f0":
                    for u in range(nch):
                        hidden(u)
                for g in range(len(groups)):
                    if t == "f0":
                        for u in range(nch * (g + 1), min(nch * (g + 2), nch * len(groups))):
                            hidden(u)
                    for i, e in enumerate(groups[g]):
                        add_expert(first_of(groups, g) + i, e)
                    if g == 0 and after:
                        ready_spread(*after)
                    if g == 1 and after:
                        ready_normed(*after)
                    if g == 1 and t != "f0":
                        turned_weights()
                    if g == 3 and after:
                        ready_logits(*after)
                    if g == 4 and after:
                        ready_weights(*after)
                if t == "f0":
                    return
                dve.wait_ge(s[t + "_b2"], since(t, r, "b2") + 1)
                dve.wait_ge(s[t + "_y_used"], since(t, r, "y_used") + NT * ne)
                for k in range(NT):
                    ins = v.tensor_tensor(total[:, k, :], total[:, k, :], ps[:, 6, P * k:P * k + P], ALU.add)
                    if t == "f2":
                        link(ins)
                    else:
                        ins.then_inc(s["x_done"], 1)
                if t == "f2":
                    for k in range(NT):
                        ins = v.bn_stats(end_stats[:, k, :], acc[:, k, :])
                    link(ins)
                    for k in range(NT):
                        v.bn_aggr(end_mv[:, k, :], end_stats[:, k, :]).then_inc(s["f2_e_stats"], 1)
                    dve.wait_ge(s["f2_e_rstd"], since("f2", r, "e_rstd") + 1)
                    for k in range(NT):
                        ins = v.tensor_scalar(acc[:, k, :], acc[:, k, :], end_mv[:, k, 0:1], end_rstd[:, k:k + 1],
                                              ALU.subtract, ALU.mult)
                    for j, op in ((1, ALU.mult), (2, ALU.add)):
                        link(ins)
                        for k in range(NT):
                            ins = v.tensor_tensor(acc[:, k, :], acc[:, k, :], sb2[:, j, :], op)
                    link(ins)
                    for k in range(NT):
                        v.tensor_tensor(X[:, r, k, :], X[:, r, k, :], acc[:, k, :], ALU.add).then_inc(s["x_done"], 1)

            with dve.Fori(0, B // 2):
                step[0] = 0
                dve.wait_ge(s["loaded"], N_LOAD)
                ready_spread(*RUNS[0])
                ready_normed(*RUNS[0])
                ready_context(*RUNS[0])
                for n, (t, r) in enumerate(RUNS):
                    after = RUNS[n + 1] if n + 1 < len(RUNS) else None
                    dve.wait_ge(s["x_done"], before(t, r, "x_done"))
                    if t == "f0":
                        dve.wait_ge(w_rest, n_rest[0])
                    if t[0] == "f":
                        mixture(t, r, after)
                        continue
                    if t == "a2":
                        attention2(r, after)
                        continue
                    if t != "a1":
                        v.tensor_scalar(bias0[:, 0:S2], mask_u8[:, r, 0 if t == "a0" else 1, :], -1.0, FAR, ALU.add, ALU.mult)
                    for j in range(0, len(proj_jobs(t)), 2):
                        dve.wait_ge(s[t + "_proj"], since(t, r, "proj") + j + 1)
                        dst, src = proj_out(t, j)
                        v.tensor_copy(dst, src).then_inc(s[t + "_ev_dve"], 1)
                    if t == "a0":
                        for c in range(0, HALF, 2):
                            dve.wait_ge(s[t + "_qproj"], since(t, r, "qproj") + c + 1)
                            for j in range(2):
                                v.tensor_scalar(qm[:, 2 * c + j, :], ps[:, 6, 0:S], rowmask[:, j:j + 1], None, ALU.mult) \
                                    .then_inc(s[t + "_qm"], 1)
                    else:
                        for g in range(4):
                            stacked(t, r, g, True)
                            stacked(t, r, g, False)
                            if g == 0:
                                stacked_queries(t, r, 0)
                                stacked_queries(t, r, 1)
                    attention(t, r, after)
                iteration_end(dve, "dve")


def kernel(**inputs):
    import numpy as _np
    import concourse.bacc as _bacc
    from concourse import mybir as _mybir
    from concourse.bass_utils import run_bass_kernel_spmd as _run

    given = {k: _np.asarray(v) for k, v in inputs.items()}
    given["mask0"] = given.pop("mask_BxS2_bk0")
    given["mask3"] = given.pop("mask_BxS2_bf1")
    m = given.pop("mask_1x1xSxS2_bk0")
    given["mask1"] = m.reshape(m.shape[2:])
    given["ctxT"] = given["ctx_1024"].transpose(0, 2, 1)
    for name in ("L1_xattn_Wq", "L1_xattn_Wk", "L1_xattn_Wv", "L1_xattn_Wo", "L1_ffn_routing_W", "L2_xattn_Wq",
                 "L3_xattn_Wq", "L3_xattn_Wk", "L3_xattn_Wv", "L3_xattn_Wo"):
        given[name + "T"] = given.pop(name).T
    for name in ("L1_ffn_rb1", "L2_ffn_b1", "L3_ffn_sb1", "L3_ffn_rb1"):
        given[name + "c"] = given.pop(name).reshape(-1, P).T

    nc = _bacc.Bacc("TRN2", target_bir_lowering=False, num_devices=1)
    arrays, aps = {}, {}
    for name, x in given.items():
        x = _np.ascontiguousarray(x)
        arrays[f"in_{name}_dram"] = x
        aps[name] = nc.dram_tensor(f"in_{name}_dram", x.shape, _mybir.dt.from_np(x.dtype), kind="ExternalInput").ap()
    shape = given["x"].shape
    out = nc.dram_tensor("out_0_dram", shape, _mybir.dt.float32, kind="ExternalOutput").ap()
    build(nc, aps, out)
    r = _run(nc, [arrays], core_ids=[0])
    return r.results[0]["out_0_dram"]
```

```python
import math
from contextlib import ExitStack

import concourse.bass as bass
from concourse import mybir

ALU = mybir.AluOpType
ACT = mybir.ActivationFunctionType
F32 = mybir.dt.float32
F32R = mybir.dt.float32r
U8 = mybir.dt.uint8
AX_X = mybir.AxisListType.X
AX_XY = mybir.AxisListType.XY

P = 128
D = 128
EPS = 1e-5
FAR = 1e30
NEVER = 3.0e38
HEADS = 16
MOE = {
    "f0": dict(routed=8, shared=1, fixed=1.0, chunks=2),
    "f1": dict(routed=8, shared=1, fixed=1.0, chunks=1),
    "f2": dict(routed=8, shared=0, fixed=0.0, chunks=4),
    "f3": dict(routed=4, shared=2, fixed=0.5, chunks=4),
}
PHASES = ["a0", "f0", "a1", "f1", "a2", "f2", "a3", "f3"]
RUNS = [(t, r) for t in PHASES for r in range(2)]


def build(nc, a, out):
    B, S, _ = a["x"].shape
    S2 = a["ctx_1024"].shape[1]
    NT, CT = S // P, S2 // P
    KV0 = S2 + S
    HALF = HEADS // 2
    ATT = {
        "a0": dict(nk=KV0, hpc=2, rows=64, scale=1.0 / 8.0),
        "a1": dict(nk=S2, hpc=4, rows=32, scale=float(8 ** -0.5)),
        "a3": dict(nk=S2, hpc=4, rows=32, scale=float(8 ** -0.5)),
    }

    with ExitStack() as ctx:
        def sb(name, shape, dt=F32):
            return ctx.enter_context(nc.sbuf_tensor(name, shape, dt))

        wq0 = sb("wq0", [P, 1024])
        wkv0 = sb("wkv0", [P, 2048])
        wo0 = sb("wo0", [P, HALF, D])
        wqkv = {t: sb("wqkv_" + t, [P, 3, D]) for t in ("a1", "a3")}
        wo_pad = {t: sb("wo_pad_" + t, [P, 4, D]) for t in ("a1", "a3")}
        wq2 = sb("wq2", [P, D])
        w_up = {"f1": sb("up_f1", [P, 10, 64])}
        w_dn = {"f1": sb("dn_f1", [P, 10, D])}
        big = sb("big", [P, 2 * 8 * 512])
        w_up["f0"] = big[:, 0:9 * 512].rearrange("p (e j f) -> p e j f", e=9, j=2)
        w_dn["f0"] = big[:, 9 * 512:9 * 768].rearrange("p (e c o) -> p e c o", e=9, c=2)
        w_up["f2"] = w_up["f3"] = big_up = big[:, 0:4096].rearrange("p (e f) -> p e f", e=8)
        w_dn["f2"] = w_dn["f3"] = big_dn = big[:, 4096:8192].rearrange("p (e c o) -> p e c o", e=8, c=4)
        w_shared2 = sb("w_shared2", [P, D])
        w_gate = {t: sb("gate_" + t, [P, MOE[t]["routed"]]) for t in MOE}
        b_gate = {"f1": sb("bgate_f1", [P, 8]), "f3": sb("bgate_f3", [P, 4])}
        b_up = {"f1": sb("bup_f1", [P, 5]), "f2": sb("bup_f2", [P, 32]), "f3": sb("bup_f3", [P, 24])}
        b_dn = {"f1": sb("bdn_f1", [9, D]), "f2": sb("bdn_f2", [8, D]), "f3": sb("bdn_f3", [6, D])}
        gb0 = sb("gb0", [P, 4])
        split = sb("split", [P, 2])
        lane8 = sb("lane8", [P, 4])
        bqk3 = sb("bqk3", [P, 2, 4])
        bqk3_split = sb("bqk3_split", [P, 2, 4])
        bv_pad = sb("bv_pad", [P, 4])
        bo = {"a1": sb("bo_a1", [P, D]), "a3": sb("bo_a3", [P, D])}
        bo3_all = sb("bo3_all", [P, D])
        sb2 = sb("sb2", [P, 3, D])
        ident = sb("ident", [P, P])
        rowmask = sb("rowmask", [P, 2 + HEADS])
        neg_half = sb("neg_half", [P, 6])
        pos_half = sb("pos_half", [P, 2, 8])
        euler = sb("euler", [P, 2, 8])
        bias1 = sb("bias1", [P, NT, S2])
        bias2 = sb("bias2", [P, NT, S])
        mask1_u8 = sb("mask1_u8", [P, NT, S2], U8)
        tok = sb("tok", [P, 2, CT + NT, D])
        X = tok[:, :, CT:CT + NT, :]
        xin = sb("xin", [P, 2, NT, D])
        nrm = sb("nrm", [P, CT + NT, D])
        stats = sb("stats", [P, CT + NT, 6])
        mv = sb("mv", [P, CT + NT, 2])
        var_eps = sb("var_eps", [P, CT + NT])
        rstd = sb("rstd", [P, CT + NT])
        ctxT = sb("ctxT", [P, 2, S2])
        kvT = sb("kvT", [P, KV0])
        xnT = sb("xnT", [P, 2, S])
        mask_u8 = sb("mask_u8", [P, 2, 2, S2], U8)
        bias0 = sb("bias0", [P, KV0])
        bias3 = bias0[:, 0:S2]
        with nc.sbuf_tensor("keysT", [P, HALF, KV0], F32) as keysT, \
                nc.sbuf_tensor("qm", [P, HEADS, S], F32) as qm:
            pass
        kst = sb("kst", [P, 4, S2], F32R)
        qst = sb("qst", [P, 4, S], F32R)
        qst_m = sb("qst_m", [P, HEADS, S], F32R)
        probT_more = sb("probT_more", [P, HALF * KV0 - 4 * S2 - 4 * S]).ap().rearrange("p (s k q) -> p s k q", s=3, k=CT)
        vals = sb("vals", [P, 6, 1024])
        vals_pad = vals[:, 0:2, :].rearrange("p a b -> p (a b)").rearrange("p (k h r) -> p k h r", k=CT, h=HEADS)
        prob = sb("prob", [P, 4, KV0])
        probT = sb("probT", [P, 24, P])
        probT_heads = probT[:].rearrange("p (s k t) q -> p s k (t q)", s=3, k=CT)
        negmax = sb("negmax", [P, HEADS * NT])
        lsum = sb("lsum", [P, HEADS, NT])
        linv = sb("linv", [P, HEADS, NT])
        linv_wide = sb("linv_wide", [P, 2, NT, P])
        o_raw = sb("o_raw", [P, 2, S])
        oT = sb("oT", [P, HALF, S])
        hT = keysT[:, 0:4, 0:512].rearrange("p a (b c) -> p a b c", b=2)
        act_tmp = prob[:, :, 0:S]
        logit = sb("logit", [P, NT, 8])
        top8 = sb("top8", [P, NT, 8])
        cut = sb("cut", [P, NT, 8])
        rt = [sb(f"rt{i}", [P, NT, 8]) for i in range(5)]
        rsum = sb("rsum", [P, NT])
        rinv = sb("rinv", [P, NT])
        comb = sb("comb", [P, 2, NT, 10])
        combT = sb("combT", [16, S])
        acc = o_raw[:, 0, :].rearrange("p (k d) -> p k d", d=D)
        gl = sb("gl", [P, 2, NT, D])
        end_stats = sb("end_stats", [P, NT, 6])
        end_mv = sb("end_mv", [P, NT, 2])
        end_var = sb("end_var", [P, NT])
        end_rstd = sb("end_rstd", [P, NT])
        ps = ctx.enter_context(nc.psum_tensor("ps", [P, 8, 512], F32))

        def sem(name):
            return ctx.enter_context(nc.semaphore(name))

        w_early, w_rest, w_out = sem("w_early"), sem("w_rest"), sem("w_out")
        masks = sem("masks")
        zeroed = sem("zeroed")
        consts_ready = sem("consts_ready")
        loaded = sem("loaded")
        go = {e: sem("go_" + e) for e in ("pe", "act", "dve", "pool")}
        names = ["bv_wide", "bv_out", "bo3", "stats", "rstd", "normed", "xT", "xnT", "x_done", "vals_zeroed",
                 "big0_loaded", "big2_loaded", "big3_loaded", "dve_step", "pool_step", "stored", "ended"]
        for t in PHASES:
            if t[0] == "a":
                names += [t + "_" + n for n in ("proj", "ev_dve", "ev_act", "qproj", "qm", "scores", "biased", "exped",
                                                "turned", "pt_dve", "y")]
                if t != "a2":
                    names += [t + "_" + n for n in ("pt_act", "av", "o_raw", "linv", "r", "oT",
                                                    "qm_act")]
            else:
                names += [t + "_" + n for n in ("logits", "logit", "r_act", "comb", "up", "act", "down", "y_used")]
                names += ["f0_h"] if t == "f0" else [t + "_" + n for n in ("combT", "combT_sb", "b2", "r_mid")]
        names += ["f1_r_pool", "f2_sh", "f2_gl", "f2_e_stats", "f2_e_rstd"]
        s = {n: sem(n) for n in names}
        nums = sorted(x.num for x in s.values())
        assert nums == list(range(nums[0], nums[0] + len(nums)))
        block = ctx.enter_context(nc.Block())

        def unit(t, u):
            c, rest = divmod(u, NT * ATT[t]["hpc"])
            if t == "a0":
                qt, j = divmod(rest, ATT[t]["hpc"])
            else:
                j, qt = divmod(rest, NT)
            return c * ATT[t]["hpc"] + j, qt

        def turned_at(u):
            n = KV0 // P
            return u % (24 // n) * n

        def turned_head(h):
            return (probT_heads if h % 6 < 3 else probT_more)[:, h % 3]

        def turned_to(t, u, half):
            n = ATT[t]["nk"] // P // 2
            if t == "a0":
                return probT[:, turned_at(u) + half * n:turned_at(u) + half * n + n, :]
            h, qt = unit(t, u)
            return turned_head(h)[:, half * n:half * n + n, P * qt:P * qt + P]

        def contracted(t, u):
            if t == "a0":
                old = u - 24 // (KV0 // P)
                return old // ATT[t]["hpc"] + 1 if old >= 0 else 0
            old = unit(t, u)[0] - 6
            return old // ATT[t]["hpc"] + 1 if old >= 0 else 0

        def nth(t, r):
            return RUNS.index((t, r))

        def before(t, r, name):
            once = {"stats": NT, "rstd": 1, "normed": NT, "xT": NT, "xnT": 1, "x_done": NT}[name]
            more = {"stats": CT + NT, "rstd": 1, "normed": CT + NT, "xT": CT, "xnT": 1}.get(name, 0)
            return once * nth(t, r) + more * min(nth(t, r), 2)

        def since(t, r, name):
            if r == 0:
                return 0
            if t == "a2":
                return {"proj": 1 + NT, "scores": NT, "biased": NT, "exped": NT, "turned": NT, "pt_dve": NT,
                        "y": NT}.get(name, 1)
            if t[0] == "a":
                nj, nch, units = len(proj_jobs()), HEADS // ATT[t]["hpc"], HEADS * NT
                if t != "a0" and name in ("proj", "ev_act", "ev_dve"):
                    return 8 if name == "ev_dve" else 9
                return {"proj": nj, "ev_dve": (nj + 1) // 2, "ev_act": nj // 2, "qproj": HALF,
                        "qm": HALF, "qm_act": HALF, "scores": units,
                        "biased": units, "exped": units, "turned": 2 * units, "pt_dve": units, "pt_act": units,
                        "av": HEADS * NT // 2 if t == "a0" else nch, "y": NT}.get(name, nch)
            groups = expert_groups(t)
            ne, units = first_of(groups, len(groups)), len(groups) * MOE[t]["chunks"]
            return {"up": units, "act": units, "h": units, "down": ne, "y_used": NT * (ne - (t == "f0")),
                    "r_act": 3 if t == "f1" else 1}.get(name, 1)

        def proj_jobs():
            def keys(lo, hi):
                return [(hi - lo, wkv0[:, P * c:P * c + P], kvT[:, lo:hi], keysT[:, c, lo:hi]) for c in range(HALF)]

            def values(lo, hi):
                return [(512, kvT[:, P * k:P * k + P], wkv0[:, 1024 + 512 * j:1536 + 512 * j],
                         vals[:, k, 512 * j:512 * j + 512]) for k in range(lo, hi) for j in range(2)]

            return keys(0, S2) + values(0, CT) + keys(S2, KV0) + values(CT, KV0 // P)

        LATE = HALF + 2 * CT

        def proj_order():
            order = []
            for j in range(len(proj_jobs())):
                order.append(("kv", j))
                if 0 <= j - LATE < HALF:
                    order.append(("q", j - LATE))
            return order

        def stack_out(g, keys):
            return ps[:, (0, 2, 1, 3)[g], :] if keys else ps[:, 4 + g, 0:S]

        def turned_bank(t, u, half):
            return 4 + half if t == "a0" or u % 2 == 0 else 1 + 2 * half

        def expert_groups(t):
            e, n = MOE[t]["routed"], MOE[t]["shared"]
            if t == "f1":
                return [[8]] + [[i, i + 1] for i in range(0, e, 2)]
            return [[i] for i in (*range(e, e + n), *range(e))]

        def first_of(groups, g):
            return sum(len(x) for x in groups[:g])

        def down_before(t, u):
            return first_of(expert_groups(t), (u - 8) // MOE[t]["chunks"] + 1)

        def iteration_end(eng, me):
            eng.drain().then_inc(s["ended"], 1)
            eng.wait_ge(go[me], 1)
            eng.sem_clear(go[me])

        N_EARLY, N_REST = 16 * 7, 16 * 55
        N_LOAD, N_BIG0, N_BIG = 16 * 10, 16 * 13, 16 * 4
        N_CONSTS = 1 + NT + 2

        @block.sync
        def _(sp):
            issued = {"early": 0, "rest": 0}

            def early(dst, src):
                sp.dma_start(dst, src).then_inc(w_early, 16)
                issued["early"] += 1

            def rest(dst, src):
                sp.dma_start(dst, src).then_inc(w_rest, 16)
                issued["rest"] += 1

            def col(name):
                return a[name].rearrange("(p o) -> p o", o=1)

            def load_pair(pair):
                for r in range(2):
                    one = bass.ds(2 * pair + r, 1)
                    for dst, src in (
                            (tok[:, r, 0:CT, :], a["ctx_1024"][one].rearrange("o (t p) d -> p (o t) d", p=P)),
                            (xin[:, r], a["x"][one].rearrange("o (t p) d -> p (o t) d", p=P)),
                            (mask_u8[:, r, 0, :], a["mask0"][one, :].broadcast_to([P, S2])),
                            (mask_u8[:, r, 1, :], a["mask3"][one, :].broadcast_to([P, S2])),
                            (ctxT[:, r, :], a["ctxT"][one].rearrange("o d s -> d (o s)"))):
                        sp.dma_start(dst, src).then_inc(loaded, 16)

            load_pair(0)
            for j, n in enumerate(("g1", "b1", "g2", "b2")):
                early(gb0[:, j:j + 1], col("L0_xattn_" + n))
            early(wkv0[:], a["L0_xattn_Wkv"])
            early(wq0[:], a["L0_xattn_Wq"])
            early(wo0[:], a["L0_xattn_Wout"].rearrange("(c p) o -> p c o", p=P))
            rest(mask1_u8[:], a["mask1"].rearrange("(t p) k -> p t k", p=P))

            for t, l in (("a1", "L1"), ("a3", "L3")):
                rest(bo[t][:], a[f"{l}_xattn_bo"].rearrange("(o d) -> o d", o=1).broadcast_to([P, D]))
            sp.wait_ge(zeroed, 5)
            for t, l in (("a1", "L1"), ("a3", "L3")):
                wo = a[f"{l}_xattn_WoT"].rearrange("(c j i) o -> j i c o", c=4, j=4)
                for j in range(4):
                    rest(wo_pad[t][32 * j:32 * j + 8], wo[j])
            bv = a["L3_xattn_bv"].rearrange("(c j i) -> j i c", c=4, j=4)
            with nc.allow_non_contiguous_dma(reason="128 biases into columns"):
                for j in range(4):
                    rest(bv_pad[32 * j:32 * j + 8, :], bv[j])
            rest(w_gate["f0"][:], a["L0_ffn_Wg"])
            for t, l in (("a1", "L1"), ("a3", "L3")):
                for j, n in enumerate("qkv"):
                    rest(wqkv[t][:, j, :], a[f"{l}_xattn_W{n}T"])
            with nc.allow_non_contiguous_dma(reason="128 biases into columns"):
                for j, n in enumerate(("bq", "bk")):
                    for k in range(4):
                        rest(bqk3[32 * k:32 * k + 32, j, :], a["L3_xattn_" + n].rearrange("(g r) -> r g", r=32))
            rest(w_gate["f1"][:], a["L1_ffn_routing_WT"])
            rest(b_gate["f1"][:], a["L1_ffn_expert_bias"].rearrange("(o d) -> o d", o=1).broadcast_to([P, 8]))
            rest(w_up["f1"][:, 0:8, :], a["L1_ffn_rW1"].rearrange("e d f -> d e f"))
            rest(w_up["f1"][:, 8, :], a["L1_ffn_sW1"])
            rest(b_dn["f1"][0:8, :], a["L1_ffn_rb2"])
            rest(b_dn["f1"][8:9, :], a["L1_ffn_sb2"].rearrange("(o d) -> o d", o=1))
            rest(wq2[:], a["L2_xattn_WqT"])
            rest(w_gate["f2"][:], a["L2_ffn_gate_W"])
            rest(w_shared2[:], a["L2_ffn_shared_W"])
            rest(b_up["f2"][:], a["L2_ffn_b1c"])
            rest(b_dn["f2"][:], a["L2_ffn_b2"])
            for j, n in enumerate(("shared_b", "gamma", "beta")):
                rest(sb2[:, j, :], a["L2_ffn_" + n].rearrange("(o d) -> o d", o=1).broadcast_to([P, D]))
            rest(w_gate["f3"][:], a["L3_ffn_gate_w"])
            rest(b_gate["f3"][:], a["L3_ffn_gate_b"].rearrange("(o d) -> o d", o=1).broadcast_to([P, 4]))
            rest(b_up["f3"][:, 0:16], a["L3_ffn_rb1c"])
            rest(b_up["f3"][:, 16:24], a["L3_ffn_sb1c"])
            rest(b_dn["f3"][0:4, :], a["L3_ffn_rb2"])
            rest(b_dn["f3"][4:6, :], a["L3_ffn_sb2"])
            rest(b_up["f1"][:, 0:4], a["L1_ffn_rb1c"])
            rest(b_up["f1"][0:64, 4:5], col("L1_ffn_sb1"))
            w2 = a["L1_ffn_rW2"].rearrange("(q two) h o -> two h q o", two=2)
            pad_dn = w_dn["f1"][:].rearrange("p (q two) o -> p two q o", two=2)
            rest(pad_dn[0:64, 0, 0:4, :], w2[0])
            rest(pad_dn[64:128, 1, 0:4, :], w2[1])
            rest(w_dn["f1"][0:64, 8, :], a["L1_ffn_sW2"])
            assert (16 * issued["early"], 16 * issued["rest"]) == (N_EARLY, N_REST)

            with sp.Fori(0, B // 2) as i:
                def load_big(which, dst, src):
                    sp.dma_start(dst, src).then_inc(s[which], 16)

                load_big("big0_loaded", w_up["f0"][:, 8, 0, :], a["L0_ffn_Ws1"])
                load_big("big0_loaded", w_up["f0"][:, 8, 1, :], a["L0_ffn_Ws3"])
                load_big("big0_loaded", w_dn["f0"][:, 8], a["L0_ffn_Ws2"].rearrange("(c p) o -> p c o", p=P))
                load_big("big0_loaded", w_up["f0"][:, 0:8, 0, :], a["L0_ffn_We1"].rearrange("e d f -> d e f"))
                load_big("big0_loaded", w_up["f0"][:, 0:8, 1, :], a["L0_ffn_We3"].rearrange("e d f -> d e f"))
                for e in range(8):
                    load_big("big0_loaded", w_dn["f0"][:, e], a["L0_ffn_We2"][e].rearrange("(c p) o -> p c o", p=P))
                sp.wait_ge(s["x_done"], before("f0", 1, "x_done") + NT)
                for e in range(0, 8, 4):
                    load_big("big2_loaded", big_up[:, e:e + 4, :], a["L2_ffn_W1"][e:e + 4].rearrange("e d f -> d e f"))
                    load_big("big2_loaded", big_dn[:, e:e + 4], a["L2_ffn_W2"][e:e + 4].rearrange("e (c p) o -> p e c o", p=P))
                sp.wait_ge(s["x_done"], before("f2", 1, "x_done") + NT)
                load_big("big3_loaded", big_up[:, 0:4, :], a["L3_ffn_rw1"].rearrange("e d f -> d e f"))
                load_big("big3_loaded", big_up[:, 4:6, :], a["L3_ffn_sw1"].rearrange("e d f -> d e f"))
                load_big("big3_loaded", big_dn[:, 0:4], a["L3_ffn_rw2"].rearrange("e (c p) o -> p e c o", p=P))
                load_big("big3_loaded", big_dn[:, 4:6], a["L3_ffn_sw2"].rearrange("e (c p) o -> p e c o", p=P))
                sp.wait_ge(s["x_done"], before("a3", 1, "x_done") + NT)
                load_pair((i + 1) % (B // 2))
                for r in range(2):
                    sp.wait_ge(s["x_done"], before("f3", r, "x_done") + NT)
                    sp.dma_start(out[bass.ds(2 * i + r, 1)].rearrange("o (t p) d -> p (o t) d", p=P), X[:, r]) \
                        .then_inc(s["stored"], 16)
                sp.wait_ge(s["stored"], 32)
                sp.wait_ge(s["ended"], 4)
                sp.sem_clear(range(nums[0], nums[-1] + 1))
                for e in go:
                    sp.sem_inc(go[e], 1)
            sp.wait_ge(loaded, N_LOAD)

        @block.gpsimd
        def _(pool):
            for tile, value in ((ident, 0.0), (neg_half, -0.5), (rowmask, 1.0)):
                nc.gpsimd.memset(tile[:], value).then_inc(masks, 1)
            pool.wait_ge(masks, 3)
            nc.gpsimd.affine_select(out=ident[:], in_=ident[:], compare_op=ALU.not_equal, fill=1.0, base=0,
                                    pattern=[[-1, P]], channel_multiplier=1).then_inc(consts_ready, 1)
            for tile in (wo_pad["a1"][:], wo_pad["a3"][:], bv_pad[:], b_up["f1"][:], w_dn["f1"][:], w_up["f1"][:, 9, :],
                         bias0[:], bias2[:]):
                nc.gpsimd.memset(tile, 0.0).then_inc(zeroed, 1)
            nc.gpsimd.memset(pos_half[:], 0.5).then_inc(zeroed, 1)
            nc.gpsimd.memset(euler[:], math.e).then_inc(zeroed, 1)
            pool.wait_ge(zeroed, 10)
            for t in range(NT):
                nc.gpsimd.affine_select(out=bias2[:, t, :], in_=bias2[:, t, :], compare_op=ALU.is_ge, fill=-FAR,
                                        base=P * t, pattern=[[-1, S]], channel_multiplier=1).then_inc(consts_ready, 1)
            for c0, n, w in ((0, 2, 64), (2, HEADS, 8)):
                m = rowmask[:, c0:c0 + n]
                nc.gpsimd.affine_select(out=m, in_=m, compare_op=ALU.is_ge, fill=0.0, base=0, pattern=[[-w, n]],
                                        channel_multiplier=1).then_inc(masks, 1)
            pool.wait_ge(masks, 5)
            for c0, n, w in ((0, 2, 64), (2, HEADS, 8)):
                m = rowmask[:, c0:c0 + n]
                nc.gpsimd.affine_select(out=m, in_=m, compare_op=ALU.is_ge, fill=0.0, base=w - 1, pattern=[[w, n]],
                                        channel_multiplier=-1).then_inc(consts_ready, 1)
            with pool.Fori(0, B // 2):
                def root(mean_var, tmp, dst, signal):
                    nc.gpsimd.tensor_scalar(tmp, mean_var[:, :, 1], EPS, None, ALU.add).then_inc(s["pool_step"], 1)
                    n_pool[0] += 1
                    pool.wait_ge(s["pool_step"], n_pool[0])
                    nc.gpsimd.tensor_tensor(dst, tmp, neg_half[:, 0:tmp.shape[1]], ALU.pow).then_inc(signal, 1)

                n_pool = [0]

                def ready_next(t, r):
                    n = before(t, r, "stats")
                    if t == "a0":
                        pool.wait_ge(s["stats"], n + CT + NT)
                        root(mv[:], var_eps[:], rstd[:], s["rstd"])
                        n += CT + NT
                    pool.wait_ge(s["stats"], n + NT)
                    root(mv[:, CT:CT + NT, :], var_eps[:, CT:CT + NT], rstd[:, CT:CT + NT], s["rstd"])
                    if t == "f2":
                        pool.wait_ge(s["f2_r_mid"], since(t, r, "r_mid") + 1)
                        nc.gpsimd.tensor_tensor(rt[3][:], euler[:], rt[1][:], ALU.pow).then_inc(s["f2_r_act"], 1)
                    if t == "f1":
                        pool.wait_ge(s["f1_r_mid"], since(t, r, "r_mid") + 1)
                        nc.gpsimd.tensor_tensor(rt[3][:], rt[2][:], pos_half[:], ALU.pow).then_inc(s["f1_r_pool"], 1)

                ready_next(*RUNS[0])
                for n, (t, r) in enumerate(RUNS):
                    if (t, r) == ("f0", 0):
                        pool.wait_ge(s["x_done"], before(t, r, "x_done"))
                        nc.gpsimd.memset(vals_pad, 0.0).then_inc(s["vals_zeroed"], 1)
                    if n + 1 < len(RUNS):
                        ready_next(*RUNS[n + 1])
                    if t == "f2":
                        pool.wait_ge(s["f2_e_stats"], since(t, r, "e_stats") * NT + NT)
                        root(end_mv[:], end_var[:], end_rstd[:], s["f2_e_rstd"])
                iteration_end(pool, "pool")

        @block.tensor
        def _(pe):
            mm, tr = nc.tensor.matmul, nc.tensor.transpose
            pe.wait_ge(consts_ready, N_CONSTS)

            def constant_out():
                pe.wait_ge(s["bv_wide"], 1)
                pe.wait_ge(s["x_done"], before("f0", 0, "x_done"))
                for c in range(4):
                    m = mm(ps[:, 6, 0:D], vals[:, 2 + c, 0:P], wo_pad["a3"][:, c, :], start=(c == 0), stop=(c == 3))
                m.then_inc(s["bv_out"], 1)

            def turn_x(t, r, first=False):
                ready, seen = before(t, r, "normed"), before(t, r, "xnT")
                if t == "a0":
                    for k in range(CT):
                        pe.wait_ge(s["normed"], ready + k + 1)
                        tr(ps[:, 7, P * k:P * k + P], nrm[:, k, :], ident[:]).then_inc(s["xT"], 1)
                    ready += CT + NT
                    pe.wait_ge(s["xnT"], seen + 1)
                    if first:
                        begin(t, r)
                for k in range(NT):
                    pe.wait_ge(s["normed"], ready + k + 1)
                    tr(ps[:, 7, P * k:P * k + P], nrm[:, CT + k, :], ident[:]).then_inc(s["xT"], 1)

            def route(t, r):
                if t[0] == "a":
                    return
                pe.wait_ge(s["xnT"], before(t, r, "xnT") + 1)
                if t == "f0":
                    pe.wait_ge(w_rest, N_REST)
                for k in range(NT):
                    m = mm(ps[:, 7, 8 * k:8 * k + MOE[t]["routed"]], xnT[:, r, P * k:P * k + P], w_gate[t][:],
                           start=True, stop=True)
                if t == "f2":
                    for k in range(NT):
                        m = mm(ps[:, 7, S + P * k:S + P * k + P], xnT[:, r, P * k:P * k + P], w_shared2[:],
                               start=True, stop=True)
                m.then_inc(s[t + "_logits"], 1)

            def projections(t, r, part):
                jobs = proj_jobs()
                if part == 1 and nth(t, r):
                    pe.wait_ge(s["x_done"], before(t, r, "x_done"))
                for kind, j in proj_order()[:6] if part == 0 else proj_order()[6:]:
                    if kind == "q":
                        if j >= 2:
                            pe.wait_ge(s[t + ("_qm_act" if j % 2 else "_qm")], since(t, r, "qm") + 2 * (j // 2))
                        mm(ps[:, 6 + j % 2, 0:S], wq0[:, P * j:P * j + P], kvT[:, S2:KV0], start=True, stop=True) \
                            .then_inc(s[t + "_qproj"], 1)
                        continue
                    if j == LATE:
                        pe.wait_ge(s["xnT"], before(t, r, "xnT") + 2)
                    n, lhsT, rhs, _ = jobs[j]
                    if j >= 6:
                        k = j - 6
                        pe.wait_ge(s[t + ("_ev_act" if k % 2 else "_ev_dve")],
                                   since(t, r, "ev_act" if k % 2 else "ev_dve") + k // 2 + 1)
                    mm(ps[:, j % 6, 0:n], lhsT, rhs, start=True, stop=True).then_inc(s[t + "_proj"], 1)

            def stacked_projections(t, r, part):
                for g in (0, 1) if part == 0 else (2, 3):
                    if g == 2:
                        pe.wait_ge(s["x_done"], before(t, r, "x_done"))
                    for w, rhs in ((1, ctxT[:, r, :]), (0, xnT[:, r, :])):
                        for k in range(4):
                            m = mm(stack_out(g, w == 1)[32 * k:32 * k + 32, :], wqkv[t][:, w, 32 * g:32 * g + 32], rhs,
                                   start=True, stop=True)
                        m.then_inc(s[t + "_proj"], 1)
                if part == 0:
                    return
                pe.wait_ge(s[t + "_ev_dve"], since(t, r, "ev_dve") + 2)
                for k in range(CT):
                    m = mm(ps[:, 4, P * k:P * k + P], ctxT[:, r, P * k:P * k + P], wqkv[t][:, 2, :], start=True, stop=True)
                m.then_inc(s[t + "_proj"], 1)

            def attention(t, r, after):
                nk, hpc, rows = ATT[t]["nk"], ATT[t]["hpc"], ATT[t]["rows"]
                half = nk // P // 2
                if t == "a0":
                    nj = len(proj_jobs())
                    pe.wait_ge(s[t + "_ev_dve"], since(t, r, "ev_dve") + (nj + 1) // 2)
                    pe.wait_ge(s[t + "_ev_act"], since(t, r, "ev_act") + nj // 2)
                U = HEADS * NT

                def scores(u):
                    h, qt = unit(t, u)
                    if t == "a0":
                        pe.wait_ge(s[t + ("_qm_act" if h // 2 % 2 else "_qm")],
                                   since(t, r, "qm") + 2 * (h // 4) + h % 2 + 1)
                    else:
                        pe.wait_ge(s[t + "_ev_dve"], since(t, r, "ev_dve") + (4 if u == 1 else 2 * (h // 4) + 2))
                        pe.wait_ge(s[t + ("_qm_act" if h % 4 >= 2 else "_qm")],
                                   since(t, r, "qm") + 2 * (h // 4) + h % 2 + 1)
                    if u >= 2:
                        pe.wait_ge(s[t + "_biased"], since(t, r, "biased") + u - 1)
                    if t == "a0":
                        lhsT, kt = qm[:, h, P * qt:P * qt + P], keysT[:, h // 2, :]
                        mm(ps[:, 2 * (u % 2), 0:512], lhsT, kt[:, 0:512], start=True, stop=True)
                        m = mm(ps[:, 2 * (u % 2) + 1, 0:nk - 512], lhsT, kt[:, 512:nk], start=True, stop=True)
                    else:
                        m = mm(ps[:, 2 * (u % 2), :], qst_m[:, h, P * qt:P * qt + P], kst[:, h // 4, :],
                               start=True, stop=True)
                    m.then_inc(s[t + "_scores"], 1)

                def turn(u):
                    pe.wait_ge(s[t + "_exped"], since(t, r, "exped") + u + 1)
                    if t != "a0" and u == 0:
                        pe.wait_ge(s[t + "_ev_dve"], since(t, r, "ev_dve") + 8)
                        pe.wait_ge(s[t + "_ev_act"], since(t, r, "ev_act") + 9)
                    ago = 1 if t == "a0" else 2
                    for g in range(2):
                        if u >= ago:
                            pe.wait_ge(s[t + ("_pt_act" if g else "_pt_dve")], since(t, r, "pt_dve") + u - ago + 1)
                        for k in range(half):
                            kk = g * half + k
                            m = tr(ps[:, turned_bank(t, u, g), P * k:P * k + P], prob[:, u % 4, P * kk:P * kk + P],
                                   ident[:])
                        m.then_inc(s[t + "_turned"], 1)

                def spread_inverses(c):
                    pe.wait_ge(s[t + "_linv"], since(t, r, "linv") + c + 1)
                    for q in range(NT):
                        m = tr(ps[:, 6, S + P * q:S + P * q + P], linv_wide[:, c % 2, q, :], ident[:])
                    m.then_inc(s[t + "_r"], 1)

                def av(g):
                    (c, qt), units = divmod(g, NT), range(hpc * g, hpc * g + hpc)
                    pe.wait_ge(s[t + "_pt_dve"], since(t, r, "pt_dve") + units[-1] + 1)
                    pe.wait_ge(s[t + "_pt_act"], since(t, r, "pt_act") + units[-1] + 1)
                    if g == 0:
                        pe.wait_ge(s[t + "_qm"], since(t, r, "qm") + HEADS // 2)
                        pe.wait_ge(s[t + "_qm_act"], since(t, r, "qm_act") + HEADS // 2)
                    if qt == 0 and c >= 1:
                        pe.wait_ge(s[t + "_oT"], since(t, r, "oT") + c)
                    for k in range(nk // P):
                        for j, u in enumerate(units):
                            h = hpc * c + j
                            m = mm(ps[rows * j:rows * j + rows, 6, P * qt:P * qt + P], vals[:, k, 64 * h:64 * h + 64],
                                   probT[:, turned_at(u) + k, :], start=(k == 0), stop=(k == nk // P - 1))
                    m.then_inc(s[t + "_av"], 1)
                    if qt == NT - 1:
                        spread_inverses(c)

                def av_both(c, key_tiles):
                    if key_tiles[0] == 0:
                        pe.wait_ge(s[t + "_pt_dve"], since(t, r, "pt_dve") + NT * hpc * (c + 1))
                        pe.wait_ge(s[t + "_pt_act"], since(t, r, "pt_act") + NT * hpc * (c + 1))
                        if c >= 1:
                            pe.wait_ge(s[t + "_oT"], since(t, r, "oT") + c)
                    for k in key_tiles:
                        for j in range(hpc):
                            h = hpc * c + j
                            m = mm(ps[rows * j:rows * j + rows, 6, 0:S], vals_pad[:, k, h, :], turned_head(h)[:, k, :],
                                   start=(k == 0), stop=(k == CT - 1))
                    if key_tiles[-1] == CT - 1:
                        m.then_inc(s[t + "_av"], 1)
                        spread_inverses(c)

                for i in range(U + 5):
                    if i < U:
                        scores(i)
                    if 3 <= i < U + 3:
                        turn(i - 3)
                    if t == "a0":
                        if i >= 5 and (i - 5) % hpc == hpc - 1:
                            av((i - 5) // hpc)
                    elif i == U + 4:
                        av_both(HEADS // hpc - 1, range(CT))
                    elif i >= 12 and (i - 12) % 8 < 3:
                        av_both((i - 12) // 8, ([0, 1], [2], [3])[(i - 12) % 8])
                    if after and i == 17:
                        turn_x(*after)
                    if after and i == 25:
                        route(*after)
                begin(*after)
                nch = HEADS // hpc
                wo = wo0 if t == "a0" else wo_pad[t]
                pe.wait_ge(s[t + "_oT"], since(t, r, "oT") + nch)
                for qt in range(NT):
                    for c in range(nch):
                        m = mm(ps[:, 6, P * qt:P * qt + P], oT[:, c, P * qt:P * qt + P], wo[:, c, :],
                               start=(c == 0), stop=(c == nch - 1))
                    m.then_inc(s[t + "_y"], 1)

            def attention2(r, after):
                t = "a2"
                pe.wait_ge(s["x_done"], before(t, r, "x_done"))
                mm(ps[:, 0, 0:S], wq2[:], ctxT[:, r, 0:S], start=True, stop=True).then_inc(s[t + "_proj"], 1)
                for k in range(NT):
                    mm(ps[:, 1, P * k:P * k + P], ctxT[:, r, P * k:P * k + P], wq2[:], start=True, stop=True) \
                        .then_inc(s[t + "_proj"], 1)
                mm(ps[:, 6, 0:S], wq2[:], xnT[:, r, :], start=True, stop=True).then_inc(s[t + "_qproj"], 1)
                pe.wait_ge(s[t + "_qm"], since(t, r, "qm") + 1)
                pe.wait_ge(s[t + "_ev_dve"], since(t, r, "ev_dve") + 1)
                pe.wait_ge(s[t + "_ev_act"], since(t, r, "ev_act") + 1)
                for qt in range(NT):
                    mm(ps[:, 2 + qt, 0:S], qm[:, 0, P * qt:P * qt + P], keysT[:, 0, 0:S], start=True, stop=True) \
                        .then_inc(s[t + "_scores"], 1)
                turn_x(*after)
                for qt in range(NT):
                    pe.wait_ge(s[t + "_exped"], since(t, r, "exped") + qt + 1)
                    for k in range(qt + 1):
                        m = tr(ps[:, 4 + qt, P * k:P * k + P], prob[:, qt, P * k:P * k + P], ident[:])
                    m.then_inc(s[t + "_turned"], 1)
                route(*after)
                if after[0] != "a2":
                    begin(*after)
                for qt in range(NT):
                    pe.wait_ge(s[t + "_pt_dve"], since(t, r, "pt_dve") + qt + 1)
                    for k in range(qt + 1):
                        m = mm(ps[:, 6, P * qt:P * qt + P], probT[:, NT * qt + k, :], vals[:, 2, P * k:P * k + P],
                               start=(k == 0), stop=(k == qt))
                    m.then_inc(s[t + "_y"], 1)

            def up(t, r, u):
                g, c = divmod(u, MOE[t]["chunks"])
                if u >= 4:
                    pe.wait_ge(s[t + ("_h" if t == "f0" else "_act")], since(t, r, "up") + u - 3)
                e = expert_groups(t)[g][0]
                if t == "f0":
                    for j in range(2):
                        m = mm(ps[:, u % 4, S * j:S * j + S], w_up[t][:, e, j, P * c:P * c + P], xnT[:, r, :],
                               start=True, stop=True)
                elif t == "f1":
                    m = mm(ps[:, u % 4, 0:S], w_up[t][:, e:e + 2, :].rearrange("p a b -> p (a b)"), xnT[:, r, :],
                           start=True, stop=True)
                else:
                    m = mm(ps[:, u % 4, 0:S], w_up[t][:, e, P * c:P * c + P], xnT[:, r, :], start=True, stop=True)
                m.then_inc(s[t + "_up"], 1)

            def mixture(t, r, after):
                cfg = MOE[t]
                ne, nch = cfg["routed"] + cfg["shared"], cfg["chunks"]
                groups = expert_groups(t)

                def down(g):
                    pe.wait_ge(s[t + ("_h" if t == "f0" else "_act")], since(t, r, "up") + nch * (g + 1))
                    for i, e in enumerate(groups[g]):
                        n = first_of(groups, g) + i
                        if n >= 2:
                            pe.wait_ge(s[t + "_y_used"], since(t, r, "y_used") + NT * (n - 1))
                        elif r == 1 and t == "f0":
                            pe.wait_ge(s["x_done"], before(t, r, "x_done"))
                        elif r == 1:
                            pe.wait_ge(s[t + "_y_used"], NT * (ne - (ne - 1 - n) % 2))
                        for k in range(NT):
                            for c in range(nch):
                                u = g * nch + c
                                w = w_dn[t][:, e, :] if t == "f1" else w_dn[t][:, e, c, :]
                                m = mm(ps[:, 4 + n % 2, P * k:P * k + P], hT[:, u % 8 // 2, u % 2, P * k:P * k + P], w,
                                       start=(c == 0), stop=(c == nch - 1))
                        m.then_inc(s[t + "_down"], 1)

                def turn_weights():
                    pe.wait_ge(s["x_done"], before(t, r, "x_done"))
                    pe.wait_ge(s[t + "_comb"], since(t, r, "comb") + 1)
                    for k in range(NT):
                        m = tr(ps[0:ne, 6, P * k:P * k + P], comb[:, r, k, 0:ne], ident[:])
                    m.then_inc(s[t + "_combT"], 1)

                def biases():
                    pe.wait_ge(s[t + "_combT_sb"], since(t, r, "combT_sb") + 1)
                    for k in range(NT):
                        m = mm(ps[:, 6, P * k:P * k + P], combT[0:ne, P * k:P * k + P], b_dn[t][:], start=True, stop=True)
                    m.then_inc(s[t + "_b2"], 1)

                for g in range(len(groups)):
                    for u in range(max(4, nch * (g + 1)), min(nch * (g + 2), len(groups) * nch)):
                        up(t, r, u)
                    down(g)
                    if g == 1 and t != "f0":
                        turn_weights()
                    if g == 2 and t != "f0":
                        biases()
                    if after and g == 2:
                        turn_x(*after)
                    if (t, r) == ("f0", 0) and g == 7:
                        constant_out()
                    if after and g == 3:
                        route(*after)

            def begin(t, r):
                if t[0] == "f":
                    if t == "f0":
                        pe.wait_ge(s["big0_loaded"], N_BIG0)
                    elif t == "f2":
                        pe.wait_ge(s["big2_loaded"], N_BIG)
                    elif t == "f3":
                        pe.wait_ge(s["big3_loaded"], N_BIG)
                    pe.wait_ge(w_rest, N_REST)
                    pe.wait_ge(s["xnT"], before(t, r, "xnT") + 1)
                    for u in range(4):
                        up(t, r, u)
                    return
                pe.wait_ge(s["xnT"], before(t, r, "xnT") + 1)
                if t == "a0":
                    pe.wait_ge(w_early, N_EARLY)
                    projections(t, r, 0)
                elif t != "a2":
                    stacked_projections(t, r, 0)

            with pe.Fori(0, B // 2):
                turn_x(*RUNS[0], first=True)
                for n, (t, r) in enumerate(RUNS):
                    after = RUNS[n + 1] if n + 1 < len(RUNS) else None
                    if n and (t == "a2" or RUNS[n - 1][0][0] == "f"):
                        if t[0] == "a":
                            pe.wait_ge(s["x_done"], before(t, r, "x_done"))
                        begin(t, r)
                    if t[0] == "f":
                        mixture(t, r, after)
                    elif t == "a2":
                        attention2(r, after)
                    else:
                        (projections if t == "a0" else stacked_projections)(t, r, 1)
                        attention(t, r, after)
                iteration_end(pe, "pe")

        @block.scalar
        def _(act):
            f = nc.scalar.activation

            def attention(t, r, after):
                nk, hpc = ATT[t]["nk"], ATT[t]["hpc"]
                half = nk // P // 2
                U = HEADS * NT

                def exps(u):
                    act.wait_ge(s[t + "_biased"], since(t, r, "biased") + u + 1)
                    p = prob[:, u % 4, 0:nk]
                    h, qt = unit(t, u)
                    f(p, p, ACT.Exp, bias=negmax[:, u:u + 1], scale=-1.0, accum_out=lsum[:, h, qt:qt + 1]) \
                        .then_inc(s[t + "_exped"], 1)

                def copy_turned(u):
                    act.wait_ge(s[t + "_turned"], since(t, r, "turned") + 2 * u + 2)
                    if contracted(t, u):
                        act.wait_ge(s[t + "_av"], since(t, r, "av") + contracted(t, u))
                    nc.scalar.copy(turned_to(t, u, 1),
                                   ps[:, turned_bank(t, u, 1), 0:half * P].rearrange("p (k q) -> p k q", q=P)) \
                        .then_inc(s[t + "_pt_act"], 1)

                def copy_out(c):
                    act.wait_ge(s[t + "_r"], since(t, r, "r") + c + 1)
                    if c >= 2:
                        act.wait_ge(s[t + "_oT"], since(t, r, "oT") + c - 1)
                    nc.scalar.copy(o_raw[:, c % 2, :], ps[:, 6, 0:S]).then_inc(s[t + "_o_raw"], 1)

                lag = 6 if t == "a0" else 8
                for i in range(U + lag + 1):
                    if t != "a0" and i % 8 in (1, 3) and i < 24:
                        stacked_queries(t, r, 4 * (i // 8 + 1) + 2 + i % 8 // 2)
                    if i >= lag and (i - lag) % (NT * hpc) == NT * hpc - 1:
                        copy_out((i - lag) // (NT * hpc))
                    if 3 <= i < U + 3:
                        copy_turned(i - 3)
                    if i < U:
                        exps(i)
                    if after and i == 18:
                        ready_tokens(*after)
                    if after and i == (U + 4 if after[0] == "f1" else 27):
                        ready_router(*after)

            def stacked(t, g, keys):
                j = 1 if keys else 0
                dst, src = (kst if keys else qst)[:, g, :], stack_out(g, keys)
                if t == "a3":
                    ins = f(dst, src, ACT.Identity, bias=bqk3_split[:, j, g:g + 1], scale=split[:, j:j + 1])
                else:
                    ins = f(dst, src, ACT.Copy, scale=split[:, j:j + 1])
                ins.then_inc(s[t + "_ev_act"], 1)

            def stacked_queries(t, r, h):
                act.wait_ge(s[t + "_ev_dve"], since(t, r, "ev_dve") + 2 * (h // 4) + 2)
                f(qst_m[:, h, :], qst[:, h // 4, :], ACT.Copy, scale=lane8[:, h % 4:h % 4 + 1]) \
                    .then_inc(s[t + "_qm_act"], 1)

            def ready_tokens(t, r):
                n = before(t, r, "xT")
                if t == "a0":
                    act.wait_ge(w_early, N_EARLY)
                    act.wait_ge(s["xT"], n + CT + NT)
                    if r == 1:
                        act.wait_ge(s["a0_qproj"], HALF)
                    f(kvT[:, S2:KV0], ps[:, 7, 0:S], ACT.Identity, bias=gb0[:, 3:4], scale=gb0[:, 2:3]) \
                        .then_inc(s["xnT"], 1)
                    return
                act.wait_ge(s["xT"], n + NT)
                nc.scalar.copy(xnT[:, r, :], ps[:, 7, 0:S]).then_inc(s["xnT"], 1)

            def ready_router(t, r):
                if t == "f0":
                    act.wait_ge(s[t + "_logit"], since(t, r, "logit") + 1)
                    f(rt[1][:], logit[:], ACT.Exp, scale=-1.0).then_inc(s[t + "_r_act"], 1)
                elif t == "f1":
                    act.wait_ge(s[t + "_logit"], since(t, r, "logit") + 1)
                    f(rt[1][:], logit[:], ACT.Abs).then_inc(s[t + "_r_act"], 1)
                    act.wait_ge(s[t + "_r_act"], since(t, r, "r_act") + 1)
                    f(rt[1][:], rt[1][:], ACT.Exp, scale=-1.0).then_inc(s[t + "_r_act"], 1)
                    act.wait_ge(s[t + "_r_act"], since(t, r, "r_act") + 2)
                    f(rt[1][:], rt[1][:], ACT.Ln, bias=1.0).then_inc(s[t + "_r_act"], 1)
                elif t == "f3":
                    act.wait_ge(s[t + "_r_mid"], since(t, r, "r_mid") + 1)
                    f(rt[3][:], rt[1][:], ACT.Exp).then_inc(s[t + "_r_act"], 1)
                if t == "f2":
                    act.wait_ge(s["f2_sh"], since("f2", r, "sh") + 1)
                    f(gl[:, r], gl[:, r], ACT.Gelu).then_inc(s["f2_gl"], 1)

            def mixture(t, r, after):
                groups, nch = expert_groups(t), MOE[t]["chunks"]
                for u in range(len(groups) * nch):
                    if after and u == 3 * nch:
                        ready_tokens(*after)
                    if after and t != "f1" and u == 5 * nch:
                        ready_router(*after)
                    e, c = groups[u // nch][0], u % nch
                    act.wait_ge(s[t + "_up"], since(t, r, "up") + u + 1)
                    h = hT[:, u % 8 // 2, u % 2, :]
                    if t == "f0":
                        if u >= 4:
                            act.wait_ge(s[t + "_h"], since(t, r, "h") + u - 3)
                        f(act_tmp[:, u % 4, :], ps[:, u % 4, 0:S], ACT.Silu).then_inc(s[t + "_act"], 1)
                        continue
                    if u >= 8:
                        act.wait_ge(s[t + "_down"], since(t, r, "down") + down_before(t, u))
                    col = e // 2 if t == "f1" else e * nch + c
                    f(h, ps[:, u % 4, 0:S], {"f1": ACT.Silu, "f2": ACT.Gelu, "f3": ACT.Relu}[t],
                      bias=b_up[t][:, col:col + 1]).then_inc(s[t + "_act"], 1)
                if after and t == "f1":
                    ready_router(*after)

            with act.Fori(0, B // 2):
                ready_tokens(*RUNS[0])
                for n, (t, r) in enumerate(RUNS):
                    after = RUNS[n + 1] if n + 1 < len(RUNS) else None
                    if t[0] == "f":
                        mixture(t, r, after)
                        continue
                    if t == "a2":
                        act.wait_ge(s[t + "_proj"], since(t, r, "proj") + 1 + NT)
                        nc.scalar.copy(vals[:, 2, 0:S], ps[:, 1, 0:S]).then_inc(s[t + "_ev_act"], 1)
                        for qt in range(NT):
                            act.wait_ge(s[t + "_biased"], since(t, r, "biased") + qt + 1)
                            p = prob[:, qt, 0:S]
                            f(p, p, ACT.Exp, bias=negmax[:, qt:qt + 1], scale=-1.0, accum_out=lsum[:, 0, qt:qt + 1]) \
                                .then_inc(s[t + "_exped"], 1)
                            if qt == 0:
                                ready_tokens(*after)
                        ready_router(*after)
                    elif t == "a0":
                        for kind, j in proj_order():
                            if j % 2 == 0:
                                continue
                            if kind == "kv":
                                act.wait_ge(s[t + "_proj"], since(t, r, "proj") + j + 1)
                                n, _, _, dst = proj_jobs()[j]
                                nc.scalar.copy(dst, ps[:, j % 6, 0:n]).then_inc(s[t + "_ev_act"], 1)
                            else:
                                act.wait_ge(s[t + "_qproj"], since(t, r, "qproj") + j + 1)
                                for k in range(2):
                                    f(qm[:, 2 * j + k, :], ps[:, 7, 0:S], ACT.Copy, scale=rowmask[:, k:k + 1]) \
                                        .then_inc(s[t + "_qm_act"], 1)
                        attention(t, r, after)
                    else:
                        for j in range(8):
                            act.wait_ge(s[t + "_proj"], since(t, r, "proj") + j + 1)
                            stacked(t, j // 2, j % 2 == 0)
                        for h in (2, 3):
                            stacked_queries(t, r, h)
                        if t == "a1":
                            act.wait_ge(s["vals_zeroed"], 1)
                        act.wait_ge(s[t + "_proj"], since(t, r, "proj") + 9)
                        nc.scalar.copy(vals_pad[:, :, :, 0:8], ps[:, 4, :].rearrange("p (k h i) -> p k h i", k=CT, i=8)) \
                            .then_inc(s[t + "_ev_act"], 1)
                        attention(t, r, after)
                iteration_end(act, "act")

        @block.vector
        def _(dve):
            v = nc.vector
            step = [0]

            def link(ins):
                step[0] += 1
                ins.then_inc(s["dve_step"], 1)
                dve.wait_ge(s["dve_step"], step[0])

            def spread(src, lo, hi):
                for k in range(lo, hi):
                    ins = v.bn_stats(stats[:, k, :], src[:, k, :])
                link(ins)
                for k in range(lo, hi):
                    v.bn_aggr(mv[:, k, :], stats[:, k, :]).then_inc(s["stats"], 1)

            def normed(src, lo, hi, n_rstd):
                dve.wait_ge(s["rstd"], n_rstd)
                for k in range(lo, hi):
                    v.tensor_scalar(nrm[:, k, :], src[:, k, :], mv[:, k, 0:1], rstd[:, k:k + 1], ALU.subtract, ALU.mult) \
                        .then_inc(s["normed"], 1)

            def ready_spread(t, r):
                if nth(t, r) >= 2:
                    dve.wait_ge(s["x_done"], NT * (nth(t, r) - 1))
                dve.wait_ge(s["xT"], before(t, r, "xT"))
                if t == "a0":
                    spread(tok[:, r], 0, CT + NT)
                else:
                    spread(tok[:, r], CT, CT + NT)

            def ready_normed(t, r):
                n, m = before(t, r, "rstd"), before(t, r, "normed")
                if t != "a0":
                    normed(tok[:, r], CT, CT + NT, n + 1)
                    return
                normed(tok[:, r], 0, CT + NT, n + 1)
                dve.wait_ge(s["normed"], m + CT + NT)
                spread(nrm, CT, CT + NT)

            def ready_normed_twice(t, r):
                if t == "a0":
                    normed(nrm, CT, CT + NT, before(t, r, "rstd") + 2)

            def ready_context(t, r):
                if t != "a0":
                    return
                dve.wait_ge(w_early, N_EARLY)
                dve.wait_ge(s["xT"], before(t, r, "xT") + CT)
                if r == 1:
                    dve.wait_ge(s["a0_qproj"], HALF)
                v.tensor_scalar(kvT[:, 0:S2], ps[:, 7, 0:S2], gb0[:, 0:1], gb0[:, 1:2], ALU.mult, ALU.add) \
                    .then_inc(s["xnT"], 1)

            def attention(t, r, after):
                nk, hpc, rows, scale = (ATT[t][x] for x in ("nk", "hpc", "rows", "scale"))
                half = nk // P // 2
                U = HEADS * NT

                def add_bias(u):
                    dve.wait_ge(s[t + "_scores"], since(t, r, "scores") + u + 1)
                    if u >= 4:
                        dve.wait_ge(s[t + "_turned"], since(t, r, "turned") + 2 * (u - 3))
                    b = 2 * (u % 2)
                    sc = ps[:, b:b + 2, :].rearrange("p b n -> p (b n)")[:, 0:nk]
                    bias = {"a0": bias0[:], "a1": bias1[:, unit(t, u)[1], :], "a3": bias3[:]}[t]
                    v.tensor_tensor_reduce(out=prob[:, u % 4, 0:nk], in0=sc, in1=bias, scale=-scale, scalar=NEVER,
                                           op0=ALU.add, op1=ALU.min, accum_out=negmax[:, u:u + 1]) \
                        .then_inc(s[t + "_biased"], 1)

                def copy_turned(u):
                    dve.wait_ge(s[t + "_turned"], since(t, r, "turned") + 2 * u + 1)
                    if contracted(t, u):
                        dve.wait_ge(s[t + "_av"], since(t, r, "av") + contracted(t, u))
                    v.tensor_copy(turned_to(t, u, 0),
                                  ps[:, turned_bank(t, u, 0), 0:half * P].rearrange("p (k q) -> p k q", q=P)) \
                        .then_inc(s[t + "_pt_dve"], 1)

                def inverse(c):
                    dve.wait_ge(s[t + "_exped"], since(t, r, "exped") + NT * hpc * (c + 1))
                    hs = slice(hpc * c, hpc * c + hpc)
                    link(v.reciprocal(linv[:, hs, :], lsum[:, hs, :]))
                    if c >= 2:
                        dve.wait_ge(s[t + "_r"], since(t, r, "r") + c - 1)
                    for qt in range(NT):
                        ins = v.tensor_copy(linv_wide[:, c % 2, qt, :].rearrange("p (h r) -> p h r", h=hpc),
                                            linv[:, hs, qt:qt + 1].broadcast_to([P, hpc, rows]))
                    ins.then_inc(s[t + "_linv"], 1)

                def scale_out(c):
                    dve.wait_ge(s[t + "_r"], since(t, r, "r") + c + 1)
                    dve.wait_ge(s[t + "_o_raw"], since(t, r, "o_raw") + c + 1)
                    v.tensor_tensor(oT[:, c, :], o_raw[:, c % 2, :], ps[:, 6, S:2 * S], ALU.mult).then_inc(s[t + "_oT"], 1)

                w = NT * hpc
                lag = 7 if t == "a0" else 9
                for i in range(U + lag + 1):
                    if i >= 4 and (i - 4) % w == w - 1 and (i - 4) // w < HEADS // hpc:
                        inverse((i - 4) // w)
                    if i >= lag and (i - lag) % w == w - 1:
                        scale_out((i - lag) // w)
                    if i < U:
                        add_bias(i)
                    if t != "a0" and i % 8 in (1, 3) and i < 24:
                        stacked_queries(t, r, 4 * (i // 8 + 1) + i % 8 // 2)
                    if after and i == 8:
                        ready_spread(*after)
                    if after and i == 12:
                        ready_normed(*after)
                    if after and i == 15:
                        ready_normed_twice(*after)
                    if after and i == 17:
                        ready_context(*after)
                    if after and i == 26:
                        ready_logits(*after)
                    if after and i == 30 and after[0] != "f1":
                        ready_weights(*after)
                    if 3 <= i < U + 3:
                        copy_turned(i - 3)
                if t != "a0":
                    for k in range(NT):
                        if t == "a3" and k == 0:
                            dve.wait_ge(s["bo3"], 1)
                        ins = v.tensor_tensor(X[:, r, k, :], X[:, r, k, :], (bo3_all if t == "a3" else bo[t])[:], ALU.add)
                    link(ins)
                if after[0] == t:
                    start(*after, 0)
                if after[0] == "f1":
                    ready_weights(*after)
                dve.wait_ge(s[t + "_y"], since(t, r, "y") + NT)
                for k in range(NT):
                    v.tensor_tensor(X[:, r, k, :], X[:, r, k, :], ps[:, 6, P * k:P * k + P], ALU.add) \
                        .then_inc(s["x_done"], 1)

            def stacked(t, r, g, keys):
                j = 1 if keys else 0
                dst, src = (kst if keys else qst)[:, g, :], stack_out(g, keys)
                dve.wait_ge(s[t + "_ev_act"], since(t, r, "ev_act") + 2 * g + 2 - j)
                if t == "a3":
                    ins = v.scalar_tensor_tensor(out=dst, in0=src, scalar=bqk3[:, j, g:g + 1], in1=dst, op0=ALU.add,
                                                 op1=ALU.add)
                else:
                    ins = v.tensor_tensor(dst, src, dst, ALU.add)
                ins.then_inc(s[t + "_ev_dve"], 1)

            def stacked_queries(t, r, h):
                dve.wait_ge(s[t + "_ev_dve"], since(t, r, "ev_dve") + 2 * (h // 4) + 2)
                v.tensor_scalar(qst_m[:, h, :], qst[:, h // 4, :], lane8[:, h % 4:h % 4 + 1], None, ALU.mult) \
                    .then_inc(s[t + "_qm"], 1)

            def start(t, r, part):
                if part == 0 and t != "a1":
                    v.tensor_scalar(bias0[:, 0:S2], mask_u8[:, r, 0 if t == "a0" else 1, :], -1.0, FAR, ALU.add, ALU.mult)
                if t == "a0":
                    for kind, j in proj_order()[:6] if part == 0 else proj_order()[6:]:
                        if j % 2:
                            continue
                        if kind == "kv":
                            dve.wait_ge(s[t + "_proj"], since(t, r, "proj") + j + 1)
                            n, _, _, dst = proj_jobs()[j]
                            v.tensor_copy(dst, ps[:, j % 6, 0:n]).then_inc(s[t + "_ev_dve"], 1)
                        else:
                            dve.wait_ge(s[t + "_qproj"], since(t, r, "qproj") + j + 1)
                            for k in range(2):
                                v.tensor_scalar(qm[:, 2 * j + k, :], ps[:, 6, 0:S], rowmask[:, k:k + 1], None, ALU.mult) \
                                    .then_inc(s[t + "_qm"], 1)
                    return
                for g in (0, 1) if part == 0 else (2, 3):
                    stacked(t, r, g, True)
                    stacked(t, r, g, False)
                    if g == 0:
                        stacked_queries(t, r, 0)
                        stacked_queries(t, r, 1)

            def attention2(r, after):
                t = "a2"
                ready_spread(*after)
                dve.wait_ge(s[t + "_proj"], since(t, r, "proj") + 1)
                v.tensor_copy(keysT[:, 0, 0:S], ps[:, 0, 0:S]).then_inc(s[t + "_ev_dve"], 1)
                dve.wait_ge(s[t + "_qproj"], since(t, r, "qproj") + 1)
                v.tensor_copy(qm[:, 0, :], ps[:, 6, 0:S]).then_inc(s[t + "_qm"], 1)
                ready_normed(*after)
                for qt in range(NT):
                    dve.wait_ge(s[t + "_scores"], since(t, r, "scores") + qt + 1)
                    v.tensor_tensor_reduce(out=prob[:, qt, 0:S], in0=ps[:, 2 + qt, 0:S], in1=bias2[:, qt, :],
                                           scale=-float(D ** -0.5), scalar=NEVER, op0=ALU.add, op1=ALU.min,
                                           accum_out=negmax[:, qt:qt + 1]).then_inc(s[t + "_biased"], 1)
                for qt in range(NT):
                    dve.wait_ge(s[t + "_turned"], since(t, r, "turned") + qt + 1)
                    n = P * (qt + 1)
                    v.tensor_copy(probT[:, NT * qt:NT * qt + qt + 1, :], ps[:, 4 + qt, 0:n].rearrange("p (k q) -> p k q", q=P)) \
                        .then_inc(s[t + "_pt_dve"], 1)
                ready_logits(*after)
                dve.wait_ge(s[t + "_exped"], since(t, r, "exped") + NT)
                link(v.reciprocal(linv[:, 0, :], lsum[:, 0, :]))
                for qt in range(NT):
                    dve.wait_ge(s[t + "_y"], since(t, r, "y") + NT)
                    v.scalar_tensor_tensor(out=X[:, r, qt, :], in0=ps[:, 6, P * qt:P * qt + P], scalar=linv[:, 0, qt:qt + 1],
                                           in1=X[:, r, qt, :], op0=ALU.mult, op1=ALU.add).then_inc(s["x_done"], 1)
                ready_weights(*after)

            def ready_logits(t, r):
                if t[0] == "a":
                    return
                E = MOE[t]["routed"]
                if E < 8:
                    link(v.memset(logit[:], -1e38))
                fixed = 1.0 / 3.0 if t == "f0" else MOE[t]["fixed"]
                v.memset(comb[:, r], fixed)
                dve.wait_ge(s[t + "_logits"], since(t, r, "logits") + 1)
                lg = ps[:, 7, 0:8 * NT].rearrange("p (k e) -> p k e", e=8)[:, :, 0:E]
                if t in b_gate:
                    for k in range(NT):
                        ins = v.tensor_tensor(logit[:, k, 0:E], b_gate[t][:], lg[:, k, :], ALU.add)
                else:
                    ins = v.tensor_copy(logit[:, :, 0:E], lg)
                ins.then_inc(s[t + "_logit"], 1)
                if t == "f2":
                    for k in range(NT):
                        ins = v.tensor_tensor(gl[:, r, k, :], sb2[:, 0, :], ps[:, 7, S + P * k:S + P * k + P], ALU.add)
                    ins.then_inc(s["f2_sh"], 1)
                dve.wait_ge(s[t + "_logit"], since(t, r, "logit") + 1)
                for k in range(NT):
                    ins = v.max(top8[:, k, :], logit[:, k, :])
                link(ins)
                if t in ("f2", "f3"):
                    for k in range(NT):
                        ins = v.tensor_scalar(rt[1][:, k, :], logit[:, k, :], top8[:, k, 0:1], None, ALU.subtract)
                    ins.then_inc(s[t + "_r_mid"], 1)
                link(v.memset(top8[:, :, 2:8], NEVER))
                for k in range(NT):
                    ins = v.match_replace(cut[:, k, :], top8[:, k, :], logit[:, k, :], -NEVER)
                link(ins)
                link(v.tensor_tensor(rt[0][:], cut[:], logit[:], ALU.not_equal))

            def ready_weights(t, r):
                if t[0] == "a":
                    return
                E = MOE[t]["routed"]
                if t == "f0":
                    dve.wait_ge(s[t + "_r_act"], since(t, r, "r_act") + 1)
                    link(v.tensor_scalar(rt[2][:], rt[1][:], 1.0, None, ALU.add))
                    link(v.reciprocal(rt[3][:], rt[2][:]))
                elif t == "f1":
                    dve.wait_ge(s[t + "_r_act"], since(t, r, "r_act") + 3)
                    v.scalar_tensor_tensor(out=rt[2][:], in0=logit[:], scalar=0.0, in1=rt[1][:], op0=ALU.max,
                                           op1=ALU.add).then_inc(s[t + "_r_mid"], 1)
                    dve.wait_ge(s["f1_r_pool"], since("f1", r, "r_pool") + 1)
                else:
                    dve.wait_ge(s[t + "_r_act"], since(t, r, "r_act") + 1)
                if t == "f1":
                    v.tensor_tensor(comb[:, r, :, 0:E], rt[3][:, :, 0:E], rt[0][:, :, 0:E], ALU.mult).then_inc(s[t + "_comb"], 1)
                else:
                    link(v.tensor_tensor(rt[4][:], rt[3][:], rt[0][:], ALU.mult))
                    link(v.tensor_reduce(rsum[:], (rt[3] if t == "f3" else rt[4])[:], AX_X, ALU.add))
                    link(v.reciprocal(rinv[:], rsum[:]))
                    for k in range(NT):
                        ins = v.tensor_scalar(comb[:, r, k, 0:E], rt[4][:, k, 0:E], rinv[:, k:k + 1],
                                              1.0 / 3.0 if t == "f0" else 1.0, ALU.mult, ALU.mult)
                    ins.then_inc(s[t + "_comb"], 1)
                dve.wait_ge(s[t + "_comb"], since(t, r, "comb") + 1)

            def later_constants():
                dve.wait_ge(consts_ready, N_CONSTS)
                v.tensor_copy(vals[:, 2:6, 0:P], bv_pad[:].rearrange("p (c o) -> p c o", o=1).broadcast_to([P, 4, P])) \
                    .then_inc(s["bv_wide"], 1)
                v.tensor_scalar(bias1[:], mask1_u8[:], -1.0, FAR, ALU.add, ALU.mult)
                v.tensor_reduce(lane8[:], rowmask[:, 2:2 + HEADS].rearrange("p (q j) -> p j q", j=4), AX_X, ALU.add)
                v.tensor_scalar(split[:, 0:1], rowmask[:, 1:2], -1.0, None, ALU.mult)
                link(v.tensor_reduce(split[:, 1:2], rowmask[:, 2:2 + HEADS].rearrange("p (a b j) -> p b a j", a=2, b=2)[:, 1],
                                     AX_XY, ALU.add, negate=True))
                for j in range(2):
                    v.tensor_scalar(bqk3_split[:, j, :], bqk3[:, j, :], split[:, j:j + 1], None, ALU.mult)

            def output_constant():
                dve.wait_ge(s["bv_out"], 1)
                v.tensor_tensor(bo3_all[:], bo["a3"][:], ps[:, 6, 0:D], ALU.add).then_inc(s["bo3"], 1)

            def mixture(t, r, after):
                groups, nch = expert_groups(t), MOE[t]["chunks"]
                ne = first_of(groups, len(groups))
                total = acc if t == "f2" else X[:, r]
                if t == "f2":
                    dve.wait_ge(s["f2_gl"], since("f2", r, "gl") + 1)
                    link(v.tensor_scalar(acc, gl[:, r], 0.5, None, ALU.mult))

                def hidden(u):
                    dve.wait_ge(s[t + "_act"], since(t, r, "act") + u + 1)
                    if u >= 8:
                        dve.wait_ge(s[t + "_down"], since(t, r, "down") + down_before(t, u))
                    v.tensor_tensor(hT[:, u % 8 // 2, u % 2, :], act_tmp[:, u % 4, :], ps[:, u % 4, S:2 * S], ALU.mult) \
                        .then_inc(s[t + "_h"], 1)

                def add_expert(n, e):
                    dve.wait_ge(s[t + "_down"], since(t, r, "down") + n + 1)
                    for k in range(NT):
                        if n >= 1:
                            dve.wait_ge(s[t + "_y_used"], since(t, r, "y_used") + NT * (n - 1) + k + 1)
                        last = t == "f0" and n == ne - 1
                        v.scalar_tensor_tensor(out=total[:, k, :], in0=ps[:, 4 + n % 2, P * k:P * k + P],
                                               scalar=comb[:, r, k, e:e + 1], in1=total[:, k, :], op0=ALU.mult,
                                               op1=ALU.add).then_inc(s["x_done" if last else t + "_y_used"], 1)

                def turned_weights():
                    dve.wait_ge(s[t + "_combT"], since(t, r, "combT") + 1)
                    v.tensor_copy(combT[0:ne, :], ps[0:ne, 6, 0:S]).then_inc(s[t + "_combT_sb"], 1)

                if t == "f0":
                    for u in range(nch):
                        hidden(u)
                for g in range(len(groups)):
                    if t == "f0":
                        for u in range(nch * (g + 1), min(nch * (g + 2), nch * len(groups))):
                            hidden(u)
                    for i, e in enumerate(groups[g]):
                        add_expert(first_of(groups, g) + i, e)
                    if g == 0 and after:
                        ready_spread(*after)
                    if g == 1 and after:
                        ready_normed(*after)
                    if g == 1 and t != "f0":
                        turned_weights()
                    if (t, r) == ("f0", 0) and g == 5:
                        later_constants()
                    if (t, r) == ("f0", 0) and g == 8:
                        output_constant()
                    if g == 3 and after:
                        ready_logits(*after)
                    if g == 4 and after:
                        ready_weights(*after)
                if t == "f0":
                    return
                dve.wait_ge(s[t + "_b2"], since(t, r, "b2") + 1)
                dve.wait_ge(s[t + "_y_used"], since(t, r, "y_used") + NT * ne)
                for k in range(NT):
                    ins = v.tensor_tensor(total[:, k, :], total[:, k, :], ps[:, 6, P * k:P * k + P], ALU.add)
                    if t == "f2":
                        link(ins)
                    else:
                        ins.then_inc(s["x_done"], 1)
                if t == "f2":
                    for k in range(NT):
                        ins = v.bn_stats(end_stats[:, k, :], acc[:, k, :])
                    link(ins)
                    for k in range(NT):
                        v.bn_aggr(end_mv[:, k, :], end_stats[:, k, :]).then_inc(s["f2_e_stats"], 1)
                    dve.wait_ge(s["f2_e_rstd"], since("f2", r, "e_rstd") + 1)
                    for k in range(NT):
                        ins = v.tensor_scalar(acc[:, k, :], acc[:, k, :], end_mv[:, k, 0:1], end_rstd[:, k:k + 1],
                                              ALU.subtract, ALU.mult)
                    for j, op in ((1, ALU.mult), (2, ALU.add)):
                        link(ins)
                        for k in range(NT):
                            ins = v.tensor_tensor(acc[:, k, :], acc[:, k, :], sb2[:, j, :], op)
                    link(ins)
                    for k in range(NT):
                        v.tensor_tensor(X[:, r, k, :], X[:, r, k, :], acc[:, k, :], ALU.add).then_inc(s["x_done"], 1)

            with dve.Fori(0, B // 2):
                step[0] = 0
                dve.wait_ge(loaded, N_LOAD)
                dve.sem_clear(loaded)
                link(v.tensor_copy(X, xin[:]))
                ready_spread(*RUNS[0])
                ready_normed(*RUNS[0])
                ready_context(*RUNS[0])
                ready_normed_twice(*RUNS[0])
                for n, (t, r) in enumerate(RUNS):
                    after = RUNS[n + 1] if n + 1 < len(RUNS) else None
                    dve.wait_ge(s["x_done"], before(t, r, "x_done"))
                    if t == "f0":
                        dve.wait_ge(w_rest, N_REST)
                    if t[0] == "f":
                        mixture(t, r, after)
                        continue
                    if t == "a2":
                        attention2(r, after)
                        continue
                    if not (r == 1 and t[0] == "a"):
                        start(t, r, 0)
                    start(t, r, 1)
                    attention(t, r, after)
                iteration_end(dve, "dve")


def kernel(**inputs):
    import numpy as _np
    import concourse.bacc as _bacc
    from concourse import mybir as _mybir
    from concourse.bass_utils import run_bass_kernel_spmd as _run

    given = {k: _np.asarray(v) for k, v in inputs.items()}
    given["mask0"] = given.pop("mask_BxS2_bk0")
    given["mask3"] = given.pop("mask_BxS2_bf1")
    m = given.pop("mask_1x1xSxS2_bk0")
    given["mask1"] = m.reshape(m.shape[2:])
    given["ctxT"] = given["ctx_1024"].transpose(0, 2, 1)
    for name in ("L1_xattn_Wq", "L1_xattn_Wk", "L1_xattn_Wv", "L1_xattn_Wo", "L1_ffn_routing_W", "L2_xattn_Wq",
                 "L3_xattn_Wq", "L3_xattn_Wk", "L3_xattn_Wv", "L3_xattn_Wo"):
        given[name + "T"] = given.pop(name).T
    for name in ("L1_ffn_rb1", "L2_ffn_b1", "L3_ffn_sb1", "L3_ffn_rb1"):
        given[name + "c"] = given.pop(name).reshape(-1, P).T

    nc = _bacc.Bacc("TRN2", target_bir_lowering=False, num_devices=1)
    arrays, aps = {}, {}
    for name, x in given.items():
        x = _np.ascontiguousarray(x)
        arrays[f"in_{name}_dram"] = x
        aps[name] = nc.dram_tensor(f"in_{name}_dram", x.shape, _mybir.dt.from_np(x.dtype), kind="ExternalInput").ap()
    shape = given["x"].shape
    out = nc.dram_tensor("out_0_dram", shape, _mybir.dt.float32, kind="ExternalOutput").ap()
    build(nc, aps, out)
    r = _run(nc, [arrays], core_ids=[0])
    return r.results[0]["out_0_dram"]
```
